# Optimizing a Trainium2 kernel written in Bass

```python
import numpy as np
import jax
import jax.numpy as jnp

def _softmax(x, axis=-1):
    return jax.nn.softmax(x, axis=axis)

def _gelu(x):
    return jax.nn.gelu(x, approximate=True)

def _silu(x):
    return jax.nn.silu(x)

def _sigmoid(x):
    return jax.nn.sigmoid(x)

def _layernorm(x, axis=-1, eps=1e-05):
    m = jnp.mean(x, axis=axis, keepdims=True)
    v = jnp.var(x, axis=axis, keepdims=True)
    return (x - m) / jnp.sqrt(v + eps)

def _scatter_add(tgt, idx, src, axis=0):
    return tgt.at[idx].add(src)

def _segment_sum(src, seg, n):
    return jax.ops.segment_sum(src, seg, n)
kernel_name = 'mk_hybrid_d1_jaxref_r8_c76305'

def setup_inputs(seed: int=0):
    np.random.seed(seed)
    _w = jnp.asarray

    def _L0_attn_a_setup():
        import jax, jax.numpy as jnp
        import numpy as np
        import math
        D_MODEL = 128
        LN_EPS = 1e-05

        def _layer_norm(x):
            mu = jnp.mean(x, axis=-1, keepdims=True)
            var = jnp.var(x, axis=-1, keepdims=True)
            return (x - mu) * jax.lax.rsqrt(var + LN_EPS)
        key = jax.random.key(seed)
        ks = jax.random.split(key, 5)
        B, S, D = (4, 256, D_MODEL)
        scale = 1.0 / math.sqrt(D)
        x = jax.random.normal(ks[0], (B, S, D), dtype=jnp.float32)
        Wq = jax.random.normal(ks[1], (D, D), dtype=jnp.float32) * scale
        Wk = jax.random.normal(ks[2], (D, D), dtype=jnp.float32) * scale
        Wv = jax.random.normal(ks[3], (D, D), dtype=jnp.float32) * scale
        Wo = jax.random.normal(ks[4], (D, D), dtype=jnp.float32) * scale
        b = jnp.zeros((D,), dtype=jnp.float32)
        layerscale = 0.0001 * jnp.ones((D,), dtype=jnp.float32)
        return {'x': x, 'Wq': Wq, 'bq': b, 'Wk': Wk, 'bk': b, 'Wv': Wv, 'bv': b, 'Wo': Wo, 'bo': b, 'layerscale': layerscale}
    _L0_attn_a_in = _L0_attn_a_setup()

    def _L0_attn_b_setup():
        import jax, jax.numpy as jnp
        import numpy as np
        H = 16
        D = 64
        BQ = 64
        BKV = 64

        def _flash_tiled(q, k, v, scale):
            B, nh, S, d = q.shape
            nq, nkv = (S // BQ, S // BKV)
            qb = q.reshape(B, nh, nq, BQ, d)
            kb = k.reshape(B, nh, nkv, BKV, d).transpose(2, 0, 1, 3, 4)
            vb = v.reshape(B, nh, nkv, BKV, d).transpose(2, 0, 1, 3, 4)
            o0 = jnp.zeros((B, nh, nq, BQ, d), q.dtype)
            m0 = jnp.full((B, nh, nq, BQ), -jnp.inf, q.dtype)
            l0 = jnp.zeros((B, nh, nq, BQ), q.dtype)

            def step(carry, kv):
                o, m, l = carry
                kj, vj = kv
                s = jnp.einsum('bhnqd,bhkd->bhnqk', qb, kj) * scale
                m_new = jnp.maximum(m, s.max(axis=-1))
                p = jnp.exp(s - m_new[..., None])
                alpha = jnp.exp(m - m_new)
                l_new = alpha * l + p.sum(axis=-1)
                o_new = (alpha[..., None] * o + jnp.einsum('bhnqk,bhkd->bhnqd', p, vj)) / l_new[..., None]
                return ((o_new, m_new, l_new), None)
            (o, _, _), _ = jax.lax.scan(step, (o0, m0, l0), (kb, vb))
            return o.reshape(B, nh, S, d)
        key = jax.random.key(seed)
        ks = jax.random.split(key, 5)
        B, S, dim = (2, 256, 128)
        x = jax.random.normal(ks[0], (B, S, dim), dtype=jnp.float32)
        Wq = jax.random.normal(ks[1], (dim, H * D), dtype=jnp.float32) * 0.02
        Wk = jax.random.normal(ks[2], (dim, H * D), dtype=jnp.float32) * 0.02
        Wv = jax.random.normal(ks[3], (dim, H * D), dtype=jnp.float32) * 0.02
        Wo = jax.random.normal(ks[4], (H * D, dim), dtype=jnp.float32) * 0.02
        return {'x': x, 'Wq': Wq, 'Wk': Wk, 'Wv': Wv, 'Wo': Wo}
    _L0_attn_b_in = _L0_attn_b_setup()

    def _L0_ffn_setup():
        import jax, jax.numpy as jnp
        import numpy as np
        D, H, E, K = (128, 512, 8, 2)
        B, T = (2, 256)

        def _layernorm(x, g, b, eps=1e-05):
            mu = jnp.mean(x, axis=-1, keepdims=True)
            var = jnp.mean(jnp.square(x - mu), axis=-1, keepdims=True)
            return (x - mu) * jax.lax.rsqrt(var + eps) * g + b

        def _expert(x, g, b, W1, b1, W2, b2, Wo, bo):
            x = _layernorm(x, g, b)
            x1 = x @ W1 + b1
            x2 = jnp.clip(x @ W2 + b2, -20.0, 20.0)
            hidden = jnp.clip(x1 * (x2 * jax.nn.sigmoid(x2)), -10000.0, 10000.0)
            return jnp.clip(hidden @ Wo + bo, -10000.0, 10000.0)
        key = jax.random.key(seed)
        ks = jax.random.split(key, 6)
        s = 0.02
        return {'x': jax.random.normal(ks[0], (B, T, D), jnp.float32), 'ln_g': jnp.ones((D,), jnp.float32), 'ln_b': jnp.zeros((D,), jnp.float32), 'router_w': jax.random.normal(ks[1], (D, E), jnp.float32) * s, 'eg': jnp.ones((E, D), jnp.float32), 'eb': jnp.zeros((E, D), jnp.float32), 'W1': jax.random.normal(ks[2], (E, D, H), jnp.float32) * s, 'b1': jnp.zeros((E, H), jnp.float32), 'W2': jax.random.normal(ks[3], (E, D, H), jnp.float32) * s, 'b2': jnp.zeros((E, H), jnp.float32), 'Wo': jax.random.normal(ks[4], (E, H, D), jnp.float32) * s, 'bo': jnp.zeros((E, D), jnp.float32)}
    _L0_ffn_in = _L0_ffn_setup()
    _d = {'L0_attn_a_x': _L0_attn_a_in['x'], 'L0_attn_a_Wq': _L0_attn_a_in['Wq'], 'L0_attn_a_bq': _L0_attn_a_in['bq'], 'L0_attn_a_Wk': _L0_attn_a_in['Wk'], 'L0_attn_a_bk': _L0_attn_a_in['bk'], 'L0_attn_a_Wv': _L0_attn_a_in['Wv'], 'L0_attn_a_bv': _L0_attn_a_in['bv'], 'L0_attn_a_Wo': _L0_attn_a_in['Wo'], 'L0_attn_a_bo': _L0_attn_a_in['bo'], 'L0_attn_a_layerscale': _L0_attn_a_in['layerscale'], 'L0_attn_b_Wq': _L0_attn_b_in['Wq'], 'L0_attn_b_Wk': _L0_attn_b_in['Wk'], 'L0_attn_b_Wv': _L0_attn_b_in['Wv'], 'L0_attn_b_Wo': _L0_attn_b_in['Wo'], 'L0_ffn_ln_g': _L0_ffn_in['ln_g'], 'L0_ffn_ln_b': _L0_ffn_in['ln_b'], 'L0_ffn_router_w': _L0_ffn_in['router_w'], 'L0_ffn_eg': _L0_ffn_in['eg'], 'L0_ffn_eb': _L0_ffn_in['eb'], 'L0_ffn_W1': _L0_ffn_in['W1'], 'L0_ffn_b1': _L0_ffn_in['b1'], 'L0_ffn_W2': _L0_ffn_in['W2'], 'L0_ffn_b2': _L0_ffn_in['b2'], 'L0_ffn_Wo': _L0_ffn_in['Wo'], 'L0_ffn_bo': _L0_ffn_in['bo']}
    _x0 = _d['L0_attn_a_x']
    _d['L0_attn_a_x'] = jax.random.normal(jax.random.fold_in(jax.random.key(seed), 1), (4, 1024, 128), dtype=_x0.dtype)
    del _x0
    return _d

def reference(L0_attn_a_x, L0_attn_a_Wq, L0_attn_a_bq, L0_attn_a_Wk, L0_attn_a_bk, L0_attn_a_Wv, L0_attn_a_bv, L0_attn_a_Wo, L0_attn_a_bo, L0_attn_a_layerscale, L0_attn_b_Wq, L0_attn_b_Wk, L0_attn_b_Wv, L0_attn_b_Wo, L0_ffn_ln_g, L0_ffn_ln_b, L0_ffn_router_w, L0_ffn_eg, L0_ffn_eb, L0_ffn_W1, L0_ffn_b1, L0_ffn_W2, L0_ffn_b2, L0_ffn_Wo, L0_ffn_bo):

    def _L0_attn_a_ref(x, Wq, bq, Wk, bk, Wv, bv, Wo, bo, layerscale):
        import jax, jax.numpy as jnp
        import numpy as np
        import math
        D_MODEL = 128
        LN_EPS = 1e-05

        def _layer_norm(x):
            mu = jnp.mean(x, axis=-1, keepdims=True)
            var = jnp.var(x, axis=-1, keepdims=True)
            return (x - mu) * jax.lax.rsqrt(var + LN_EPS)
        B, S, D = x.shape
        q = jnp.einsum('bsd,ed->bse', x, Wq) + bq
        k = jnp.einsum('bsd,ed->bse', x, Wk) + bk
        v = jnp.einsum('bsd,ed->bse', x, Wv) + bv
        qn = _layer_norm(q)
        kn = _layer_norm(k)
        scores = jnp.einsum('bse,bte->bst', qn, kn) / jnp.sqrt(jnp.float32(D))
        attn = jax.nn.sigmoid(scores - jnp.log(jnp.float32(S)))
        out = jnp.einsum('bst,bte->bse', attn, v)
        proj = jnp.einsum('bsd,ed->bse', out, Wo) + bo
        return proj * layerscale

    def _L0_attn_b_ref(x, Wq, Wk, Wv, Wo):
        import jax, jax.numpy as jnp
        import numpy as np
        H = 16
        D = 64
        BQ = 64
        BKV = 64

        def _flash_tiled(q, k, v, scale):
            B, nh, S, d = q.shape
            nq, nkv = (S // BQ, S // BKV)
            qb = q.reshape(B, nh, nq, BQ, d)
            kb = k.reshape(B, nh, nkv, BKV, d).transpose(2, 0, 1, 3, 4)
            vb = v.reshape(B, nh, nkv, BKV, d).transpose(2, 0, 1, 3, 4)
            o0 = jnp.zeros((B, nh, nq, BQ, d), q.dtype)
            m0 = jnp.full((B, nh, nq, BQ), -jnp.inf, q.dtype)
            l0 = jnp.zeros((B, nh, nq, BQ), q.dtype)

            def step(carry, kv):
                o, m, l = carry
                kj, vj = kv
                s = jnp.einsum('bhnqd,bhkd->bhnqk', qb, kj) * scale
                m_new = jnp.maximum(m, s.max(axis=-1))
                p = jnp.exp(s - m_new[..., None])
                alpha = jnp.exp(m - m_new)
                l_new = alpha * l + p.sum(axis=-1)
                o_new = (alpha[..., None] * o + jnp.einsum('bhnqk,bhkd->bhnqd', p, vj)) / l_new[..., None]
                return ((o_new, m_new, l_new), None)
            (o, _, _), _ = jax.lax.scan(step, (o0, m0, l0), (kb, vb))
            return o.reshape(B, nh, S, d)
        B, S, dim = x.shape
        scale = D ** (-0.5)
        q = (x @ Wq).reshape(B, S, H, D).transpose(0, 2, 1, 3)
        k = (x @ Wk).reshape(B, S, H, D).transpose(0, 2, 1, 3)
        v = (x @ Wv).reshape(B, S, H, D).transpose(0, 2, 1, 3)
        o = _flash_tiled(q, k, v, scale)
        out = o.transpose(0, 2, 1, 3).reshape(B, S, H * D)
        return out @ Wo

    def _L0_ffn_ref(x, ln_g, ln_b, router_w, eg, eb, W1, b1, W2, b2, Wo, bo):
        import jax, jax.numpy as jnp
        import numpy as np
        D, H, E, K = (128, 512, 8, 2)
        B, T = (2, 256)

        def _layernorm(x, g, b, eps=1e-05):
            mu = jnp.mean(x, axis=-1, keepdims=True)
            var = jnp.mean(jnp.square(x - mu), axis=-1, keepdims=True)
            return (x - mu) * jax.lax.rsqrt(var + eps) * g + b

        def _expert(x, g, b, W1, b1, W2, b2, Wo, bo):
            x = _layernorm(x, g, b)
            x1 = x @ W1 + b1
            x2 = jnp.clip(x @ W2 + b2, -20.0, 20.0)
            hidden = jnp.clip(x1 * (x2 * jax.nn.sigmoid(x2)), -10000.0, 10000.0)
            return jnp.clip(hidden @ Wo + bo, -10000.0, 10000.0)
        Bb, Tt, Dd = x.shape
        xf = _layernorm(x.reshape(-1, Dd), ln_g, ln_b)
        N = xf.shape[0]
        logits = xf @ router_w
        scores, idx = jax.lax.top_k(logits, K)
        gate = jax.nn.softmax(scores, axis=-1)
        gates_e = jnp.zeros((N, E), xf.dtype).at[jnp.arange(N)[:, None], idx].add(gate)

        def body(acc, p):
            gcol, g, b, w1, bb1, w2, bb2, wo, bbo = p
            return (acc + gcol[:, None] * _expert(xf, g, b, w1, bb1, w2, bb2, wo, bbo), None)
        out, _ = jax.lax.scan(body, jnp.zeros_like(xf), (gates_e.T, eg, eb, W1, b1, W2, b2, Wo, bo))
        return out.reshape(Bb, Tt, Dd)
    x = L0_attn_a_x
    x = x + _L0_attn_a_ref(_layernorm(x, axis=-1), L0_attn_a_Wq, L0_attn_a_bq, L0_attn_a_Wk, L0_attn_a_bk, L0_attn_a_Wv, L0_attn_a_bv, L0_attn_a_Wo, L0_attn_a_bo, L0_attn_a_layerscale)
    x = x + _L0_ffn_ref(_layernorm(x, axis=-1), L0_ffn_ln_g, L0_ffn_ln_b, L0_ffn_router_w, L0_ffn_eg, L0_ffn_eb, L0_ffn_W1, L0_ffn_b1, L0_ffn_W2, L0_ffn_b2, L0_ffn_Wo, L0_ffn_bo)
    x = x + _L0_attn_b_ref(_layernorm(x, axis=-1), L0_attn_b_Wq, L0_attn_b_Wk, L0_attn_b_Wv, L0_attn_b_Wo)
    x = x + _L0_ffn_ref(_layernorm(x, axis=-1), L0_ffn_ln_g, L0_ffn_ln_b, L0_ffn_router_w, L0_ffn_eg, L0_ffn_eb, L0_ffn_W1, L0_ffn_b1, L0_ffn_W2, L0_ffn_b2, L0_ffn_Wo, L0_ffn_bo)
    return x

_drawn_inputs = setup_inputs


def setup_inputs(seed=0):
    import zlib

    import numpy as np

    out = dict(_drawn_inputs(seed))
    spreads = {'L0_attn_a_bq': (0.0, 0.8),
     'L0_attn_a_bk': (0.0, 0.8),
     'L0_attn_a_bv': (0.0, 0.8),
     'L0_attn_a_bo': (0.0, 0.8),
     'L0_attn_a_layerscale': (9.999999747378752e-05, 0.6),
     'L0_ffn_ln_g': (1.0, 0.2),
     'L0_ffn_ln_b': (0.0, 0.1),
     'L0_ffn_eg': (1.0, 0.6),
     'L0_ffn_eb': (0.0, 0.8),
     'L0_ffn_b1': (0.0, 0.8),
     'L0_ffn_b2': (0.0, 0.8),
     'L0_ffn_bo': (0.0, 0.1)}
    factors = {'L0_attn_a_Wq': 8.0,
     'L0_attn_a_Wk': 8.0,
     'L0_attn_a_Wv': 8.0,
     'L0_attn_a_Wo': 8.0,
     'L0_attn_b_Wq': 8.0,
     'L0_attn_b_Wk': 8.0,
     'L0_attn_b_Wv': 8.0,
     'L0_attn_b_Wo': 8.0,
     'L0_ffn_W1': 2.715,
     'L0_ffn_W2': 2.723}
    for name, (base, spread) in spreads.items():
        noise = np.random.default_rng([zlib.crc32(name.encode()), seed]).standard_normal(out[name].shape)
        drawn = base * np.exp(spread * noise) if base else spread * noise
        out[name] = jnp.asarray(drawn.astype(out[name].dtype))
    for name, factor in factors.items():
        out[name] = (out[name] * factor).astype(out[name].dtype)
    return out
```

```python
import math
from contextlib import ExitStack

import concourse.bass as bass
from concourse import mybir

F32 = mybir.dt.float32
F32R = mybir.dt.float32r
ALU = mybir.AluOpType
ACT = mybir.ActivationFunctionType
AX = mybir.AxisListType.X

P = 128
D = 128
BATCH = 4
SEQ = 1024
TPB = SEQ // P
TILES = BATCH * TPB
HALF = 512
EPS = 1e-5


class Shared:

    def __init__(self, sem):
        self.chain_sem = sem("dve_chain")
        self.links = 0
        self.norm_sems = [sem("ln_" + n) for n in ("centred", "squared", "var_ready", "std_ready")]
        self.norms = 0


class Chain:

    def __init__(self, eng, shared):
        self.eng, self.shared, self.sem = eng, shared, shared.chain_sem
        self.base, self.k = shared.links, 0

    def close(self):
        self.shared.links = self.base + self.k

    def link(self, ins):
        ins.then_inc(self.sem, 1)
        self.k += 1
        self.eng.wait_ge(self.sem, self.base + self.k)

    def enter(self, i, per):
        self.start, self.per = self.base + self.k, per
        self.base, self.k = i * per + self.start, 0

    def enter_from(self, i, first, per):
        self.start, self.per = self.base + self.k, per
        self.base, self.k = (i - first) * per + self.start, 0

    def leave(self, times):
        assert self.k == self.per, (self.k, self.per)
        self.base, self.k = self.start + times * self.per, 0


class Norm:

    def __init__(self, sb, shared, rows, calls):
        self.sums = sb("ln_sums", [P, rows])
        self.mean = sb("ln_mean", [P, rows])
        self.var = sb("ln_var", [P, rows])
        self.std = sb("ln_std", [P, rows])
        self.rstd = sb("ln_rstd", [P, rows])
        self.sq = sb("ln_sq", [P, rows * D])
        self.centred, self.squared, self.var_ready, self.std_ready = shared.norm_sems
        self.before = shared.norms
        shared.norms += calls
        self.LINKS = 8

    def dve(self, dve, chain, src, dst, n, call):
        shape = list(src.shape)
        per = lambda t: t[:, 0:n] if len(shape) == 3 else t[:, 0:n].rearrange("p (a b) -> p a b", b=shape[2])
        dve_wide = lambda t: per(t).unsqueeze(len(shape) - 1).to_broadcast(shape)
        chain.link(dve.tensor_reduce(per(self.sums), src, AX, ALU.add))
        chain.link(dve.tensor_scalar(self.mean[:, 0:n], self.sums[:, 0:n], 1.0 / D, None, ALU.mult))
        dve.tensor_tensor(dst, src, dve_wide(self.mean), ALU.subtract).then_inc(self.centred, 1)
        dve.wait_ge(self.squared, self.before + call + 1)
        chain.link(dve.tensor_reduce(self.sums[:, 0:n], self.sq[:, 0:n * D].rearrange("p (n d) -> p n d", d=D), AX, ALU.add))
        dve.tensor_scalar(self.var[:, 0:n], self.sums[:, 0:n], 1.0 / D, EPS, ALU.mult, ALU.add).then_inc(self.var_ready, 1)
        dve.wait_ge(self.std_ready, self.before + call + 1)
        chain.link(dve.reciprocal(self.rstd[:, 0:n], self.std[:, 0:n]))
        chain.link(dve.tensor_tensor(self.mean[:, 0:n], self.rstd[:, 0:n], self.rstd[:, 0:n], ALU.mult))
        chain.link(dve.tensor_tensor(self.sums[:, 0:n], self.mean[:, 0:n], self.var[:, 0:n], ALU.mult))
        chain.link(dve.tensor_scalar(self.mean[:, 0:n], self.sums[:, 0:n], -0.5, 1.5, ALU.mult, ALU.add))
        chain.link(dve.tensor_tensor(self.rstd[:, 0:n], self.rstd[:, 0:n], self.mean[:, 0:n], ALU.mult))
        return dve.tensor_tensor(dst, dst, dve_wide(self.rstd), ALU.mult)

    def act(self, act, dst, n, call):
        act.wait_ge(self.centred, self.before + call + 1)
        sq = self.sq[:, 0:n * D]
        sq = sq.rearrange("p (n d) -> p n d", d=D) if len(dst.shape) == 3 else sq.rearrange("p (a b d) -> p a b d", b=dst.shape[2], d=D)
        act.activation(sq, dst, ACT.Square).then_inc(self.squared, 1)
        act.wait_ge(self.var_ready, self.before + call + 1)
        act.activation(self.std[:, 0:n], self.var[:, 0:n], ACT.Sqrt).then_inc(self.std_ready, 1)



def sigmoid_attention(nc, X, ident, w, shared):
    with ExitStack() as ctx:
        sb = lambda name, shape, dt=F32: ctx.enter_context(nc.sbuf_tensor("a_" + name, shape, dt))
        bank = lambda name: ctx.enter_context(nc.psum_tensor("a_" + name, [P, HALF], F32))
        sem = lambda name: ctx.enter_context(nc.semaphore("a_" + name))

        wnat = sb("wnat", [P, 4, D])
        wT = sb("wT", [P, 4, D])
        bqkv = sb("bqkv", [P, 3, D])
        bo = sb("bo", [P, D])
        ls = sb("ls", [P, D])
        norm = Norm(sb, shared, 2 * TPB, 2 * BATCH)
        hn = sb("hn", [P, TPB, D])
        hT = sb("hT", [P, SEQ])
        qkv = sb("qkv", [P, TPB, 3, D])
        qkT = sb("qkT", [P, 2, SEQ])
        AT = sb("AT", [P, 3, HALF])
        oT = sb("oT", [P, SEQ])
        upd = sb("upd", [P, 2, 4, D])
        neg_log = sb("neg_log", [P, 1])

        ring = [bank(f"ring{i}") for i in range(2)]
        score = [bank(f"score{i}") for i in range(2)]
        acc = [bank(f"acc{i}") for i in range(2)]
        proj = [bank(f"proj{i}") for i in range(2)]

        loaded = sem("loaded")
        consts = sem("consts")
        w_turned = sem("w_turned")
        w_ready = sem("w_ready")
        hn_ready = sem("hn_ready")
        turned = sem("turned")
        evac = sem("evac")
        qkv_made = sem("qkv_made")
        qkv_taken = sem("qkv_taken")
        qk_ready = sem("qk_ready")
        scored = sem("scored")
        attn_ready = sem("attn_ready")
        pv_done = sem("pv_done")
        o_ready = sem("o_ready")
        proj_done = sem("proj_done")
        proj_taken = sem("proj_taken")

        with nc.Block() as block:

            @block.sync
            def _(sp):
                for i, name in enumerate(("Wq", "Wk", "Wv", "Wo")):
                    sp.dma_start(wnat[:, i, :], w["L0_attn_a_" + name]).then_inc(loaded, 16)
                for i, name in enumerate(("bq", "bk", "bv")):
                    sp.dma_start(bqkv[:, i, :], w["L0_attn_a_" + name].partition_broadcast(P)).then_inc(loaded, 16)
                sp.dma_start(bo[:], w["L0_attn_a_bo"].partition_broadcast(P)).then_inc(loaded, 16)
                sp.dma_start(ls[:], w["L0_attn_a_layerscale"].partition_broadcast(P)).then_inc(loaded, 16)

            @block.tensor
            def _(pe):
                pe.wait_ge(loaded, 9 * 16)
                for i in range(4):
                    last = pe.transpose(ring[0][:, i * P:(i + 1) * P], wnat[:, i, :], ident[:])
                last.then_inc(w_turned, 1)
                pe.wait_ge(w_ready, 1)
                with pe.Fori(0, BATCH) as b:
                    pe.wait_ge(hn_ready, b + 1)
                    for g in range(2):
                        for j in range(4):
                            last = pe.transpose(ring[g][:, j * P:(j + 1) * P], hn[:, 4 * g + j, :], ident[:])
                        last.then_inc(turned, 1)
                    for j in range(TPB):
                        if j < 2:
                            pe.wait_ge(evac, 6 * b + 2)
                        else:
                            pe.wait_ge(qkv_taken, TPB * b + j - 1)
                        pe.matmul(ring[j % 2][:, 0:3 * D], hT[:, j * P:(j + 1) * P],
                                  wT[:, 0:3, :].rearrange("p a e -> p (a e)"), start=True, stop=True).then_inc(qkv_made, 1)
                    pe.wait_ge(qk_ready, b + 1)
                    for g in range(4):
                        if g >= 2:
                            pe.wait_ge(evac, 6 * b + g + 1)
                        for j in range(4):
                            last = pe.transpose(ring[g % 2][:, j * P:(j + 1) * P], qkv[:, 4 * (g % 2) + j, g // 2, :], ident[:])
                        last.then_inc(turned, 1)

                    def scores(u):
                        t, h = u // 2, u % 2
                        if u >= 2:
                            pe.wait_ge(attn_ready, 16 * b + u - 1)
                        pe.matmul(score[u % 2][:], qkT[:, 1, t * P:(t + 1) * P], qkT[:, 0, h * HALF:(h + 1) * HALF],
                                  start=True, stop=True).then_inc(scored, 1)

                    pe.wait_ge(evac, 6 * b + 6)
                    scores(0)
                    for u in range(2 * TPB):
                        if u + 1 < 2 * TPB:
                            scores(u + 1)
                        t, h = u // 2, u % 2
                        pe.wait_ge(attn_ready, 16 * b + u + 1)
                        pe.matmul(acc[h][:], qkv[:, t, 2, :], AT[:, u % 3, :], start=t == 0, stop=t == TPB - 1).then_inc(pv_done, 1)
                    for h in range(2):
                        pe.wait_ge(o_ready, 2 * b + h + 1)
                        for j in range(4):
                            last = pe.matmul(proj[h][:, j * D:(j + 1) * D], oT[:, (4 * h + j) * P:(4 * h + j + 1) * P],
                                             wT[:, 3, :], start=True, stop=True)
                        last.then_inc(proj_done, 1)

            @block.scalar
            def _(act):
                act.wait_ge(consts, 1)
                with act.Fori(0, BATCH) as b:
                    norm.act(act, hn[:], TPB, 2 * b)
                    for g in range(2):
                        act.wait_ge(turned, 6 * b + g + 1)
                        act.activation(hT[:, g * HALF:(g + 1) * HALF], ring[g][:], ACT.Copy).then_inc(evac, 1)
                    norm.act(act, qkv[:, :, 0:2, :], 2 * TPB, 2 * b + 1)
                    for g in range(4):
                        act.wait_ge(turned, 6 * b + 3 + g)
                        act.activation(qkT[:, g // 2, (g % 2) * HALF:(g % 2 + 1) * HALF], ring[g % 2][:], ACT.Copy).then_inc(evac, 1)
                    for u in range(2 * TPB):
                        act.wait_ge(scored, 16 * b + u + 1)
                        if u >= 3:
                            act.wait_ge(pv_done, 16 * b + u - 2)
                        act.activation(AT[:, u % 3, :], score[u % 2][:], ACT.Sigmoid, bias=neg_log[:],
                                       scale=1.0 / math.sqrt(D)).then_inc(attn_ready, 1)
                    for h in range(2):
                        act.wait_ge(pv_done, 16 * b + 15 + h)
                        act.activation(oT[:, h * HALF:(h + 1) * HALF], acc[h][:], ACT.Copy).then_inc(o_ready, 1)

            @block.vector
            def _(dve):
                chain = Chain(dve, shared)
                dve.memset(neg_log[:], -math.log(float(SEQ))).then_inc(consts, 1)
                dve.wait_ge(loaded, 9 * 16)
                dve.wait_ge(w_turned, 1)
                dve.tensor_copy(wT[:].rearrange("p a e -> p (a e)"), ring[0][:]).then_inc(w_ready, 1)
                with dve.Fori(0, BATCH) as b:
                    chain.enter(b, 2 * norm.LINKS + 2 * 2)
                    Xb = X[:, bass.ds(b * TPB, TPB), :]
                    norm.dve(dve, chain, Xb, hn[:], TPB, 2 * b).then_inc(hn_ready, 1)
                    for j in range(TPB):
                        dve.wait_ge(qkv_made, TPB * b + j + 1)
                        dve.tensor_tensor(qkv[:, j, :, :].rearrange("p a e -> p (a e)"), ring[j % 2][:, 0:3 * D],
                                          bqkv[:].rearrange("p a e -> p (a e)"), ALU.add).then_inc(qkv_taken, 1)
                    dve.wait_ge(qkv_taken, TPB * (b + 1))
                    norm.dve(dve, chain, qkv[:, :, 0:2, :], qkv[:, :, 0:2, :], 2 * TPB, 2 * b + 1).then_inc(qk_ready, 1)
                    for h in range(2):
                        dve.wait_ge(proj_done, 2 * b + h + 1)
                        wide = lambda t: t[:].unsqueeze(1).to_broadcast([P, 4, D])
                        Xh = X[:, bass.ds(b * TPB + 4 * h, 4), :]
                        chain.link(dve.tensor_tensor(upd[:, h], proj[h][:].rearrange("p (j e) -> p j e", e=D), wide(bo), ALU.add))
                        chain.link(dve.tensor_tensor(upd[:, h], upd[:, h], wide(ls), ALU.mult))
                        dve.tensor_tensor(Xh, Xh, upd[:, h], ALU.add).then_inc(proj_taken, 1)
                chain.leave(BATCH)
                chain.close()


EXPERTS = 8
HIDDEN = 512
HC = HIDDEN // P
ROWS = 512
BLOCKS = 2 * BATCH * SEQ // ROWS + EXPERTS
CLAMP = 10000.0


class ExpertWeights:

    def __init__(self, nc):
        dram = lambda name, shape: nc.dram_tensor(name, shape, F32, kind="Internal").ap()
        self.w12 = dram("f_w12", [EXPERTS * P, 2 * HIDDEN])
        self.bias = dram("f_bias", [EXPERTS * P, 4 * HC])


def fold_expert_weights(nc, w, folded, shared):
    with ExitStack() as ctx:
        sb = lambda name, shape, dt=F32: ctx.enter_context(nc.sbuf_tensor("fw_" + name, shape, dt))
        sem = lambda name: ctx.enter_context(nc.semaphore("fw_" + name))
        eg, eb = sb("eg", [P, EXPERTS]), sb("eb", [P, EXPERTS])
        b12 = sb("b12", [P, EXPERTS, 2 * HC])
        wbuf = [sb(f"wbuf{i}", [P, 2, HIDDEN]) for i in range(2)]
        wg = [sb(f"wg{i}", [P, 2, HIDDEN]) for i in range(2)]
        bout = [sb(f"bout{i}", [P, 4, HC]) for i in range(2)]
        rows = ctx.enter_context(nc.psum_tensor("fw_rows", [P, 2, HALF], F32))
        vec_loaded, made, scaled, bias_ready = (sem(n) for n in ("vec_loaded", "made", "scaled", "bias_ready"))
        loaded, stored = ([sem(f"{n}{i}") for i in range(2)] for n in ("loaded", "stored"))

        with nc.allow_non_contiguous_dma("small vectors, once"), nc.Block() as block:

            @block.sync
            def _(sp):
                sp.dma_start(eg[:], w["L0_ffn_eg"].rearrange("e d -> d e")).then_inc(vec_loaded, 16)
                sp.dma_start(eb[:], w["L0_ffn_eb"].rearrange("e d -> d e")).then_inc(vec_loaded, 16)
                for a, name in enumerate(("b1", "b2")):
                    for e in range(EXPERTS):
                        sp.dma_start(b12[:, e, a * HC:(a + 1) * HC], w["L0_ffn_" + name][e, :].rearrange("(c p) -> p c", p=P))\
                          .then_inc(vec_loaded, 16)
                for e in range(EXPERTS):
                    if e >= 2:
                        sp.wait_ge(made, e - 1)
                        sp.wait_ge(scaled, e - 1)
                    for a, name in enumerate(("W1", "W2")):
                        sp.dma_start(wbuf[e % 2][:, a, :], w["L0_ffn_" + name][e, :, :]).then_inc(loaded[e % 2], 16)

            @block.scalar
            def _(act):
                for e in range(EXPERTS):
                    act.wait_ge(bias_ready, e + 1)
                    act.dma_start(folded.w12[e * P:(e + 1) * P, :], wg[e % 2][:].rearrange("p a h -> p (a h)")).then_inc(stored[e % 2], 16)
                    act.dma_start(folded.bias[e * P:(e + 1) * P, :], bout[e % 2][:].rearrange("p a c -> p (a c)")).then_inc(stored[e % 2], 16)
                for i in range(2):
                    act.wait_ge(stored[i], 16 * EXPERTS)

            @block.tensor
            def _(pe):
                pe.wait_ge(vec_loaded, 16 * (2 + 2 * EXPERTS))
                for e in range(EXPERTS):
                    pe.wait_ge(loaded[e % 2], 32 * (e // 2 + 1))
                    if e >= 2:
                        pe.wait_ge(bias_ready, e - 1)
                    for a in range(2):
                        for c in range(HC):
                            last = pe.matmul(rows[:, e % 2, a * HC + c:a * HC + c + 1], wbuf[e % 2][:, a, c * P:(c + 1) * P],
                                             eb[:, e:e + 1], start=True, stop=True)
                    last.then_inc(made, 1)

            @block.vector
            def _(dve):
                chain = Chain(dve, shared)
                dve.wait_ge(vec_loaded, 16 * (2 + 2 * EXPERTS))
                for e in range(EXPERTS):
                    dve.wait_ge(loaded[e % 2], 32 * (e // 2 + 1))
                    if e >= 2:
                        dve.wait_ge(stored[e % 2], 32 * (e // 2))
                    dve.tensor_scalar(wg[e % 2][:], wbuf[e % 2][:], eg[:, e:e + 1], None, ALU.mult).then_inc(scaled, 1)
                    dve.wait_ge(made, e + 1)
                    flat = bout[e % 2][:, 0:2, :].rearrange("p a c -> p (a c)")
                    chain.link(dve.tensor_tensor(flat, rows[:, e % 2, 0:2 * HC], b12[:, e, :], ALU.add))
                    dve.tensor_scalar(bout[e % 2][:, 2, :], bout[e % 2][:, 1, :], -1.0, -20.0, ALU.mult, ALU.add)
                    dve.tensor_scalar(bout[e % 2][:, 3, :], bout[e % 2][:, 1, :], -1.0, 20.0, ALU.mult, ALU.add).then_inc(bias_ready, 1)
                chain.close()


def gated_experts(nc, X, ident, w, folded, shared, tag):
    dram = lambda name, shape: nc.dram_tensor(tag + name, shape, F32, kind="Internal").ap()
    z_sorted = dram("z_sorted", [BLOCKS * ROWS, D])
    y_sorted = dram("y_sorted", [BLOCKS * ROWS, D])
    with ExitStack() as ctx:
        sb = lambda name, shape, dt=F32: ctx.enter_context(nc.sbuf_tensor(tag + name, shape, dt))
        slots = sb("slots", [P, 2, TILES], mybir.dt.uint32)
        gates = sb("gates", [P, 2, TILES])
        expert_of = sb("expert_of", [P, BLOCKS], mybir.dt.int32)
        with ExitStack() as inner:
            zall = inner.enter_context(nc.sbuf_tensor(tag + "zall", [P, TILES, D], F32))
            logits = inner.enter_context(nc.sbuf_tensor(tag + "logits", [P, TILES, EXPERTS], F32))
            route_inputs(nc, X, ident, w, zall, logits, z_sorted, shared, tag + "r_")
            sort_rows(nc, zall, logits, slots, gates, expert_of, z_sorted, shared, tag + "s_")
        run_experts(nc, ident, w, folded, expert_of, z_sorted, y_sorted, shared, tag + "e_")
        combine(nc, X, slots, gates, y_sorted, tag + "c_")


def route_inputs(nc, X, ident, w, zall, logits, z_sorted, shared, tag):
    with ExitStack() as ctx:
        sb = lambda name, shape, dt=F32: ctx.enter_context(nc.sbuf_tensor(tag + name, shape, dt))
        sem = lambda name: ctx.enter_context(nc.semaphore(tag + name))
        norm = Norm(sb, shared, TPB, 3 * BATCH)
        gain, shift = sb("gain", [P, D]), sb("shift", [P, D])
        rw = sb("rw", [P, EXPERTS])
        zero = sb("zero", [P, 2, HALF])
        xn = sb("xn", [P, TPB, D])
        xfT = sb("xfT", [P, SEQ])
        turn = [ctx.enter_context(nc.psum_tensor(f"{tag}turn{i}", [P, HALF], F32)) for i in range(2)]
        lg = ctx.enter_context(nc.psum_tensor(tag + "lg", [P, HALF], F32))
        loaded, zeroed, cleared, xf_ready, turned, evac, routed, taken = (
            sem(n) for n in ("loaded", "zeroed", "cleared", "xf_ready", "turned", "evac", "routed", "taken"))

        with nc.Block() as block:

            @block.sync
            def _(sp):
                sp.dma_start(gain[:], w["L0_ffn_ln_g"].partition_broadcast(P)).then_inc(loaded, 16)
                sp.dma_start(shift[:], w["L0_ffn_ln_b"].partition_broadcast(P)).then_inc(loaded, 16)
                sp.dma_start(rw[:], w["L0_ffn_router_w"]).then_inc(loaded, 16)
                sp.wait_ge(zeroed, 1)
                rows = z_sorted.rearrange("(n p k) d -> n p (k d)", p=P, k=8)
                for n in range(BLOCKS * ROWS // (8 * P)):
                    sp.dma_start(rows[n], zero[:].rearrange("p a k -> p (a k)")).then_inc(cleared, 16)
                sp.wait_ge(cleared, 16 * (BLOCKS * ROWS // (8 * P)))

            @block.gpsimd
            def _(pool):
                pool.memset(zero[:], 0.0).then_inc(zeroed, 1)

            @block.tensor
            def _(pe):
                pe.wait_ge(loaded, 48)
                with pe.Fori(0, BATCH) as b:
                    pe.wait_ge(xf_ready, b + 1)
                    for g in range(2):
                        for j in range(4):
                            last = pe.transpose(turn[g][:, j * P:(j + 1) * P], xn[:, 4 * g + j, :], ident[:])
                        last.then_inc(turned, 1)
                    pe.wait_ge(evac, 2 * b + 2)
                    for j in range(TPB):
                        last = pe.matmul(lg[:, j * EXPERTS:(j + 1) * EXPERTS], xfT[:, j * P:(j + 1) * P], rw[:], start=True, stop=True)
                    last.then_inc(routed, 1)

            @block.scalar
            def _(act):
                with act.Fori(0, BATCH) as b:
                    Z = zall[:, bass.ds(b * TPB, TPB), :]
                    norm.act(act, xn[:], TPB, 3 * b)
                    norm.act(act, xn[:], TPB, 3 * b + 1)
                    for g in range(2):
                        act.wait_ge(turned, 2 * b + g + 1)
                        act.activation(xfT[:, g * HALF:(g + 1) * HALF], turn[g][:], ACT.Copy).then_inc(evac, 1)
                    norm.act(act, Z, TPB, 3 * b + 2)

            @block.vector
            def _(dve):
                chain = Chain(dve, shared)
                wide = lambda t: t[:].unsqueeze(1).to_broadcast([P, TPB, D])
                dve.wait_ge(loaded, 48)
                with dve.Fori(0, BATCH) as b:
                    chain.enter(b, 3 * norm.LINKS + 3)
                    Z = zall[:, bass.ds(b * TPB, TPB), :]
                    chain.link(norm.dve(dve, chain, X[:, bass.ds(b * TPB, TPB), :], xn[:], TPB, 3 * b))
                    chain.link(norm.dve(dve, chain, xn[:], xn[:], TPB, 3 * b + 1))
                    chain.link(dve.tensor_tensor(xn[:], xn[:], wide(gain), ALU.mult))
                    dve.tensor_tensor(xn[:], xn[:], wide(shift), ALU.add).then_inc(xf_ready, 1)
                    dve.wait_ge(xf_ready, b + 1)
                    norm.dve(dve, chain, xn[:], Z, TPB, 3 * b + 2)
                    dve.wait_ge(routed, b + 1)
                    dve.tensor_copy(logits[:, bass.ds(b * TPB, TPB), :], lg[:, 0:TPB * EXPERTS].rearrange("p (j e) -> p j e", e=EXPERTS))\
                       .then_inc(taken, 1)
                chain.leave(BATCH)
                chain.close()


def sort_rows(nc, zall, logits, slots, gates, expert_of, z_sorted, shared, tag):
    E8 = EXPERTS
    with ExitStack() as ctx:
        sb = lambda name, shape, dt=F32: ctx.enter_context(nc.sbuf_tensor(tag + name, shape, dt))
        sem = lambda name: ctx.enter_context(nc.semaphore(tag + name))
        tri = sb("tri", [P, E8, E8])
        before = sb("before", [P, P])
        ones = sb("ones", [P, P])
        counts_to = sb("counts_to", [P, E8, TPB])
        block_no = sb("block_no", [P, BLOCKS, E8])
        first_zero = sb("first_zero", [P, E8, TILES])
        cmp = sb("cmp", [P, TILES, E8, E8])
        cmp2 = sb("cmp2", [P, TILES, E8, E8])
        rank = sb("rank", [P, TILES, E8])
        picked = sb("picked", [P, 3, TILES, E8])
        work = sb("work", [P, TILES, E8])
        top = sb("top", [P, 4, TILES])
        per_tile = sb("per_tile", [P, E8, TILES])
        prefix = sb("prefix", [P, E8, TILES])
        pos = sb("pos", [P, TILES, E8])
        blocks_of = sb("blocks_of", [P, E8])
        block_end = sb("block_end", [P, E8])
        start = sb("start", [P, E8])
        cmp3 = sb("cmp3", [P, E8, TPB])
        cmp4 = sb("cmp4", [P, BLOCKS, E8])
        owner = sb("owner", [P, BLOCKS])
        slot_f = sb("slot_f", [P, 2, TILES])
        within = ctx.enter_context(nc.psum_tensor(tag + "within", [P, HALF], F32))
        totals = ctx.enter_context(nc.psum_tensor(tag + "totals", [P, HALF], F32))
        consts, picked_ready, counted, gap_ready, exp_ready, slots_ready, moved = (
            sem(n) for n in ("consts", "picked_ready", "counted", "gap_ready", "exp_ready", "slots_ready", "moved"))
        n_consts = 7

        with nc.Block() as block:

            @block.gpsimd
            def _(pool):
                pool.memset(tri[:], 1.0).then_inc(consts, 1)
                pool.memset(before[:], 1.0).then_inc(consts, 1)
                pool.memset(ones[:], 1.0).then_inc(consts, 1)
                pool.wait_ge(consts, 3)
                pool.affine_select(out=tri[:], in_=tri[:], compare_op=ALU.is_gt, fill=0.0, base=0,
                                   pattern=[[1, E8], [-1, E8]], channel_multiplier=0).then_inc(consts, 1)
                pool.affine_select(out=before[:], in_=before[:], compare_op=ALU.is_gt, fill=0.0, base=0,
                                   pattern=[[1, P]], channel_multiplier=-1).then_inc(consts, 1)
                pool.iota(counts_to[:], pattern=[[0, E8], [ROWS, TPB]], base=0, channel_multiplier=0,
                          allow_small_or_imprecise_dtypes=True).then_inc(consts, 1)
                pool.iota(block_no[:], pattern=[[1, BLOCKS], [0, E8]], base=0, channel_multiplier=0,
                          allow_small_or_imprecise_dtypes=True).then_inc(consts, 1)
                pool.wait_ge(slots_ready, 1)
                for n in range(TILES):
                    for k in range(2):
                        pool.indirect_dma_start(out=z_sorted, out_offset=bass.IndirectOffsetOnAxis(ap=slots[:, k, n:n + 1], axis=0),
                                                in_=zall[:, n, :], in_offset=None).then_inc(moved, 16)
                pool.wait_ge(moved, 32 * TILES)

            @block.tensor
            def _(pe):
                pe.wait_ge(consts, n_consts)
                pe.wait_ge(picked_ready, 1)
                flat = picked[:, 2, :, :].rearrange("p n e -> p (n e)")
                pe.matmul(within[:, 0:TILES * E8], before[:], flat, start=True, stop=True)
                pe.matmul(totals[:, 0:TILES * E8], ones[:], flat, start=True, stop=True).then_inc(counted, 1)

            @block.scalar
            def _(act):
                act.wait_ge(gap_ready, 1)
                act.activation(top[:, 3, :], top[:, 2, :], ACT.Exp).then_inc(exp_ready, 1)

            @block.vector
            def _(dve):
                chain = Chain(dve, shared)
                link, tt, ts = chain.link, dve.tensor_tensor, dve.tensor_scalar
                full = [P, TILES, E8, E8]
                other, own = logits[:].unsqueeze(2).to_broadcast(full), logits[:].unsqueeze(3).to_broadcast(full)
                dve.wait_ge(consts, n_consts)
                tt(cmp[:], other, own, ALU.is_gt)
                link(tt(cmp2[:], other, own, ALU.is_equal))
                link(tt(cmp2[:], cmp2[:], tri[:].unsqueeze(1).to_broadcast(full), ALU.mult))
                link(tt(cmp[:], cmp[:], cmp2[:], ALU.add))
                link(dve.tensor_reduce(rank[:], cmp[:], AX, ALU.add))
                link(ts(picked[:, 0], rank[:], 0.0, None, ALU.is_equal))
                link(ts(picked[:, 1], rank[:], 1.0, None, ALU.is_equal))
                tt(picked[:, 2], picked[:, 0], picked[:, 1], ALU.add).then_inc(picked_ready, 1)
                link(tt(work[:], logits[:], picked[:, 1], ALU.mult))
                link(dve.tensor_reduce(top[:, 1, :], work[:], AX, ALU.add))
                link(dve.tensor_reduce(top[:, 0, :], logits[:], AX, ALU.max))
                tt(top[:, 2, :], top[:, 1, :], top[:, 0, :], ALU.subtract).then_inc(gap_ready, 1)
                dve.wait_ge(exp_ready, 1)
                link(ts(top[:, 0, :], top[:, 3, :], 1.0, None, ALU.add))
                link(dve.reciprocal(gates[:, 0, :], top[:, 0, :]))
                link(tt(gates[:, 1, :], gates[:, 0, :], top[:, 3, :], ALU.mult))
                link(dve.memset(first_zero[:], 1.0))
                link(dve.memset(first_zero[:, :, 0:1], 0.0))
                dve.wait_ge(counted, 1)
                link(dve.tensor_copy(per_tile[:], totals[:, 0:TILES * E8].rearrange("p (n e) -> p e n", e=E8)))
                flat = lambda t: t[:].rearrange("p e n -> p (e n)")
                link(dve.tensor_tensor_scan(flat(prefix), flat(first_zero), flat(per_tile), 0.0, ALU.mult, ALU.add))
                link(tt(cmp3[:], prefix[:, :, TILES - 1:TILES].to_broadcast([P, E8, TPB]), counts_to[:], ALU.is_gt))
                link(dve.tensor_reduce(blocks_of[:], cmp3[:], AX, ALU.add))
                link(dve.memset(start[:], 1.0))
                link(dve.tensor_tensor_scan(block_end[:], start[:], blocks_of[:], 0.0, ALU.mult, ALU.add))
                link(tt(start[:], block_end[:], blocks_of[:], ALU.subtract))
                link(ts(start[:], start[:], float(ROWS), None, ALU.mult))
                link(tt(cmp4[:], block_end[:].unsqueeze(1).to_broadcast([P, BLOCKS, E8]), block_no[:], ALU.is_le))
                link(dve.tensor_reduce(owner[:], cmp4[:], AX, ALU.add))
                link(ts(expert_of[:], owner[:], float(E8 - 1), None, ALU.min))
                link(tt(prefix[:], prefix[:], per_tile[:], ALU.subtract))
                link(tt(prefix[:], prefix[:], start[:].unsqueeze(2).to_broadcast([P, E8, TILES]), ALU.add))
                link(tt(pos[:], within[:, 0:TILES * E8].rearrange("p (n e) -> p n e", e=E8),
                        prefix[:].rearrange("p e n -> p n e"), ALU.add))
                for k in range(2):
                    link(tt(work[:], pos[:], picked[:, k], ALU.mult))
                    link(dve.tensor_reduce(slot_f[:, k, :], work[:], AX, ALU.add))
                dve.tensor_copy(slots[:], slot_f[:]).then_inc(slots_ready, 1)
                chain.close()


def run_experts(nc, ident, w, folded, expert_of, z_sorted, y_sorted, shared, tag):
    QB = ROWS // P
    with ExitStack() as ctx:
        sb = lambda name, shape, dt=F32: ctx.enter_context(nc.sbuf_tensor(tag + name, shape, dt))
        bank = lambda name: ctx.enter_context(nc.psum_tensor(tag + name, [P, HALF], F32))
        sem = lambda name: ctx.enter_context(nc.semaphore(tag + name))
        both = lambda name, shape: [sb(f"{name}{i}", shape) for i in range(2)]
        w12 = both("w12", [P, 2, HIDDEN])
        wo = both("wo", [P, HC, D])
        bias = both("bias", [P, 4, HC])
        bo = both("bo", [P, D])
        z = both("z", [P, QB, D])
        zT = both("zT", [P, ROWS])
        x2 = both("x2", [P, ROWS])
        act2 = both("act2", [P, ROWS])
        hid = both("hid", [P, ROWS])
        hT = both("hT", [P, HC, ROWS])
        y = both("y", [P, QB, D])
        turn = bank("turn")
        p1 = [bank(f"p1{i}") for i in range(2)]
        p2 = [bank(f"p2{i}") for i in range(2)]
        py = [bank(f"py{i}") for i in range(2)]
        turned, zT_ready, x2_done, up_done, x2_ready, act_ready, x1_taken, hT_ready, down_done, y_ready = (
            sem(n) for n in ("turned", "zT_ready", "x2_done", "up_done", "x2_ready", "act_ready", "x1_taken", "hT_ready", "down_done", "y_ready"))
        up_loaded, down_loaded, z_loaded, stored = ([sem(f"{n}{i}") for i in range(2)]
                                                    for n in ("up_loaded", "down_loaded", "z_loaded", "stored"))

        def loop(eng, step):
            for t in range(4):
                step(t // 2, t, t % 2)
            with eng.Fori(2, BLOCKS // 2) as j:
                for par in range(2):
                    step(j, 2 * j + par, par)

        z_view = z_sorted.rearrange("(t q p) d -> t p q d", q=QB, p=P)
        y_view = y_sorted.rearrange("(t q p) d -> t p q d", q=QB, p=P)

        with nc.Block() as block:

            @block.sync
            def _(sp):
                def load_rows(t, par):
                    sp.dma_start(z[par][:], z_view[bass.ds(t, 1), :, :, :].rearrange("a p q d -> (a p) q d")).then_inc(z_loaded[par], 16)

                def step(j, t, par):
                    e = sp.value_load(expert_of[0:1, bass.ds(t, 1)], min_val=0, max_val=EXPERTS - 1)
                    row, after = e * P, (t + 1) % BLOCKS
                    first = isinstance(t, int) and t < 2
                    if not (isinstance(t, int) and t == 0):
                        sp.wait_ge(turned, t)
                    load_rows(after, 1 - par)
                    if not first:
                        sp.wait_ge(x1_taken, HC * (t - 1))
                    sp.dma_start(w12[par][:].rearrange("p a h -> p (a h)"), folded.w12[bass.ds(row, P), :]).then_inc(up_loaded[par], 16)
                    sp.dma_start(bias[par][:].rearrange("p a c -> p (a c)"), folded.bias[bass.ds(row, P), :]).then_inc(up_loaded[par], 16)
                    if not first:
                        sp.wait_ge(y_ready, t - 1)
                    sp.dma_start(wo[par][:], w["L0_ffn_Wo"][bass.ds(e, 1), :, :].rearrange("a (c p) d -> (a p) c d", p=P)).then_inc(down_loaded[par], 16)
                    sp.dma_start(bo[par][:], w["L0_ffn_bo"][bass.ds(e, 1), :].rearrange("a d -> (a d)").partition_broadcast(P)).then_inc(down_loaded[par], 16)

                load_rows(0, 0)
                loop(sp, step)
                sp.wait_ge(z_loaded[0], 16 * (BLOCKS // 2 + 1))

            @block.tensor
            def _(pe):
                def up(t, par, c):
                    n = HC * t + c
                    if not (isinstance(n, int) and n < 2):
                        pe.wait_ge(x1_taken, n - 1)
                    pe.matmul(p2[c % 2][:], w12[par][:, 1, c * P:(c + 1) * P], zT[par][:], start=True, stop=True).then_inc(x2_done, 1)
                    pe.matmul(p1[c % 2][:], w12[par][:, 0, c * P:(c + 1) * P], zT[par][:], start=True, stop=True).then_inc(up_done, 1)

                def down(j, t, par, q):
                    if q == 0:
                        pe.wait_ge(down_loaded[par], 32 * (j + 1))
                        pe.wait_ge(hT_ready, HC * (t + 1))
                        if not (isinstance(t, int) and t < 2):
                            pe.wait_ge(y_ready, t - 1)
                    for c in range(HC):
                        last = pe.matmul(py[par][:, q * D:(q + 1) * D], hT[par][:, c, q * P:(q + 1) * P], wo[par][:, c, :],
                                         start=c == 0, stop=c == HC - 1)
                    if q == QB - 1:
                        last.then_inc(down_done, 1)

                def turn_rows(j, t, par):
                    pe.wait_ge(z_loaded[par], 16 * (j + 1))
                    for q in range(QB):
                        last = pe.transpose(turn[:, q * P:(q + 1) * P], z[par][:, q, :], ident[:])
                    last.then_inc(turned, 1)

                def step(j, t, par):
                    pe.wait_ge(up_loaded[par], 32 * (j + 1))
                    pe.wait_ge(zT_ready, t + 1)
                    for c in range(HC):
                        up(t, par, c)
                        if not (isinstance(t, int) and t == 0):
                            down(j - (1 - par), t - 1, 1 - par, c)
                        if c == 2:
                            turn_rows(j + par, t + 1, 1 - par)

                turn_rows(0, 0, 0)
                loop(pe, step)
                for q in range(QB):
                    down(BLOCKS // 2 - 1, BLOCKS - 1, 1, q)

            @block.scalar
            def _(act):
                def store(t, par):
                    act.wait_ge(y_ready, t + 1)
                    act.dma_start(y_view[bass.ds(t, 1), :, :, :].rearrange("a p q d -> (a p) q d"), y[par][:]).then_inc(stored[par], 16)

                def tokens(t, par):
                    act.wait_ge(turned, t + 1)
                    act.activation(zT[par][:], turn[:], ACT.Copy).then_inc(zT_ready, 1)

                def step(j, t, par):
                    for c in range(HC):
                        act.wait_ge(x2_ready, HC * t + c + 1)
                        act.activation(act2[c % 2][:], x2[c % 2][:], ACT.Silu, bias=bias[par][:, 1, c:c + 1]).then_inc(act_ready, 1)
                        if c == 1 and not (isinstance(t, int) and t < 2):
                            store(t - 2, par)
                        if c == 2:
                            tokens(t + 1, 1 - par)

                tokens(0, 0)
                loop(act, step)
                for par in range(2):
                    store(BLOCKS - 2 + par, par)
                for par in range(2):
                    act.wait_ge(stored[par], 16 * (BLOCKS // 2))

            @block.vector
            def _(dve):
                chain = Chain(dve, shared)

                def finish(j, t, par):
                    dve.wait_ge(down_done, t + 1)
                    if not isinstance(t, int) or t >= 2:
                        dve.wait_ge(stored[par], 16 * j)
                    chain.link(dve.tensor_tensor(y[par][:], py[par][:].rearrange("p (q d) -> p q d", d=D),
                                                 bo[par][:].unsqueeze(1).to_broadcast([P, QB, D]), ALU.add))
                    dve.tensor_scalar(y[par][:], y[par][:], CLAMP, -CLAMP, ALU.min, ALU.max).then_inc(y_ready, 1)

                def step(j, t, par):
                    dve.wait_ge(up_loaded[par], 32 * (j + 1))
                    for c in range(HC):
                        dve.wait_ge(x2_done, HC * t + c + 1)
                        dve.tensor_scalar(x2[c % 2][:], p2[c % 2][:], bias[par][:, 2, c:c + 1], bias[par][:, 3, c:c + 1],
                                          ALU.max, ALU.min).then_inc(x2_ready, 1)
                        product(t, par, c)
                        if c == 0 and not (isinstance(t, int) and t < 2):
                            finish(j - 1, t - 2, par)

                def product(t, par, c):
                    dve.wait_ge(act_ready, HC * t + c + 1)
                    dve.wait_ge(up_done, HC * t + c + 1)
                    dve.scalar_tensor_tensor(hid[c % 2][:], p1[c % 2][:], bias[par][:, 0, c:c + 1], act2[c % 2][:],
                                             ALU.add, ALU.mult).then_inc(x1_taken, 1)
                    dve.wait_ge(x1_taken, HC * t + c + 1)
                    if not (isinstance(t, int) and t < 2) and c == 0:
                        dve.wait_ge(down_done, t - 1)
                    dve.tensor_scalar(hT[par][:, c, :], hid[c % 2][:], CLAMP, -CLAMP, ALU.min, ALU.max).then_inc(hT_ready, 1)

                for t in range(4):
                    step(t // 2, t, t % 2)
                with dve.Fori(2, BLOCKS // 2) as j:
                    chain.enter_from(j, 2, 2)
                    for par in range(2):
                        step(j, 2 * j + par, par)
                chain.leave(BLOCKS // 2 - 2)
                for par in range(2):
                    finish(BLOCKS // 2 - 1, BLOCKS - 2 + par, par)
                chain.close()


def combine(nc, X, slots, gates, y_sorted, tag):
    with ExitStack() as ctx:
        sem = lambda name: ctx.enter_context(nc.semaphore(tag + name))
        DEPTH = 4
        rows = [ctx.enter_context(nc.sbuf_tensor(f"{tag}rows{i}", [P, D], F32)) for i in range(DEPTH)]
        fetched = [sem(f"fetched{i}") for i in range(DEPTH)]
        added = sem("added")
        per = DEPTH // 2

        with nc.Block() as block:

            @block.gpsimd
            def _(pool):
                for m in range(TILES // per):
                    for i in range(DEPTH):
                        k, n = i % 2, m * per + i // 2
                        if m > 0:
                            pool.wait_ge(fetched[i], 16 * m)
                            pool.wait_ge(added, DEPTH * (m - 1) + i + 1)
                        pool.indirect_dma_start(out=rows[i][:], out_offset=None, in_=y_sorted,
                                                in_offset=bass.IndirectOffsetOnAxis(ap=slots[:, k, n:n + 1], axis=0))\
                            .then_inc(fetched[i], 16)

            @block.vector
            def _(dve):
                with dve.Fori(0, TILES // per) as m:
                    for i in range(DEPTH):
                        k, n = i % 2, m * per + i // 2
                        Xn = X[:, bass.ds(n, 1), :].rearrange("p a d -> p (a d)")
                        dve.wait_ge(fetched[i], 16 * (m + 1))
                        if k:
                            dve.wait_ge(added, DEPTH * m + i)
                        dve.scalar_tensor_tensor(Xn, rows[i][:], gates[:, k, bass.ds(n, 1)], Xn, ALU.mult, ALU.add).then_inc(added, 1)


HEADS = 16
HD = 64
KV_BLOCK = 64
NB = SEQ // KV_BLOCK
PAIRS = BATCH * HEADS // 2
QT = 2
GT = 2 * QT
GPP = TPB // QT
LAG = 3
BIG = 3.0e38


def head_inputs(nc, X, ident, hT_dram, shared, tag):
    with ExitStack() as ctx:
        sb = lambda name, shape, dt=F32: ctx.enter_context(nc.sbuf_tensor(tag + name, shape, dt))
        sem = lambda name: ctx.enter_context(nc.semaphore(tag + name))
        norm = Norm(sb, shared, TPB, BATCH)
        hn = sb("hn", [P, TPB, D])
        hT = sb("hT", [P, SEQ])
        ring = [ctx.enter_context(nc.psum_tensor(f"{tag}ring{i}", [P, HALF], F32)) for i in range(2)]
        hn_ready, turned, evac, stored = (sem(n) for n in ("hn_ready", "turned", "evac", "stored"))

        with nc.Block() as block:

            @block.tensor
            def _(pe):
                with pe.Fori(0, BATCH) as b:
                    pe.wait_ge(hn_ready, b + 1)
                    for g in range(2):
                        for j in range(4):
                            last = pe.transpose(ring[g][:, j * P:(j + 1) * P], hn[:, 4 * g + j, :], ident[:])
                        last.then_inc(turned, 1)

            @block.scalar
            def _(act):
                with act.Fori(0, BATCH) as b:
                    norm.act(act, hn[:], TPB, b)
                    for g in range(2):
                        act.wait_ge(turned, 2 * b + g + 1)
                        act.activation(hT[:, g * HALF:(g + 1) * HALF], ring[g][:], ACT.Copy).then_inc(evac, 1)

            @block.vector
            def _(dve):
                chain = Chain(dve, shared)
                with dve.Fori(0, BATCH) as b:
                    chain.enter(b, norm.LINKS)
                    norm.dve(dve, chain, X[:, bass.ds(b * TPB, TPB), :], hn[:], TPB, b).then_inc(hn_ready, 1)
                    dve.wait_ge(evac, 2 * (b + 1))
                    dve.wait_ge(stored, 16 * (b + 1))
                chain.leave(BATCH)
                chain.close()

            @block.sync
            def _(sp):
                with sp.Fori(0, BATCH) as b:
                    made, token = sp.snap(2 * (b + 1)), sp.snap(b * SEQ)
                    sp.wait_ge(evac, made)
                    sp.dma_start(hT_dram[:, bass.ds(token, SEQ)], hT[:]).then_inc(stored, 16)


def block_softmax_attention(nc, X, ident, w, shared):
    hT_dram = nc.dram_tensor("b_hT", [D, BATCH * SEQ], F32, kind="Internal").ap()
    head_inputs(nc, X, ident, hT_dram, shared, "bh_")
    with ExitStack() as ctx:
        sb = lambda name, shape, dt=F32: ctx.enter_context(nc.sbuf_tensor("b_" + name, shape, dt))
        psum = lambda name, cols: ctx.enter_context(nc.psum_tensor("b_" + name, [P, cols], F32))
        sem = lambda name: ctx.enter_context(nc.semaphore("b_" + name))

        hb = [sb(f"hb{i}", [P, SEQ]) for i in range(2)]
        wqkv = [sb(f"wqkv{i}", [P, 3, P]) for i in range(2)]
        QS = [[sb(f"QS{i}{h}", [P, SEQ], F32R) for h in range(2)] for i in range(2)]
        KH = [[sb(f"KH{i}{h}", [P, SEQ], F32R) for h in range(2)] for i in range(2)]
        KL = [[sb(f"KL{i}{h}", [P, SEQ], F32R) for h in range(2)] for i in range(2)]
        V = [sb(f"V{i}", [P, TPB, P]) for i in range(2)]
        parts = {"q": (sb("q_high", [P, SEQ], F32R), sb("q_low", [P, SEQ], F32R)),
                 "k": (sb("k_high", [P, SEQ], F32R), sb("k_low", [P, SEQ], F32R))}
        wo = sb("wo", [P, HEADS // 2, D])
        prob = [[sb(f"prob{i}{t}", [P, SEQ]) for t in range(GT)] for i in range(4)]
        bmax = [sb(f"bmax{i}", [P, GT, NB]) for i in range(2)]
        bsum = [sb(f"bsum{i}", [P, GT, NB]) for i in range(2)]
        neg_m = [sb(f"neg_m{i}", [P, GT]) for i in range(2)]
        run_max = sb("run_max", [P, GT, NB])
        run_sum = sb("run_sum", [P, GT, NB])
        drop = sb("drop", [P, GT, NB])
        rise = sb("rise", [P, GT, NB])
        inv_l = sb("inv_l", [P, GT, NB])
        weight = [sb(f"weight{i}", [P, GT, NB]) for i in range(2)]
        first_low = sb("first_low", [P, GT, NB])
        first_zero = sb("first_zero", [P, GT, NB])
        last_one = sb("last_one", [P, GT, NB])
        pT = [sb(f"pT{i}", [P, HALF]) for i in range(4)]
        oT = [sb(f"oT{i}", [P, QT * P]) for i in range(2)]

        score = [psum(f"score{i}", SEQ) for i in range(2)]
        turn = [psum(f"turn{i}", HALF) for i in range(2)]
        acc = psum("acc", HALF)
        misc = psum("misc", HALF)

        names = ("wo_loaded", "loaded", "scored", "max_ready", "prob_ready", "drop_ready", "rise_ready",
                 "weight_ready", "scaled", "turned", "evac", "pv_done", "o_ready", "wo_done", "wo_taken",
                 "qk_made", "high_ready", "qk_taken", "q_dealt", "k_dealt", "v_made", "v_taken")
        s = {n: sem(n) for n in names}
        (wo_loaded, loaded, scored, max_ready, prob_ready, drop_ready, rise_ready,
         weight_ready, scaled, turned, evac, pv_done, o_ready, wo_done, wo_taken,
         qk_made, high_ready, qk_taken, q_dealt, k_dealt, v_made, v_taken) = (s[n] for n in names)

        flat = lambda t: t[:].rearrange("p t n -> p (t n)")
        Wq, Wk, Wv, Wo = (w["L0_attn_b_" + n] for n in ("Wq", "Wk", "Wv", "Wo"))

        def slots(eng, slot):
            for r in range(8):
                slot(0, r, True, r >= LAG)
            with eng.Fori(1, PAIRS // 2) as j:
                for r in range(8):
                    slot(j, r, True, True)
            for r in range(LAG + 1):
                slot(PAIRS // 2, r, False, r < LAG)

        groups = 4 * PAIRS

        with nc.Block() as block:

            @block.sync
            def _(sp):
                raw = lambda ap: ap.bitcast(F32)
                sp.dma_start(wo[:], Wo.rearrange("(c p) d -> p c d", p=P)).then_inc(wo_loaded, 16)

                def places(i):
                    b, hp = (i % PAIRS) // (HEADS // 2), i % (HEADS // 2)
                    return (b * SEQ, hp * P) if isinstance(i, int) else (sp.snap(b * SEQ), sp.snap(hp * P))

                def load(par, token, column):
                    sp.dma_start(hb[par][:], hT_dram[:, bass.ds(token, SEQ)]).then_inc(loaded, 16)
                    for a, W in enumerate((Wq, Wk, Wv)):
                        sp.dma_start(wqkv[par][:, a, :], W[:, bass.ds(column, P)]).then_inc(loaded, 16)

                def deal(kind, par):
                    high, low = parts[kind]
                    for h in range(2):
                        mine = slice(h * HD, (h + 1) * HD)
                        if kind == "q":
                            sp.dma_start(raw(QS[par][h][0:HD, :]), raw(high[mine, :])).then_inc(q_dealt, 16)
                            sp.dma_start(raw(QS[par][h][HD:P, :]), raw(low[mine, :])).then_inc(q_dealt, 16)
                        else:
                            for part, dst in ((high, KH), (low, KL)):
                                sp.dma_start(raw(dst[par][h][0:HD, :]), raw(part[mine, :])).then_inc(k_dealt, 16)
                                sp.dma_start(raw(dst[par][h][HD:P, :]), raw(part[mine, :])).then_inc(k_dealt, 16)

                load(0, *places(0))
                sp.wait_ge(qk_taken, 2)
                deal("q", 0)
                sp.wait_ge(qk_taken, 4)
                deal("k", 0)

                def pair(i, c):
                    par, at = (c + 1) % 2, places(i + 1)
                    fixed = lambda v: v if isinstance(v, int) else sp.snap(v)
                    v_before, q_parts, k_parts = (fixed(v) for v in (2 * i, 4 * i + 6, 4 * i + 8))
                    if c == 1 or not isinstance(i, int):
                        sp.wait_ge(v_made, v_before)
                    load(par, *at)
                    sp.wait_ge(qk_taken, q_parts)
                    deal("q", par)
                    sp.wait_ge(qk_taken, k_parts)
                    deal("k", par)

                for c in range(2):
                    pair(c, c)
                with sp.Fori(1, PAIRS // 2) as j:
                    for c in range(2):
                        pair(2 * j + c, c)
                sp.wait_ge(q_dealt, 64 * (PAIRS + 1))
                sp.wait_ge(k_dealt, 128 * (PAIRS + 1))

            @block.tensor
            def _(pe):
                last_use = [None]

                def misc_free():
                    if last_use[0]:
                        pe.wait_ge(*last_use[0])

                def qk_proj(i, par, u):
                    kind, h = u // 2, u % 2
                    misc_free()
                    if u == 0:
                        pe.wait_ge(loaded, 64 * (i + 1))
                    pe.matmul(misc[:], wqkv[par][:, kind, :], hb[par][:, h * HALF:(h + 1) * HALF],
                              start=True, stop=True).then_inc(qk_made, 1)
                    last_use[0] = (qk_taken, 4 * i + u + 1)

                def v_proj(i, par, h):
                    misc_free()
                    for t in range(4):
                        last = pe.matmul(misc[:, t * P:(t + 1) * P], hb[par][:, (4 * h + t) * P:(4 * h + t + 1) * P],
                                         wqkv[par][:, 2, :], start=True, stop=True)
                    last.then_inc(v_made, 1)
                    last_use[0] = (v_taken, 2 * i + h + 1)

                def pv(g, r, kp):
                    par = (r // GPP) % 2
                    pe.wait_ge(evac, 8 * g + 2 * kp + 2)
                    if kp == 0:
                        if not (isinstance(g, int) and g == 0):
                            pe.wait_ge(o_ready, g)
                        pe.wait_ge(v_taken, 2 * (g // GPP) + 2)
                    for kk in range(2):
                        for h in range(2):
                            kt = 2 * kp + kk
                            last = pe.matmul(acc[h * HD:(h + 1) * HD, 0:QT * P], V[par][:, kt, h * HD:(h + 1) * HD],
                                             pT[(2 * kp + h) % 4][:, kk * QT * P:(kk + 1) * QT * P],
                                             start=kt == 0, stop=kt == TPB - 1)
                    last.then_inc(pv_done, 1)

                def slot(j, r, scores, finish):
                    sl, par = 8 * j + r, r // GPP
                    g, gr = sl - LAG, (r - LAG) % 8
                    before = not (isinstance(sl, int) and sl <= LAG)
                    for k in range(GT):
                        if scores:
                            h, q = k // QT, (r % GPP) * QT + k % QT
                            if k == 0:
                                i = 2 * j + par
                                pe.wait_ge(q_dealt, 64 * (i + 1))
                                pe.wait_ge(k_dealt, 128 * (i + 1))
                            if not (isinstance(sl, int) and sl == 0 and k < 2):
                                pe.wait_ge(prob_ready, 4 * sl + k - 1)
                            for c in range(2):
                                for n, Kx in enumerate((KH, KL)):
                                    last = pe.matmul(score[k % 2][:, c * HALF:(c + 1) * HALF], QS[par][h][:, q * P:(q + 1) * P],
                                                     Kx[par][h][:, c * HALF:(c + 1) * HALF], start=n == 0, stop=n == 1)
                            last.then_inc(scored, 1)
                        if finish:
                            if k == 0:
                                pe.wait_ge(scaled, 4 * g + 4)
                            for h in range(2):
                                if before or k > 0:
                                    pe.wait_ge(evac, 8 * g + 2 * k + h - 1)
                                for kk in range(2):
                                    for q in range(QT):
                                        last = pe.transpose(turn[h][:, (kk * QT + q) * P:(kk * QT + q + 1) * P],
                                                            prob[gr % 4][h * QT + q][:, (2 * k + kk) * P:(2 * k + kk + 1) * P],
                                                            ident[:])
                                last.then_inc(turned, 1)
                        if k == 0 and before:
                            pv(g - 1, (gr - 1) % 8, 3)
                        if k > 0 and finish:
                            pv(g, gr, k - 1)
                        if k == 1 and before:
                            misc_free()
                            pe.wait_ge(o_ready, g)
                            hp = ((g - 1) // GPP) % (HEADS // 2)
                            for q in range(QT):
                                last = pe.matmul(misc[:, q * D:(q + 1) * D], oT[(gr - 1) % 2][:, q * P:(q + 1) * P],
                                                 wo[:, bass.ds(hp, 1), :].rearrange("p a d -> p (a d)"), start=True, stop=True)
                            last.then_inc(wo_done, 1)
                            last_use[0] = (wo_taken, g)
                        if k >= 2 and scores:
                            i, nxt = 2 * j + par, (par + 1) % 2
                            if r % GPP == 1:
                                qk_proj(i + 1, nxt, k - 2)
                            if r % GPP == 2:
                                qk_proj(i + 1, nxt, k)
                            if r % GPP == 3:
                                v_proj(i + 1, nxt, k - 2)

                for u in range(4):
                    qk_proj(0, 0, u)
                for h in range(2):
                    v_proj(0, 0, h)
                pe.wait_ge(wo_loaded, 16)
                for r in range(8):
                    slot(0, r, True, r >= LAG)
                with pe.Fori(1, PAIRS // 2) as j:
                    last_use[0] = (v_taken, 4 * j + 2)
                    for r in range(8):
                        slot(j, r, True, True)
                last_use[0] = (v_taken, 2 * PAIRS + 2)
                for r in range(LAG + 1):
                    slot(PAIRS // 2, r, False, r < LAG)

            @block.scalar
            def _(act):
                def high(i, u):
                    kind, h = "qk"[u // 2], u % 2
                    act.wait_ge(qk_made, 4 * i + u + 1)
                    if not (isinstance(i, int) and i == 0):
                        act.wait_ge(q_dealt if kind == "q" else k_dealt, (64 if kind == "q" else 128) * i)
                    act.activation(parts[kind][0][:, h * HALF:(h + 1) * HALF], misc[:], ACT.Copy,
                                   scale=HD ** -0.5 if kind == "q" else 1.0).then_inc(high_ready, 1)

                def slot(j, r, scores, finish):
                    sl, par = 8 * j + r, r // GPP
                    g, gr = sl - LAG, (r - LAG) % 8
                    before = not (isinstance(sl, int) and sl <= LAG)
                    for k in range(GT):
                        if finish:
                            for h in range(2):
                                act.wait_ge(turned, 8 * g + 2 * k + h + 1)
                                if before or k >= 2:
                                    act.wait_ge(pv_done, 4 * g + k - 1)
                                act.activation(pT[(2 * k + h) % 4][:], turn[h][:], ACT.Copy).then_inc(evac, 1)
                        if scores:
                            act.wait_ge(max_ready, 4 * sl + k + 1)
                            if k == 0 and not (isinstance(sl, int) and sl < 4):
                                act.wait_ge(turned, 8 * (sl - 3))
                            act.activation(prob[r % 4][k][:], score[k % 2][:], ACT.Exp,
                                           bias=neg_m[r % 2][:, k:k + 1]).then_inc(prob_ready, 1)
                        if k == 0 and before:
                            act.wait_ge(pv_done, 4 * g)
                            act.activation(oT[(gr - 1) % 2][:], acc[:, 0:QT * P], ACT.Copy).then_inc(o_ready, 1)
                        if k == 0 and not (isinstance(sl, int) and sl == 0) and (scores or r == 0):
                            act.wait_ge(drop_ready, sl)
                            act.activation(flat(rise), flat(drop), ACT.Exp, scale=-1.0).then_inc(rise_ready, 1)
                        if k >= 2 and scores:
                            if r % GPP == 1:
                                high(2 * j + par + 1, k - 2)
                            if r % GPP == 2:
                                high(2 * j + par + 1, k)

                for u in range(4):
                    high(0, u)
                slots(act, slot)

            @block.vector
            def _(dve):
                chain = Chain(dve, shared)

                def low(i, u):
                    kind, h = "qk"[u // 2], u % 2
                    hi, lo = (t[:, h * HALF:(h + 1) * HALF] for t in parts[kind])
                    dve.wait_ge(high_ready, 4 * i + u + 1)
                    dve.scalar_tensor_tensor(lo, misc[:], HD ** -0.5 if kind == "q" else 1.0, hi.bitcast(F32),
                                             ALU.mult, ALU.subtract).then_inc(qk_taken, 1)

                def v_copy(i, par, h, clear):
                    dve.wait_ge(v_made, 2 * i + h + 1)
                    if clear:
                        dve.wait_ge(pv_done, 16 * (i - 1))
                    dve.tensor_copy(V[par][:, 4 * h:4 * h + 4, :].rearrange("p t e -> p (t e)"), misc[:]).then_inc(v_taken, 1)

                def block_sums(n, r, k):
                    dve.wait_ge(prob_ready, 4 * n + k + 1)
                    return dve.tensor_reduce(bsum[r % 2][:, k, :], prob[r % 4][k][:].rearrange("p (n c) -> p n c", c=KV_BLOCK), AX, ALU.add)

                def weights_begin(n, r):
                    chain.link(dve.tensor_tensor_scan(flat(run_max), flat(first_low), flat(bmax[r % 2]), 0.0, ALU.add, ALU.max))
                    dve.tensor_tensor_scan(flat(run_sum), flat(first_zero), flat(bsum[r % 2]), 0.0, ALU.mult, ALU.add)
                    chain.link(dve.tensor_tensor(run_max[:], run_max[:], neg_m[r % 2][:].unsqueeze(2).to_broadcast([P, GT, NB]), ALU.add))
                    dve.tensor_scalar(flat(drop), flat(run_max), -80.0, None, ALU.max).then_inc(drop_ready, 1)

                def weights_end(n, r, clear):
                    dve.wait_ge(rise_ready, n + 1)
                    chain.link(dve.tensor_tensor(flat(inv_l), flat(rise), flat(run_sum), ALU.mult))
                    chain.link(dve.tensor_scalar(flat(run_sum), flat(inv_l), 1.0, None, ALU.max))
                    chain.link(dve.reciprocal(flat(inv_l), flat(run_sum)))
                    if clear:
                        dve.wait_ge(scaled, 4 * n - 4)
                    dve.tensor_tensor_scan(flat(weight[r % 2])[:, ::-1], flat(last_one)[:, ::-1], flat(inv_l)[:, ::-1], 0.0,
                                           ALU.max, ALU.mult).then_inc(weight_ready, 1)

                def slot(j, r, scores, finish):
                    sl, par = 8 * j + r, r // GPP
                    g, gr = sl - LAG, (r - LAG) % 8
                    first = isinstance(sl, int) and sl == 0
                    before = not (isinstance(sl, int) and sl <= LAG)
                    rest = not first and (scores or r == 0)
                    for k in range(GT):
                        if scores:
                            dve.wait_ge(scored, 4 * sl + k + 1)
                            chain.link(dve.tensor_reduce(bmax[r % 2][:, k, :], score[k % 2][:].rearrange("p (n c) -> p n c", c=KV_BLOCK), AX, ALU.max))
                            dve.tensor_reduce(neg_m[r % 2][:, k:k + 1], bmax[r % 2][:, k, :], AX, ALU.max, negate=True).then_inc(max_ready, 1)
                        if k == 0 and rest:
                            chain.link(block_sums(sl - 1, (r - 1) % 8, GT - 1))
                            weights_begin(sl - 1, (r - 1) % 8)
                        if k == 1 and rest:
                            weights_end(sl - 1, (r - 1) % 8, not (isinstance(sl, int) and sl < 3 and scores))
                        if k > 0 and scores:
                            chain.link(block_sums(sl, r, k - 1))
                        if k == 1 and before:
                            q = (gr - 1) % GPP
                            b = (g - 1) // (4 * HEADS // 2)
                            Xq = X[:, bass.ds(b * TPB + q * QT, QT), :]
                            dve.wait_ge(wo_done, g)
                            dve.tensor_tensor(Xq, misc[:, 0:QT * D].rearrange("p (q d) -> p q d", d=D), Xq, ALU.add).then_inc(wo_taken, 1)
                        if k >= 2 and scores:
                            i, nxt = 2 * j + par + 1, (par + 1) % 2
                            if r % GPP == 1:
                                low(i, k - 2)
                            if r % GPP == 2:
                                low(i, k)
                            if r % GPP == 3:
                                v_copy(i, nxt, k - 2, not (isinstance(i, int) and i < 2))

                chain.link(dve.memset(first_low[:], 0.0))
                chain.link(dve.memset(first_low[:, :, 0:1], -BIG))
                chain.link(dve.memset(first_zero[:], 1.0))
                chain.link(dve.memset(first_zero[:, :, 0:1], 0.0))
                chain.link(dve.memset(last_one[:], 0.0))
                chain.link(dve.memset(last_one[:, :, NB - 1:NB], 1.0))
                for u in range(4):
                    low(0, u)
                for h in range(2):
                    v_copy(0, 0, h, False)

                links = 2 * GT + 2 + 3
                for r in range(8):
                    slot(0, r, True, r >= LAG)
                with dve.Fori(1, PAIRS // 2) as j:
                    chain.enter_from(j, 1, 8 * links)
                    for r in range(8):
                        slot(j, r, True, True)
                chain.leave(PAIRS // 2 - 1)
                for r in range(LAG + 1):
                    slot(PAIRS // 2, r, False, r < LAG)
                chain.close()

            @block.gpsimd
            def _(pool):
                def slot(j, r, scores, finish):
                    n, nr = 8 * j + r - 1, (r - 1) % 8
                    if isinstance(n, int) and (n < 0 or n >= groups):
                        return
                    pool.wait_ge(weight_ready, n + 1)
                    for k in range(GT):
                        tile = prob[nr % 4][k][:].rearrange("p (n c) -> p n c", c=KV_BLOCK)
                        pool.tensor_tensor(tile, tile, weight[nr % 2][:, k, :].unsqueeze(2).to_broadcast([P, NB, KV_BLOCK]),
                                           ALU.mult).then_inc(scaled, 1)

                slots(pool, slot)


def program(nc, w, out):
    with ExitStack() as ctx:
        X = ctx.enter_context(nc.sbuf_tensor("X", [P, TILES, D], F32))
        ident = ctx.enter_context(nc.sbuf_tensor("ident", [P, P], F32))
        shared = Shared(lambda name: ctx.enter_context(nc.semaphore(name)))
        x_loaded = ctx.enter_context(nc.semaphore("x_loaded"))
        ident_made = ctx.enter_context(nc.semaphore("ident_made"))
        x_stored = ctx.enter_context(nc.semaphore("x_stored"))
        tiles = lambda t: t.rearrange("b (n p) d -> p (b n) d", p=P)

        with nc.Block() as block:

            @block.sync
            def _(sp):
                sp.dma_start(X[:], tiles(w["L0_attn_a_x"])).then_inc(x_loaded, 16)
                sp.wait_ge(x_loaded, 16)

            @block.gpsimd
            def _(pool):
                pool.memset(ident[:], 0.0).then_inc(ident_made, 1)
                pool.wait_ge(ident_made, 1)
                pool.affine_select(out=ident[:], in_=ident[:], compare_op=ALU.not_equal, fill=1.0, base=0,
                                   pattern=[[-1, P]], channel_multiplier=1).then_inc(ident_made, 1)
                pool.wait_ge(ident_made, 2)

        folded = ExpertWeights(nc)
        fold_expert_weights(nc, w, folded, shared)
        sigmoid_attention(nc, X, ident, w, shared)
        gated_experts(nc, X, ident, w, folded, shared, "f1_")
        block_softmax_attention(nc, X, ident, w, shared)
        gated_experts(nc, X, ident, w, folded, shared, "f2_")

        with nc.Block() as block:

            @block.sync
            def _(sp):
                sp.dma_start(tiles(out), X[:]).then_inc(x_stored, 16)
                sp.wait_ge(x_stored, 16)


INPUTS = ["L0_attn_a_x", "L0_attn_a_Wq", "L0_attn_a_bq", "L0_attn_a_Wk", "L0_attn_a_bk", "L0_attn_a_Wv", "L0_attn_a_bv",
          "L0_attn_a_Wo", "L0_attn_a_bo", "L0_attn_a_layerscale", "L0_attn_b_Wq", "L0_attn_b_Wk", "L0_attn_b_Wv",
          "L0_attn_b_Wo", "L0_ffn_ln_g", "L0_ffn_ln_b", "L0_ffn_router_w", "L0_ffn_eg", "L0_ffn_eb", "L0_ffn_W1",
          "L0_ffn_b1", "L0_ffn_W2", "L0_ffn_b2", "L0_ffn_Wo", "L0_ffn_bo"]


def kernel(**inputs):
    import numpy as np
    import concourse.bacc as bacc
    from concourse.bass_utils import run_bass_kernel_spmd

    nc = bacc.Bacc("TRN2", target_bir_lowering=False, num_devices=1)
    arrays, w = {}, {}
    for name in INPUTS:
        arrays["in_" + name] = np.ascontiguousarray(inputs[name])
        w[name] = nc.dram_tensor("in_" + name, arrays["in_" + name].shape, F32, kind="ExternalInput").ap()
    out = nc.dram_tensor("out_0", arrays["in_L0_attn_a_x"].shape, F32, kind="ExternalOutput").ap()
    program(nc, w, out)
    r = run_bass_kernel_spmd(nc, [arrays], core_ids=[0])
    return r.results[0]["out_0"]
```

```python
import math
from contextlib import ExitStack

import concourse.bass as bass
from concourse import mybir

F32 = mybir.dt.float32
F32R = mybir.dt.float32r
ALU = mybir.AluOpType
ACT = mybir.ActivationFunctionType
AX = mybir.AxisListType.X

P = 128
D = 128
BATCH = 4
SEQ = 1024
TPB = SEQ // P
TILES = BATCH * TPB
HALF = 512
EPS = 1e-5


class Shared:

    def __init__(self, sem):
        self.chain_sem = sem("dve_chain")
        self.links = 0
        self.norm_sems = [sem("ln_" + n) for n in ("centred", "squared", "var_ready", "std_ready")]
        self.norms = 0


class Chain:

    def __init__(self, eng, shared):
        self.eng, self.shared, self.sem = eng, shared, shared.chain_sem
        self.base, self.k = shared.links, 0

    def close(self):
        self.shared.links = self.base + self.k

    def link(self, ins):
        ins.then_inc(self.sem, 1)
        self.k += 1
        self.eng.wait_ge(self.sem, self.base + self.k)

    def enter(self, i, per):
        self.start, self.per = self.base + self.k, per
        self.base, self.k = i * per + self.start, 0

    def enter_from(self, i, first, per):
        self.start, self.per = self.base + self.k, per
        self.base, self.k = (i - first) * per + self.start, 0

    def leave(self, times):
        assert self.k == self.per, (self.k, self.per)
        self.base, self.k = self.start + times * self.per, 0


class Norm:
    CENTRE, VARIANCE, SCALE = 2, 1, 5

    def __init__(self, sb, shared, rows, calls, ways=1):
        many = lambda name, cols: [sb(f"ln_{name}{i}", [P, cols]) for i in range(ways)]
        self.sums, self.mean, self.var, self.std, self.rstd = (many(n, rows) for n in ("sums", "mean", "var", "std", "rstd"))
        self.sq = many("sq", rows * D)
        self.centred, self.squared, self.var_ready, self.std_ready = shared.norm_sems
        self.before = shared.norms
        shared.norms += calls
        self.LINKS = self.CENTRE + self.VARIANCE + self.SCALE

    @staticmethod
    def wide(t, n, shape):
        per = t[:, 0:n] if len(shape) == 3 else t[:, 0:n].rearrange("p (a b) -> p a b", b=shape[2])
        return per, per.unsqueeze(len(shape) - 1).to_broadcast(shape)

    def centre(self, dve, chain, src, dst, n, call, way=0):
        sums, mean, shape = self.sums[way], self.mean[way], list(src.shape)
        chain.link(dve.tensor_reduce(self.wide(sums, n, shape)[0], src, AX, ALU.add))
        chain.link(dve.tensor_scalar(mean[:, 0:n], sums[:, 0:n], 1.0 / D, None, ALU.mult))
        dve.tensor_tensor(dst, src, self.wide(mean, n, shape)[1], ALU.subtract).then_inc(self.centred, 1)

    def square(self, act, dst, n, call, way=0):
        act.wait_ge(self.centred, self.before + call + 1)
        sq = self.sq[way][:, 0:n * D]
        sq = sq.rearrange("p (n d) -> p n d", d=D) if len(dst.shape) == 3 else sq.rearrange("p (a b d) -> p a b d", b=dst.shape[2], d=D)
        act.activation(sq, dst, ACT.Square).then_inc(self.squared, 1)

    def variance(self, dve, chain, n, call, way=0, gain=1.0, add=EPS):
        dve.wait_ge(self.squared, self.before + call + 1)
        chain.link(dve.tensor_reduce(self.sums[way][:, 0:n], self.sq[way][:, 0:n * D].rearrange("p (n d) -> p n d", d=D), AX, ALU.add))
        dve.tensor_scalar(self.var[way][:, 0:n], self.sums[way][:, 0:n], gain / D, add, ALU.mult, ALU.add).then_inc(self.var_ready, 1)

    def root(self, act, n, call, way=0):
        act.wait_ge(self.var_ready, self.before + call + 1)
        act.activation(self.std[way][:, 0:n], self.var[way][:, 0:n], ACT.Sqrt).then_inc(self.std_ready, 1)

    def scale(self, dve, chain, dst, n, call, way=0):
        sums, mean, var, std, rstd = (t[way][:, 0:n] for t in (self.sums, self.mean, self.var, self.std, self.rstd))
        dve.wait_ge(self.std_ready, self.before + call + 1)
        chain.link(dve.reciprocal(rstd, std))
        chain.link(dve.tensor_tensor(mean, rstd, rstd, ALU.mult))
        chain.link(dve.tensor_tensor(sums, mean, var, ALU.mult))
        chain.link(dve.tensor_scalar(mean, sums, -0.5, 1.5, ALU.mult, ALU.add))
        chain.link(dve.tensor_tensor(rstd, rstd, mean, ALU.mult))
        return dve.tensor_tensor(dst, dst, self.wide(self.rstd[way], n, list(dst.shape))[1], ALU.mult)


SQUARE_AT, ROOT_AT, FOLD_AT = 8, 11, 13


def sigmoid_attention(nc, X, ident, w, folded, shared):
    with ExitStack() as ctx:
        sb = lambda name, shape, dt=F32: ctx.enter_context(nc.sbuf_tensor("a_" + name, shape, dt))
        bank = lambda name: ctx.enter_context(nc.psum_tensor("a_" + name, [P, HALF], F32))
        sem = lambda name: ctx.enter_context(nc.semaphore("a_" + name))

        wnat = sb("wnat", [P, 4, D])
        wT = sb("wT", [P, 4, D])
        bqkv = sb("bqkv", [P, 3, D])
        bo = sb("bo", [P, D])
        ls = sb("ls", [P, D])
        norm = Norm(sb, shared, 2 * TPB, 2 * BATCH, ways=2)
        fold = Fold(sb, sem, w, folded)
        hn = sb("hn", [P, TPB, D])
        hT = sb("hT", [P, SEQ])
        qkv = [sb(f"qkv{i}", [P, TPB, 3, D]) for i in range(2)]
        qkT = [sb(f"qkT{i}", [P, 2, SEQ]) for i in range(2)]
        AT = sb("AT", [P, 3, HALF])
        oT = sb("oT", [P, SEQ])
        upd = sb("upd", [P, 2, 4, D])
        neg_log = sb("neg_log", [P, 1])

        ring = [bank(f"ring{i}") for i in range(2)]
        score = [bank(f"score{i}") for i in range(2)]
        acc = [bank(f"acc{i}") for i in range(2)]
        proj = [bank(f"proj{i}") for i in range(2)]

        loaded = sem("loaded")
        consts = sem("consts")
        w_turned = sem("w_turned")
        w_ready = sem("w_ready")
        hn_ready = sem("hn_ready")
        turned = sem("turned")
        evac = sem("evac")
        qkv_made = sem("qkv_made")
        qkv_taken = sem("qkv_taken")
        qk_ready = sem("qk_ready")
        scored = sem("scored")
        attn_ready = sem("attn_ready")
        pv_done = sem("pv_done")
        o_ready = sem("o_ready")
        proj_done = sem("proj_done")
        proj_taken = sem("proj_taken")


        with nc.allow_non_contiguous_dma("small vectors, once"), nc.Block() as block:

            @block.sync
            def _(sp):
                for i, name in enumerate(("Wq", "Wk", "Wv", "Wo")):
                    sp.dma_start(wnat[:, i, :], w["L0_attn_a_" + name]).then_inc(loaded, 16)
                for i, name in enumerate(("bq", "bk", "bv")):
                    sp.dma_start(bqkv[:, i, :], w["L0_attn_a_" + name].partition_broadcast(P)).then_inc(loaded, 16)
                sp.dma_start(bo[:], w["L0_attn_a_bo"].partition_broadcast(P)).then_inc(loaded, 16)
                sp.dma_start(ls[:], w["L0_attn_a_layerscale"].partition_broadcast(P)).then_inc(loaded, 16)
                fold.sync(sp)

            @block.gpsimd
            def _(pool):
                fold.pool(pool)

            @block.tensor
            def _(pe):
                def turn_tokens(b):
                    pe.wait_ge(hn_ready, b + 1)
                    for g in range(2):
                        for j in range(4):
                            last = pe.transpose(ring[g][:, j * P:(j + 1) * P], hn[:, 4 * g + j, :], ident[:])
                        last.then_inc(turned, 1)

                def project(b, j):
                    if j < 2:
                        pe.wait_ge(evac, 6 * b + 2)
                    else:
                        pe.wait_ge(qkv_taken, TPB * b + j - 1)
                    pe.matmul(ring[j % 2][:, 0:3 * D], hT[:, j * P:(j + 1) * P],
                              wT[:, 0:3, :].rearrange("p a e -> p (a e)"), start=True, stop=True).then_inc(qkv_made, 1)

                def turn_qk(b, g):
                    if g == 0:
                        pe.wait_ge(qk_ready, b + 1)
                    if g >= 2:
                        pe.wait_ge(evac, 6 * b + g + 1)
                    for j in range(4):
                        last = pe.transpose(ring[g % 2][:, j * P:(j + 1) * P], qkv[b % 2][:, 4 * (g % 2) + j, g // 2, :], ident[:])
                    last.then_inc(turned, 1)

                def scores(b, u):
                    t, h = u // 2, u % 2
                    if u >= 2:
                        pe.wait_ge(attn_ready, 16 * b + u - 1)
                    pe.matmul(score[u % 2][:], qkT[b % 2][:, 1, t * P:(t + 1) * P], qkT[b % 2][:, 0, h * HALF:(h + 1) * HALF],
                              start=True, stop=True).then_inc(scored, 1)

                def beside(b, u):
                    if u == 0:
                        turn_tokens(b)
                    if 1 <= u <= TPB // 2:
                        project(b, 2 * u - 2)
                        project(b, 2 * u - 1)
                    if u >= 2 * TPB - 2:
                        turn_qk(b, 2 * (u - 2 * TPB + 2))
                        turn_qk(b, 2 * (u - 2 * TPB + 2) + 1)

                pe.wait_ge(loaded, 9 * 16)
                for i in range(4):
                    last = pe.transpose(ring[0][:, i * P:(i + 1) * P], wnat[:, i, :], ident[:])
                last.then_inc(w_turned, 1)
                pe.wait_ge(w_ready, 1)
                for u in range(2 * TPB):
                    beside(0, u)
                for b in range(BATCH):
                    pe.wait_ge(evac, 6 * b + 6)
                    scores(b, 0)
                    for u in range(2 * TPB):
                        if u + 1 < 2 * TPB:
                            scores(b, u + 1)
                        if b + 1 < BATCH:
                            beside(b + 1, u)
                        if u == FOLD_AT:
                            if b:
                                pe.wait_ge(proj_taken, 2 * b)
                            for e in (2 * b, 2 * b + 1):
                                fold.tensor(pe, e, proj[e % 2])
                        t, h = u // 2, u % 2
                        pe.wait_ge(attn_ready, 16 * b + u + 1)
                        pe.matmul(acc[h][:], qkv[b % 2][:, t, 2, :], AT[:, u % 3, :], start=t == 0, stop=t == TPB - 1).then_inc(pv_done, 1)
                    pe.wait_ge(fold.bias_ready, 2 * b + 2)
                    for h in range(2):
                        pe.wait_ge(o_ready, 2 * b + h + 1)
                        for j in range(4):
                            last = pe.matmul(proj[h][:, j * D:(j + 1) * D], oT[:, (4 * h + j) * P:(4 * h + j + 1) * P],
                                             wT[:, 3, :], start=True, stop=True)
                        last.then_inc(proj_done, 1)

            @block.scalar
            def _(act):
                def copy_tokens(b):
                    for g in range(2):
                        act.wait_ge(turned, 6 * b + g + 1)
                        act.activation(hT[:, g * HALF:(g + 1) * HALF], ring[g][:], ACT.Copy).then_inc(evac, 1)

                def copy_qk(b, g):
                    act.wait_ge(turned, 6 * b + 3 + g)
                    act.activation(qkT[b % 2][:, g // 2, (g % 2) * HALF:(g % 2 + 1) * HALF], ring[g % 2][:], ACT.Copy).then_inc(evac, 1)

                def beside(b, u):
                    if u == 0:
                        copy_tokens(b)
                    if u == SQUARE_AT:
                        norm.square(act, qkv[b % 2][:, :, 0:2, :], 2 * TPB, 2 * b + 1, 0)
                    if u == SQUARE_AT + 1 and b + 1 < BATCH:
                        norm.square(act, hn[:], TPB, 2 * b + 2, 1)
                    if u == ROOT_AT:
                        norm.root(act, 2 * TPB, 2 * b + 1, 0)
                        if b + 1 < BATCH:
                            norm.root(act, TPB, 2 * b + 2, 1)
                    if u >= 2 * TPB - 2:
                        copy_qk(b, 2 * (u - 2 * TPB + 2))
                        copy_qk(b, 2 * (u - 2 * TPB + 2) + 1)

                norm.square(act, hn[:], TPB, 0, 1)
                norm.root(act, TPB, 0, 1)
                for u in range(2 * TPB):
                    beside(0, u)
                act.wait_ge(consts, 1)
                for b in range(BATCH):
                    for u in range(2 * TPB):
                        act.wait_ge(scored, 16 * b + u + 1)
                        if u >= 3:
                            act.wait_ge(pv_done, 16 * b + u - 2)
                        act.activation(AT[:, u % 3, :], score[u % 2][:], ACT.Sigmoid, bias=neg_log[:],
                                       scale=1.0 / math.sqrt(D)).then_inc(attn_ready, 1)
                        if b + 1 < BATCH:
                            beside(b + 1, u)
                    for h in range(2):
                        act.wait_ge(pv_done, 16 * b + 15 + h)
                        act.activation(oT[:, h * HALF:(h + 1) * HALF], acc[h][:], ACT.Copy).then_inc(o_ready, 1)

            @block.vector
            def _(dve):
                chain = Chain(dve, shared)

                def tokens(b):
                    return X[:, b * TPB:(b + 1) * TPB, :]

                def add_bias(b):
                    for j in range(TPB):
                        dve.wait_ge(qkv_made, TPB * b + j + 1)
                        dve.tensor_tensor(qkv[b % 2][:, j, :, :].rearrange("p a e -> p (a e)"), ring[j % 2][:, 0:3 * D],
                                          bqkv[:].rearrange("p a e -> p (a e)"), ALU.add).then_inc(qkv_taken, 1)
                    dve.wait_ge(qkv_taken, TPB * (b + 1))

                def norms(b):
                    qk, more = qkv[b % 2][:, :, 0:2, :], b + 1 < BATCH
                    norm.centre(dve, chain, qk, qk, 2 * TPB, 2 * b + 1, 0)
                    if more:
                        norm.centre(dve, chain, tokens(b + 1), hn[:], TPB, 2 * b + 2, 1)
                    norm.variance(dve, chain, 2 * TPB, 2 * b + 1, 0)
                    if more:
                        norm.variance(dve, chain, TPB, 2 * b + 2, 1)
                    norm.scale(dve, chain, qk, 2 * TPB, 2 * b + 1, 0).then_inc(qk_ready, 1)
                    if more:
                        norm.scale(dve, chain, hn[:], TPB, 2 * b + 2, 1).then_inc(hn_ready, 1)

                def update(b):
                    for h in range(2):
                        dve.wait_ge(proj_done, 2 * b + h + 1)
                        wide = lambda t: t[:].unsqueeze(1).to_broadcast([P, 4, D])
                        Xh = X[:, b * TPB + 4 * h:b * TPB + 4 * h + 4, :]
                        chain.link(dve.tensor_tensor(upd[:, h], proj[h][:].rearrange("p (j e) -> p j e", e=D), wide(bo), ALU.add))
                        chain.link(dve.tensor_tensor(upd[:, h], upd[:, h], wide(ls), ALU.mult))
                        dve.tensor_tensor(Xh, Xh, upd[:, h], ALU.add).then_inc(proj_taken, 1)

                dve.memset(neg_log[:], -math.log(float(SEQ))).then_inc(consts, 1)
                norm.centre(dve, chain, tokens(0), hn[:], TPB, 0, 1)
                norm.variance(dve, chain, TPB, 0, 1)
                norm.scale(dve, chain, hn[:], TPB, 0, 1).then_inc(hn_ready, 1)
                dve.wait_ge(loaded, 9 * 16)
                dve.wait_ge(w_turned, 1)
                dve.tensor_copy(wT[:].rearrange("p a e -> p (a e)"), ring[0][:]).then_inc(w_ready, 1)
                add_bias(0)
                norms(0)
                for b in range(BATCH):
                    if b:
                        update(b - 1)
                    if b + 1 < BATCH:
                        add_bias(b + 1)
                        norms(b + 1)
                    for e in (2 * b, 2 * b + 1):
                        fold.vector(dve, chain, e, proj[e % 2])
                update(BATCH - 1)
                chain.close()




EXPERTS = 8
HIDDEN = 512
HC = HIDDEN // P
ROWS = 512
BLOCKS = 2 * BATCH * SEQ // ROWS + EXPERTS
CLAMP = 10000.0


class ExpertWeights:

    def __init__(self, nc):
        dram = lambda name, shape: nc.dram_tensor(name, shape, F32, kind="Internal").ap()
        self.w12 = dram("f_w12", [EXPERTS * P, 2 * HIDDEN])
        self.bias = dram("f_bias", [EXPERTS * P, 4 * HC])


class Fold:
    LINKS = 1

    def __init__(self, sb, sem, w, folded):
        self.w, self.folded = w, folded
        self.eg, self.eb = sb("eg", [P, EXPERTS]), sb("eb", [P, EXPERTS])
        self.b12 = sb("b12", [P, EXPERTS, 2 * HC])
        self.wbuf = [sb(f"wbuf{i}", [P, 2, HIDDEN]) for i in range(2)]
        self.wg = [sb(f"wg{i}", [P, 2, HIDDEN]) for i in range(2)]
        self.bout = [sb(f"bout{i}", [P, 4, HC]) for i in range(2)]
        self.vec_loaded, self.made, self.scaled, self.bias_ready = (sem("fold_" + n) for n in ("vec_loaded", "made", "scaled", "bias_ready"))
        self.loaded, self.stored = ([sem(f"fold_{n}{i}") for i in range(2)] for n in ("loaded", "stored"))
        self.VECTORS = 16 * (2 + 2 * EXPERTS)

    def sync(self, sp):
        def load(e):
            for a, name in enumerate(("W1", "W2")):
                sp.dma_start(self.wbuf[e % 2][:, a, :], self.w["L0_ffn_" + name][e, :, :]).then_inc(self.loaded[e % 2], 16)

        sp.dma_start(self.eg[:], self.w["L0_ffn_eg"].rearrange("e d -> d e")).then_inc(self.vec_loaded, 16)
        sp.dma_start(self.eb[:], self.w["L0_ffn_eb"].rearrange("e d -> d e")).then_inc(self.vec_loaded, 16)
        for a, name in enumerate(("b1", "b2")):
            for e in range(EXPERTS):
                sp.dma_start(self.b12[:, e, a * HC:(a + 1) * HC], self.w["L0_ffn_" + name][e, :].rearrange("(c p) -> p c", p=P))\
                  .then_inc(self.vec_loaded, 16)
        load(0)
        load(1)
        for e in range(EXPERTS):
            sp.wait_ge(self.scaled, e + 1)
            sp.dma_start(self.folded.w12[e * P:(e + 1) * P, :], self.wg[e % 2][:].rearrange("p a h -> p (a h)")).then_inc(self.stored[e % 2], 16)
            sp.wait_ge(self.bias_ready, e + 1)
            sp.dma_start(self.folded.bias[e * P:(e + 1) * P, :], self.bout[e % 2][:].rearrange("p a c -> p (a c)")).then_inc(self.stored[e % 2], 16)
            if e + 2 < EXPERTS:
                load(e + 2)
        for i in range(2):
            sp.wait_ge(self.stored[i], 16 * EXPERTS)

    def pool(self, pool):
        pool.wait_ge(self.vec_loaded, self.VECTORS)
        for e in range(EXPERTS):
            pool.wait_ge(self.loaded[e % 2], 32 * (e // 2 + 1))
            if e >= 2:
                pool.wait_ge(self.stored[e % 2], 32 * (e // 2))
            pool.tensor_tensor(self.wg[e % 2][:], self.wbuf[e % 2][:],
                               self.eg[:, e:e + 1].unsqueeze(2).to_broadcast([P, 2, HIDDEN]), ALU.mult).then_inc(self.scaled, 1)

    def tensor(self, pe, e, bank):
        if e == 0:
            pe.wait_ge(self.vec_loaded, self.VECTORS)
        pe.wait_ge(self.loaded[e % 2], 32 * (e // 2 + 1))
        for a in range(2):
            for c in range(HC):
                last = pe.matmul(bank[:, a * HC + c:a * HC + c + 1], self.wbuf[e % 2][:, a, c * P:(c + 1) * P],
                                 self.eb[:, e:e + 1], start=True, stop=True)
        last.then_inc(self.made, 1)

    def vector(self, dve, chain, e, bank):
        bout = self.bout[e % 2]
        if e == 0:
            dve.wait_ge(self.vec_loaded, self.VECTORS)
        if e >= 2:
            dve.wait_ge(self.stored[e % 2], 32 * (e // 2))
        dve.wait_ge(self.made, e + 1)
        chain.link(dve.tensor_tensor(bout[:, 0:2, :].rearrange("p a c -> p (a c)"), bank[:, 0:2 * HC], self.b12[:, e, :], ALU.add))
        dve.tensor_scalar(bout[:, 2, :], bout[:, 1, :], -1.0, -20.0, ALU.mult, ALU.add)
        dve.tensor_scalar(bout[:, 3, :], bout[:, 1, :], -1.0, 20.0, ALU.mult, ALU.add).then_inc(self.bias_ready, 1)


def gated_experts(nc, X, ident, w, folded, shared, tag):
    dram = lambda name, shape: nc.dram_tensor(tag + name, shape, F32, kind="Internal").ap()
    z_sorted = dram("z_sorted", [BLOCKS * ROWS, D])
    y_sorted = dram("y_sorted", [BLOCKS * ROWS, D])
    with ExitStack() as ctx:
        sb = lambda name, shape, dt=F32: ctx.enter_context(nc.sbuf_tensor(tag + name, shape, dt))
        slots = sb("slots", [P, 2, TILES], mybir.dt.uint32)
        gates = sb("gates", [P, 2, TILES])
        expert_of = sb("expert_of", [P, BLOCKS], mybir.dt.int32)
        with ExitStack() as inner:
            zall = inner.enter_context(nc.sbuf_tensor(tag + "zall", [P, TILES, D], F32))
            logits = inner.enter_context(nc.sbuf_tensor(tag + "logits", [P, TILES, EXPERTS], F32))
            route_inputs(nc, X, ident, w, zall, logits, z_sorted, shared, tag + "r_")
            sort_rows(nc, zall, logits, slots, gates, expert_of, z_sorted, shared, tag + "s_")
        run_experts(nc, ident, w, folded, expert_of, z_sorted, y_sorted, shared, tag + "e_")
        combine(nc, X, slots, gates, y_sorted, tag + "c_")


def route_inputs(nc, X, ident, w, zall, logits, z_sorted, shared, tag):
    with ExitStack() as ctx:
        sb = lambda name, shape, dt=F32: ctx.enter_context(nc.sbuf_tensor(tag + name, shape, dt))
        bank = lambda name: ctx.enter_context(nc.psum_tensor(tag + name, [P, HALF], F32))
        sem = lambda name: ctx.enter_context(nc.semaphore(tag + name))
        norm = Norm(sb, shared, TPB, 2 * BATCH, ways=2)
        gain, shift = sb("gain", [P, D]), sb("shift", [P, D])
        rw = sb("rw", [P, EXPERTS])
        zero = sb("zero", [P, 2, HALF])
        xn = [sb(f"xn{i}", [P, TPB, D]) for i in range(2)]
        xfT = [sb(f"xfT{i}", [P, SEQ]) for i in range(2)]
        turn = [bank(f"turn{i}") for i in range(4)]
        lg = [bank(f"lg{i}") for i in range(2)]
        loaded, zeroed, cleared, normed, gained, xf_ready, turned, evac, routed = (
            sem(n) for n in ("loaded", "zeroed", "cleared", "normed", "gained", "xf_ready", "turned", "evac", "routed"))

        with nc.Block() as block:

            @block.sync
            def _(sp):
                sp.dma_start(gain[:], w["L0_ffn_ln_g"].partition_broadcast(P)).then_inc(loaded, 16)
                sp.dma_start(shift[:], w["L0_ffn_ln_b"].partition_broadcast(P)).then_inc(loaded, 16)
                sp.dma_start(rw[:], w["L0_ffn_router_w"]).then_inc(loaded, 16)
                sp.wait_ge(zeroed, 1)
                rows = z_sorted.rearrange("(n p k) d -> n p (k d)", p=P, k=8)
                for n in range(BLOCKS * ROWS // (8 * P)):
                    sp.dma_start(rows[n], zero[:].rearrange("p a k -> p (a k)")).then_inc(cleared, 16)
                sp.wait_ge(cleared, 16 * (BLOCKS * ROWS // (8 * P)))

            @block.gpsimd
            def _(pool):
                pool.memset(zero[:], 0.0).then_inc(zeroed, 1)
                pool.wait_ge(loaded, 48)
                wide = lambda t: t[:].unsqueeze(1).to_broadcast([P, TPB, D])
                for b in range(BATCH):
                    pool.wait_ge(normed, b + 1)
                    pool.tensor_tensor(xn[b % 2][:], xn[b % 2][:], wide(gain), ALU.mult).then_inc(gained, 1)
                    pool.wait_ge(gained, b + 1)
                    pool.tensor_tensor(xn[b % 2][:], xn[b % 2][:], wide(shift), ALU.add).then_inc(xf_ready, 1)

            @block.tensor
            def _(pe):
                pe.wait_ge(loaded, 48)
                for b in range(BATCH):
                    way = b % 2
                    pe.wait_ge(xf_ready, b + 1)
                    for g in range(2):
                        for t in range(4):
                            last = pe.transpose(turn[2 * way + g][:, t * P:(t + 1) * P], xn[way][:, 4 * g + t, :], ident[:])
                        last.then_inc(turned, 1)
                    pe.wait_ge(evac, 2 * b + 2)
                    for t in range(TPB):
                        last = pe.matmul(lg[way][:, t * EXPERTS:(t + 1) * EXPERTS], xfT[way][:, t * P:(t + 1) * P], rw[:], start=True, stop=True)
                    last.then_inc(routed, 1)

            @block.scalar
            def _(act):
                for j in range(BATCH // 2):
                    for way in range(2):
                        norm.square(act, xn[way][:], TPB, 4 * j + way, way)
                    for way in range(2):
                        norm.root(act, TPB, 4 * j + way, way)
                    for way in range(2):
                        b = 2 * j + way
                        for g in range(2):
                            act.wait_ge(turned, 2 * b + g + 1)
                            act.activation(xfT[way][:, g * HALF:(g + 1) * HALF], turn[2 * way + g][:], ACT.Copy).then_inc(evac, 1)
                        norm.square(act, zall[:, b * TPB:(b + 1) * TPB, :], TPB, 4 * j + 2 + way, way)
                    for way in range(2):
                        norm.root(act, TPB, 4 * j + 2 + way, way)

            @block.vector
            def _(dve):
                chain = Chain(dve, shared)
                for j in range(BATCH // 2):
                    tiles = [slice((2 * j + way) * TPB, (2 * j + way + 1) * TPB) for way in range(2)]
                    for way in range(2):
                        if j:
                            dve.wait_ge(routed, 2 * j - 1 + way)
                        norm.centre(dve, chain, X[:, tiles[way], :], xn[way][:], TPB, 4 * j + way, way)
                    for way in range(2):
                        norm.variance(dve, chain, TPB, 4 * j + way, way, gain=1.0 + EPS, add=EPS * EPS)
                    for way in range(2):
                        norm.scale(dve, chain, xn[way][:], TPB, 4 * j + way, way).then_inc(normed, 1)
                    for way in range(2):
                        dve.wait_ge(xf_ready, 2 * j + way + 1)
                        norm.centre(dve, chain, xn[way][:], zall[:, tiles[way], :], TPB, 4 * j + 2 + way, way)
                    for way in range(2):
                        norm.variance(dve, chain, TPB, 4 * j + 2 + way, way)
                    for way in range(2):
                        norm.scale(dve, chain, zall[:, tiles[way], :], TPB, 4 * j + 2 + way, way)
                    for way in range(2):
                        dve.wait_ge(routed, 2 * j + way + 1)
                        chain.link(dve.tensor_copy(logits[:, tiles[way], :], lg[way][:, 0:TPB * EXPERTS].rearrange("p (j e) -> p j e", e=EXPERTS)))
                chain.close()


def sort_rows(nc, zall, logits, slots, gates, expert_of, z_sorted, shared, tag):
    E8 = EXPERTS
    with ExitStack() as ctx:
        sb = lambda name, shape, dt=F32: ctx.enter_context(nc.sbuf_tensor(tag + name, shape, dt))
        sem = lambda name: ctx.enter_context(nc.semaphore(tag + name))
        tri = sb("tri", [P, E8, E8])
        before = sb("before", [P, P])
        ones = sb("ones", [P, P])
        counts_to = sb("counts_to", [P, E8, TPB])
        block_no = sb("block_no", [P, BLOCKS, E8])
        first_zero = sb("first_zero", [P, E8, TILES])
        cmp = sb("cmp", [P, TILES, E8, E8])
        cmp2 = sb("cmp2", [P, TILES, E8, E8])
        rank = sb("rank", [P, TILES, E8])
        picked = sb("picked", [P, 3, TILES, E8])
        work = sb("work", [P, TILES, E8])
        top = sb("top", [P, 4, TILES])
        per_tile = sb("per_tile", [P, E8, TILES])
        prefix = sb("prefix", [P, E8, TILES])
        pos = sb("pos", [P, TILES, E8])
        blocks_of = sb("blocks_of", [P, E8])
        block_end = sb("block_end", [P, E8])
        start = sb("start", [P, E8])
        cmp3 = sb("cmp3", [P, E8, TPB])
        cmp4 = sb("cmp4", [P, BLOCKS, E8])
        owner = sb("owner", [P, BLOCKS])
        slot_f = sb("slot_f", [P, 2, TILES])
        within = ctx.enter_context(nc.psum_tensor(tag + "within", [P, HALF], F32))
        totals = ctx.enter_context(nc.psum_tensor(tag + "totals", [P, HALF], F32))
        consts, picked_ready, counted, gap_ready, exp_ready, slots_ready, moved = (
            sem(n) for n in ("consts", "picked_ready", "counted", "gap_ready", "exp_ready", "slots_ready", "moved"))
        n_consts = 7

        with nc.Block() as block:

            @block.gpsimd
            def _(pool):
                pool.memset(tri[:], 1.0).then_inc(consts, 1)
                pool.memset(before[:], 1.0).then_inc(consts, 1)
                pool.memset(ones[:], 1.0).then_inc(consts, 1)
                pool.wait_ge(consts, 3)
                pool.affine_select(out=tri[:], in_=tri[:], compare_op=ALU.is_gt, fill=0.0, base=0,
                                   pattern=[[1, E8], [-1, E8]], channel_multiplier=0).then_inc(consts, 1)
                pool.affine_select(out=before[:], in_=before[:], compare_op=ALU.is_gt, fill=0.0, base=0,
                                   pattern=[[1, P]], channel_multiplier=-1).then_inc(consts, 1)
                pool.iota(counts_to[:], pattern=[[0, E8], [ROWS, TPB]], base=0, channel_multiplier=0,
                          allow_small_or_imprecise_dtypes=True).then_inc(consts, 1)
                pool.iota(block_no[:], pattern=[[1, BLOCKS], [0, E8]], base=0, channel_multiplier=0,
                          allow_small_or_imprecise_dtypes=True).then_inc(consts, 1)
                pool.wait_ge(slots_ready, 1)
                for n in range(TILES):
                    for k in range(2):
                        pool.indirect_dma_start(out=z_sorted, out_offset=bass.IndirectOffsetOnAxis(ap=slots[:, k, n:n + 1], axis=0),
                                                in_=zall[:, n, :], in_offset=None).then_inc(moved, 16)
                pool.wait_ge(moved, 32 * TILES)

            @block.tensor
            def _(pe):
                pe.wait_ge(consts, n_consts)
                pe.wait_ge(picked_ready, 1)
                flat = picked[:, 2, :, :].rearrange("p n e -> p (n e)")
                pe.matmul(within[:, 0:TILES * E8], before[:], flat, start=True, stop=True)
                pe.matmul(totals[:, 0:TILES * E8], ones[:], flat, start=True, stop=True).then_inc(counted, 1)

            @block.scalar
            def _(act):
                act.wait_ge(gap_ready, 1)
                act.activation(top[:, 3, :], top[:, 2, :], ACT.Exp).then_inc(exp_ready, 1)

            @block.vector
            def _(dve):
                chain = Chain(dve, shared)
                link, tt, ts = chain.link, dve.tensor_tensor, dve.tensor_scalar
                full = [P, TILES, E8, E8]
                other, own = logits[:].unsqueeze(2).to_broadcast(full), logits[:].unsqueeze(3).to_broadcast(full)
                dve.wait_ge(consts, n_consts)
                tt(cmp[:], other, own, ALU.is_gt)
                link(tt(cmp2[:], other, own, ALU.is_equal))
                link(tt(cmp2[:], cmp2[:], tri[:].unsqueeze(1).to_broadcast(full), ALU.mult))
                link(tt(cmp[:], cmp[:], cmp2[:], ALU.add))
                link(dve.tensor_reduce(rank[:], cmp[:], AX, ALU.add))
                link(ts(picked[:, 0], rank[:], 0.0, None, ALU.is_equal))
                link(ts(picked[:, 1], rank[:], 1.0, None, ALU.is_equal))
                tt(picked[:, 2], picked[:, 0], picked[:, 1], ALU.add).then_inc(picked_ready, 1)
                link(tt(work[:], logits[:], picked[:, 1], ALU.mult))
                link(dve.tensor_reduce(top[:, 1, :], work[:], AX, ALU.add))
                link(dve.tensor_reduce(top[:, 0, :], logits[:], AX, ALU.max))
                tt(top[:, 2, :], top[:, 1, :], top[:, 0, :], ALU.subtract).then_inc(gap_ready, 1)
                dve.wait_ge(exp_ready, 1)
                link(ts(top[:, 0, :], top[:, 3, :], 1.0, None, ALU.add))
                link(dve.reciprocal(gates[:, 0, :], top[:, 0, :]))
                link(tt(gates[:, 1, :], gates[:, 0, :], top[:, 3, :], ALU.mult))
                link(dve.memset(first_zero[:], 1.0))
                link(dve.memset(first_zero[:, :, 0:1], 0.0))
                dve.wait_ge(counted, 1)
                link(dve.tensor_copy(per_tile[:], totals[:, 0:TILES * E8].rearrange("p (n e) -> p e n", e=E8)))
                flat = lambda t: t[:].rearrange("p e n -> p (e n)")
                link(dve.tensor_tensor_scan(flat(prefix), flat(first_zero), flat(per_tile), 0.0, ALU.mult, ALU.add))
                link(tt(cmp3[:], prefix[:, :, TILES - 1:TILES].to_broadcast([P, E8, TPB]), counts_to[:], ALU.is_gt))
                link(dve.tensor_reduce(blocks_of[:], cmp3[:], AX, ALU.add))
                link(dve.memset(start[:], 1.0))
                link(dve.tensor_tensor_scan(block_end[:], start[:], blocks_of[:], 0.0, ALU.mult, ALU.add))
                link(tt(start[:], block_end[:], blocks_of[:], ALU.subtract))
                link(ts(start[:], start[:], float(ROWS), None, ALU.mult))
                link(tt(cmp4[:], block_end[:].unsqueeze(1).to_broadcast([P, BLOCKS, E8]), block_no[:], ALU.is_le))
                link(dve.tensor_reduce(owner[:], cmp4[:], AX, ALU.add))
                link(ts(expert_of[:], owner[:], float(E8 - 1), None, ALU.min))
                link(tt(prefix[:], prefix[:], per_tile[:], ALU.subtract))
                link(tt(prefix[:], prefix[:], start[:].unsqueeze(2).to_broadcast([P, E8, TILES]), ALU.add))
                link(tt(pos[:], within[:, 0:TILES * E8].rearrange("p (n e) -> p n e", e=E8),
                        prefix[:].rearrange("p e n -> p n e"), ALU.add))
                for k in range(2):
                    link(tt(work[:], pos[:], picked[:, k], ALU.mult))
                    link(dve.tensor_reduce(slot_f[:, k, :], work[:], AX, ALU.add))
                dve.tensor_copy(slots[:], slot_f[:]).then_inc(slots_ready, 1)
                chain.close()


def run_experts(nc, ident, w, folded, expert_of, z_sorted, y_sorted, shared, tag):
    QB = ROWS // P
    with ExitStack() as ctx:
        sb = lambda name, shape, dt=F32: ctx.enter_context(nc.sbuf_tensor(tag + name, shape, dt))
        bank = lambda name: ctx.enter_context(nc.psum_tensor(tag + name, [P, HALF], F32))
        sem = lambda name: ctx.enter_context(nc.semaphore(tag + name))
        both = lambda name, shape: [sb(f"{name}{i}", shape) for i in range(2)]
        w12 = both("w12", [P, 2, HIDDEN])
        wo = both("wo", [P, HC, D])
        bias = both("bias", [P, 4, HC])
        bo = both("bo", [P, D])
        z = both("z", [P, QB, D])
        zT = both("zT", [P, ROWS])
        x2 = both("x2", [P, ROWS])
        act2 = both("act2", [P, ROWS])
        hid = both("hid", [P, ROWS])
        hT = both("hT", [P, HC, ROWS])
        y = both("y", [P, QB, D])
        turn = bank("turn")
        p1 = [bank(f"p1{i}") for i in range(2)]
        p2 = [bank(f"p2{i}") for i in range(2)]
        py = [bank(f"py{i}") for i in range(2)]
        turned, zT_ready, x2_done, up_done, x2_ready, act_ready, x1_taken, hT_ready, down_done, y_ready = (
            sem(n) for n in ("turned", "zT_ready", "x2_done", "up_done", "x2_ready", "act_ready", "x1_taken", "hT_ready", "down_done", "y_ready"))
        up_loaded, down_loaded, z_loaded, stored = ([sem(f"{n}{i}") for i in range(2)]
                                                    for n in ("up_loaded", "down_loaded", "z_loaded", "stored"))

        def loop(eng, step):
            for t in range(4):
                step(t // 2, t, t % 2)
            with eng.Fori(2, BLOCKS // 2) as j:
                for par in range(2):
                    step(j, 2 * j + par, par)

        z_view = z_sorted.rearrange("(t q p) d -> t p q d", q=QB, p=P)
        y_view = y_sorted.rearrange("(t q p) d -> t p q d", q=QB, p=P)

        with nc.Block() as block:

            @block.sync
            def _(sp):
                def load_rows(t, par):
                    sp.dma_start(z[par][:], z_view[bass.ds(t, 1), :, :, :].rearrange("a p q d -> (a p) q d")).then_inc(z_loaded[par], 16)

                def step(j, t, par):
                    e = sp.value_load(expert_of[0:1, bass.ds(t, 1)], min_val=0, max_val=EXPERTS - 1)
                    row, after = e * P, (t + 1) % BLOCKS
                    first = isinstance(t, int) and t < 2
                    if not (isinstance(t, int) and t == 0):
                        sp.wait_ge(turned, t)
                    load_rows(after, 1 - par)
                    if not first:
                        sp.wait_ge(x1_taken, HC * (t - 1))
                    sp.dma_start(w12[par][:].rearrange("p a h -> p (a h)"), folded.w12[bass.ds(row, P), :]).then_inc(up_loaded[par], 16)
                    sp.dma_start(bias[par][:].rearrange("p a c -> p (a c)"), folded.bias[bass.ds(row, P), :]).then_inc(up_loaded[par], 16)
                    if not first:
                        sp.wait_ge(y_ready, t - 1)
                    sp.dma_start(wo[par][:], w["L0_ffn_Wo"][bass.ds(e, 1), :, :].rearrange("a (c p) d -> (a p) c d", p=P)).then_inc(down_loaded[par], 16)
                    sp.dma_start(bo[par][:], w["L0_ffn_bo"][bass.ds(e, 1), :].rearrange("a d -> (a d)").partition_broadcast(P)).then_inc(down_loaded[par], 16)

                load_rows(0, 0)
                loop(sp, step)
                sp.wait_ge(z_loaded[0], 16 * (BLOCKS // 2 + 1))

            @block.tensor
            def _(pe):
                def up(t, par, c):
                    n = HC * t + c
                    if not (isinstance(n, int) and n < 2):
                        pe.wait_ge(x1_taken, n - 1)
                    pe.matmul(p2[c % 2][:], w12[par][:, 1, c * P:(c + 1) * P], zT[par][:], start=True, stop=True).then_inc(x2_done, 1)
                    pe.matmul(p1[c % 2][:], w12[par][:, 0, c * P:(c + 1) * P], zT[par][:], start=True, stop=True).then_inc(up_done, 1)

                def down(j, t, par, q):
                    if q == 0:
                        pe.wait_ge(down_loaded[par], 32 * (j + 1))
                        pe.wait_ge(hT_ready, HC * (t + 1))
                        if not (isinstance(t, int) and t < 2):
                            pe.wait_ge(y_ready, t - 1)
                    for c in range(HC):
                        last = pe.matmul(py[par][:, q * D:(q + 1) * D], hT[par][:, c, q * P:(q + 1) * P], wo[par][:, c, :],
                                         start=c == 0, stop=c == HC - 1)
                    if q == QB - 1:
                        last.then_inc(down_done, 1)

                def turn_rows(j, t, par):
                    pe.wait_ge(z_loaded[par], 16 * (j + 1))
                    for q in range(QB):
                        last = pe.transpose(turn[:, q * P:(q + 1) * P], z[par][:, q, :], ident[:])
                    last.then_inc(turned, 1)

                def step(j, t, par):
                    pe.wait_ge(up_loaded[par], 32 * (j + 1))
                    pe.wait_ge(zT_ready, t + 1)
                    for c in range(HC):
                        up(t, par, c)
                        if not (isinstance(t, int) and t == 0):
                            down(j - (1 - par), t - 1, 1 - par, c)
                        if c == 2:
                            turn_rows(j + par, t + 1, 1 - par)

                turn_rows(0, 0, 0)
                loop(pe, step)
                for q in range(QB):
                    down(BLOCKS // 2 - 1, BLOCKS - 1, 1, q)

            @block.scalar
            def _(act):
                def store(t, par):
                    act.wait_ge(y_ready, t + 1)
                    act.dma_start(y_view[bass.ds(t, 1), :, :, :].rearrange("a p q d -> (a p) q d"), y[par][:]).then_inc(stored[par], 16)

                def tokens(t, par):
                    act.wait_ge(turned, t + 1)
                    act.activation(zT[par][:], turn[:], ACT.Copy).then_inc(zT_ready, 1)

                def step(j, t, par):
                    for c in range(HC):
                        act.wait_ge(x2_ready, HC * t + c + 1)
                        act.activation(act2[c % 2][:], x2[c % 2][:], ACT.Silu, bias=bias[par][:, 1, c:c + 1]).then_inc(act_ready, 1)
                        if c == 1 and not (isinstance(t, int) and t < 2):
                            store(t - 2, par)
                        if c == 2:
                            tokens(t + 1, 1 - par)

                tokens(0, 0)
                loop(act, step)
                for par in range(2):
                    store(BLOCKS - 2 + par, par)
                for par in range(2):
                    act.wait_ge(stored[par], 16 * (BLOCKS // 2))

            @block.vector
            def _(dve):
                chain = Chain(dve, shared)

                def finish(j, t, par):
                    dve.wait_ge(down_done, t + 1)
                    if not isinstance(t, int) or t >= 2:
                        dve.wait_ge(stored[par], 16 * j)
                    chain.link(dve.tensor_tensor(y[par][:], py[par][:].rearrange("p (q d) -> p q d", d=D),
                                                 bo[par][:].unsqueeze(1).to_broadcast([P, QB, D]), ALU.add))
                    dve.tensor_scalar(y[par][:], y[par][:], CLAMP, -CLAMP, ALU.min, ALU.max).then_inc(y_ready, 1)

                def step(j, t, par):
                    dve.wait_ge(up_loaded[par], 32 * (j + 1))
                    for c in range(HC):
                        dve.wait_ge(x2_done, HC * t + c + 1)
                        dve.tensor_scalar(x2[c % 2][:], p2[c % 2][:], bias[par][:, 2, c:c + 1], bias[par][:, 3, c:c + 1],
                                          ALU.max, ALU.min).then_inc(x2_ready, 1)
                        product(t, par, c)
                        if c == 0 and not (isinstance(t, int) and t < 2):
                            finish(j - 1, t - 2, par)

                def product(t, par, c):
                    dve.wait_ge(act_ready, HC * t + c + 1)
                    dve.wait_ge(up_done, HC * t + c + 1)
                    dve.scalar_tensor_tensor(hid[c % 2][:], p1[c % 2][:], bias[par][:, 0, c:c + 1], act2[c % 2][:],
                                             ALU.add, ALU.mult).then_inc(x1_taken, 1)
                    dve.wait_ge(x1_taken, HC * t + c + 1)
                    if not (isinstance(t, int) and t < 2) and c == 0:
                        dve.wait_ge(down_done, t - 1)
                    dve.tensor_scalar(hT[par][:, c, :], hid[c % 2][:], CLAMP, -CLAMP, ALU.min, ALU.max).then_inc(hT_ready, 1)

                for t in range(4):
                    step(t // 2, t, t % 2)
                with dve.Fori(2, BLOCKS // 2) as j:
                    chain.enter_from(j, 2, 2)
                    for par in range(2):
                        step(j, 2 * j + par, par)
                chain.leave(BLOCKS // 2 - 2)
                for par in range(2):
                    finish(BLOCKS // 2 - 1, BLOCKS - 2 + par, par)
                chain.close()


def combine(nc, X, slots, gates, y_sorted, tag):
    with ExitStack() as ctx:
        sem = lambda name: ctx.enter_context(nc.semaphore(tag + name))
        DEPTH = 4
        rows = [ctx.enter_context(nc.sbuf_tensor(f"{tag}rows{i}", [P, D], F32)) for i in range(DEPTH)]
        fetched = [sem(f"fetched{i}") for i in range(DEPTH)]
        added = sem("added")
        per = DEPTH // 2

        with nc.Block() as block:

            @block.gpsimd
            def _(pool):
                for m in range(TILES // per):
                    for i in range(DEPTH):
                        k, n = i % 2, m * per + i // 2
                        if m > 0:
                            pool.wait_ge(fetched[i], 16 * m)
                            pool.wait_ge(added, DEPTH * (m - 1) + i + 1)
                        pool.indirect_dma_start(out=rows[i][:], out_offset=None, in_=y_sorted,
                                                in_offset=bass.IndirectOffsetOnAxis(ap=slots[:, k, n:n + 1], axis=0))\
                            .then_inc(fetched[i], 16)

            @block.vector
            def _(dve):
                with dve.Fori(0, TILES // per) as m:
                    for i in range(DEPTH):
                        k, n = i % 2, m * per + i // 2
                        Xn = X[:, bass.ds(n, 1), :].rearrange("p a d -> p (a d)")
                        dve.wait_ge(fetched[i], 16 * (m + 1))
                        if k:
                            dve.wait_ge(added, DEPTH * m + i)
                        dve.scalar_tensor_tensor(Xn, rows[i][:], gates[:, k, bass.ds(n, 1)], Xn, ALU.mult, ALU.add).then_inc(added, 1)


HEADS = 16
HD = 64
KV_BLOCK = 64
NB = SEQ // KV_BLOCK
PAIRS = BATCH * HEADS // 2
QT = 2
GT = 2 * QT
GPP = TPB // QT
LAG = 3
BIG = 3.0e38


def head_inputs(nc, X, ident, hT_dram, shared, tag):
    with ExitStack() as ctx:
        sb = lambda name, shape, dt=F32: ctx.enter_context(nc.sbuf_tensor(tag + name, shape, dt))
        sem = lambda name: ctx.enter_context(nc.semaphore(tag + name))
        norm = Norm(sb, shared, TPB, BATCH, ways=2)
        hn = [sb(f"hn{i}", [P, TPB, D]) for i in range(2)]
        hT = [sb(f"hT{i}", [P, SEQ]) for i in range(2)]
        ring = [ctx.enter_context(nc.psum_tensor(f"{tag}ring{i}", [P, HALF], F32)) for i in range(4)]
        hn_ready, turned, evac, stored0, stored1 = (sem(n) for n in ("hn_ready", "turned", "evac", "stored0", "stored1"))
        stored = (stored0, stored1)

        with nc.Block() as block:

            @block.tensor
            def _(pe):
                with pe.Fori(0, BATCH // 2) as j:
                    for way in range(2):
                        pe.wait_ge(hn_ready, 2 * j + way + 1)
                        for g in range(2):
                            for t in range(4):
                                last = pe.transpose(ring[2 * way + g][:, t * P:(t + 1) * P], hn[way][:, 4 * g + t, :], ident[:])
                            last.then_inc(turned, 1)

            @block.scalar
            def _(act):
                with act.Fori(0, BATCH // 2) as j:
                    for way in range(2):
                        norm.square(act, hn[way][:], TPB, 2 * j + way, way)
                    for way in range(2):
                        norm.root(act, TPB, 2 * j + way, way)
                    for way in range(2):
                        for g in range(2):
                            act.wait_ge(turned, 4 * j + 2 * way + g + 1)
                            act.activation(hT[way][:, g * HALF:(g + 1) * HALF], ring[2 * way + g][:], ACT.Copy).then_inc(evac, 1)

            @block.vector
            def _(dve):
                chain = Chain(dve, shared)

                def two(j, first):
                    for way in range(2):
                        if not first:
                            dve.wait_ge(evac, 4 * j - 2 + 2 * way)
                            dve.wait_ge(stored[way], 16 * j)
                        norm.centre(dve, chain, X[:, bass.ds((2 * j + way) * TPB, TPB), :], hn[way][:], TPB, 2 * j + way, way)
                    for way in range(2):
                        norm.variance(dve, chain, TPB, 2 * j + way, way)
                    for way in range(2):
                        norm.scale(dve, chain, hn[way][:], TPB, 2 * j + way, way).then_inc(hn_ready, 1)

                for j in range(BATCH // 2):
                    two(j, j == 0)
                chain.close()

            @block.sync
            def _(sp):
                for i in range(BATCH):
                    sp.wait_ge(evac, 2 * (i + 1))
                    sp.dma_start(hT_dram[:, i * SEQ:(i + 1) * SEQ], hT[i % 2][:]).then_inc(stored[i % 2], 16)
                for way in range(2):
                    sp.wait_ge(stored[way], 16 * (BATCH // 2))


def block_softmax_attention(nc, X, ident, w, shared):
    hT_dram = nc.dram_tensor("b_hT", [D, BATCH * SEQ], F32, kind="Internal").ap()
    head_inputs(nc, X, ident, hT_dram, shared, "bh_")
    with ExitStack() as ctx:
        sb = lambda name, shape, dt=F32: ctx.enter_context(nc.sbuf_tensor("b_" + name, shape, dt))
        psum = lambda name, cols: ctx.enter_context(nc.psum_tensor("b_" + name, [P, cols], F32))
        sem = lambda name: ctx.enter_context(nc.semaphore("b_" + name))

        hb = [sb(f"hb{i}", [P, SEQ]) for i in range(2)]
        wqkv = [sb(f"wqkv{i}", [P, 3, P]) for i in range(2)]
        QS = [[sb(f"QS{i}{h}", [P, SEQ], F32R) for h in range(2)] for i in range(2)]
        KH = [[sb(f"KH{i}{h}", [P, SEQ], F32R) for h in range(2)] for i in range(2)]
        KL = [[sb(f"KL{i}{h}", [P, SEQ], F32R) for h in range(2)] for i in range(2)]
        V = [sb(f"V{i}", [P, TPB, P]) for i in range(2)]
        parts = {"q": (sb("q_high", [P, SEQ], F32R), sb("q_low", [P, SEQ], F32R)),
                 "k": (sb("k_high", [P, SEQ], F32R), sb("k_low", [P, SEQ], F32R))}
        wo = sb("wo", [P, HEADS // 2, D])
        prob = [[sb(f"prob{i}{t}", [P, SEQ]) for t in range(GT)] for i in range(4)]
        bmax = [sb(f"bmax{i}", [P, GT, NB]) for i in range(2)]
        bsum = [sb(f"bsum{i}", [P, GT, NB]) for i in range(2)]
        neg_m = [sb(f"neg_m{i}", [P, GT]) for i in range(2)]
        run_max = sb("run_max", [P, GT, NB])
        run_sum = sb("run_sum", [P, GT, NB])
        drop = sb("drop", [P, GT, NB])
        rise = sb("rise", [P, GT, NB])
        inv_l = sb("inv_l", [P, GT, NB])
        weight = [sb(f"weight{i}", [P, GT, NB]) for i in range(2)]
        first_low = sb("first_low", [P, GT, NB])
        first_zero = sb("first_zero", [P, GT, NB])
        last_one = sb("last_one", [P, GT, NB])
        pT = [sb(f"pT{i}", [P, HALF]) for i in range(4)]
        oT = [sb(f"oT{i}", [P, QT * P]) for i in range(2)]

        score = [psum(f"score{i}", SEQ) for i in range(2)]
        turn = [psum(f"turn{i}", HALF) for i in range(2)]
        acc = psum("acc", HALF)
        misc = psum("misc", HALF)

        names = ("wo_loaded", "loaded", "scored", "max_ready", "prob_ready", "sum_ready", "drop_ready", "rise_ready",
                 "weight_ready", "scaled", "turned", "evac", "pv_done", "o_ready", "wo_done", "wo_taken",
                 "qk_made", "high_ready", "qk_taken", "q_dealt", "k_dealt", "v_made", "v_taken")
        s = {n: sem(n) for n in names}
        (wo_loaded, loaded, scored, max_ready, prob_ready, sum_ready, drop_ready, rise_ready,
         weight_ready, scaled, turned, evac, pv_done, o_ready, wo_done, wo_taken,
         qk_made, high_ready, qk_taken, q_dealt, k_dealt, v_made, v_taken) = (s[n] for n in names)

        flat = lambda t: t[:].rearrange("p t n -> p (t n)")
        Wq, Wk, Wv, Wo = (w["L0_attn_b_" + n] for n in ("Wq", "Wk", "Wv", "Wo"))

        def slots(eng, slot):
            for r in range(8):
                slot(0, r, True, r >= LAG)
            with eng.Fori(1, PAIRS // 2) as j:
                for r in range(8):
                    slot(j, r, True, True)
            for r in range(LAG + 1):
                slot(PAIRS // 2, r, False, r < LAG)

        groups = 4 * PAIRS

        def projected(j, r, k, scores):
            if k >= 2 and scores:
                rr, n = r, k - 2
            else:
                return None
            i, par = 2 * j + rr // GPP + 1, (rr // GPP + 1) % 2
            return {0: None, 1: ("qk", i, par, n), 2: ("qk", i, par, 2 + n), 3: ("v", i, par, n)}[rr % GPP]

        with nc.Block() as block:

            @block.sync
            def _(sp):
                raw = lambda ap: ap.bitcast(F32)
                sp.dma_start(wo[:], Wo.rearrange("(c p) d -> p c d", p=P)).then_inc(wo_loaded, 16)

                def places(i):
                    b, hp = (i % PAIRS) // (HEADS // 2), i % (HEADS // 2)
                    return (b * SEQ, hp * P) if isinstance(i, int) else (sp.snap(b * SEQ), sp.snap(hp * P))

                def load(par, token, column):
                    sp.dma_start(hb[par][:], hT_dram[:, bass.ds(token, SEQ)]).then_inc(loaded, 16)
                    for a, W in enumerate((Wq, Wk, Wv)):
                        sp.dma_start(wqkv[par][:, a, :], W[:, bass.ds(column, P)]).then_inc(loaded, 16)

                def deal(kind, par):
                    high, low = parts[kind]
                    for h in range(2):
                        mine = slice(h * HD, (h + 1) * HD)
                        if kind == "q":
                            sp.dma_start(raw(QS[par][h][0:HD, :]), raw(high[mine, :])).then_inc(q_dealt, 16)
                            sp.dma_start(raw(QS[par][h][HD:P, :]), raw(low[mine, :])).then_inc(q_dealt, 16)
                        else:
                            for part, dst in ((high, KH), (low, KL)):
                                sp.dma_start(raw(dst[par][h][0:HD, :]), raw(part[mine, :])).then_inc(k_dealt, 16)
                                sp.dma_start(raw(dst[par][h][HD:P, :]), raw(part[mine, :])).then_inc(k_dealt, 16)

                load(0, *places(0))
                sp.wait_ge(qk_taken, 2)
                deal("q", 0)
                sp.wait_ge(qk_taken, 4)
                deal("k", 0)

                def pair(i, c):
                    par, at = (c + 1) % 2, places(i + 1)
                    fixed = lambda v: v if isinstance(v, int) else sp.snap(v)
                    v_before, q_parts, k_parts = (fixed(v) for v in (2 * i, 4 * i + 6, 4 * i + 8))
                    if c == 1 or not isinstance(i, int):
                        sp.wait_ge(v_made, v_before)
                    load(par, *at)
                    sp.wait_ge(qk_taken, q_parts)
                    deal("q", par)
                    sp.wait_ge(qk_taken, k_parts)
                    deal("k", par)

                for c in range(2):
                    pair(c, c)
                with sp.Fori(1, PAIRS // 2) as j:
                    for c in range(2):
                        pair(2 * j + c, c)
                sp.wait_ge(q_dealt, 64 * (PAIRS + 1))
                sp.wait_ge(k_dealt, 128 * (PAIRS + 1))

            @block.tensor
            def _(pe):
                last_use = [None]

                def misc_free():
                    if last_use[0]:
                        pe.wait_ge(*last_use[0])

                def qk_proj(i, par, u):
                    kind, h = u // 2, u % 2
                    misc_free()
                    if u == 0:
                        pe.wait_ge(loaded, 64 * (i + 1))
                    pe.matmul(misc[:], wqkv[par][:, kind, :], hb[par][:, h * HALF:(h + 1) * HALF],
                              start=True, stop=True).then_inc(qk_made, 1)
                    last_use[0] = (qk_taken, 4 * i + u + 1)

                def v_proj(i, par, h):
                    misc_free()
                    for t in range(4):
                        last = pe.matmul(misc[:, t * P:(t + 1) * P], hb[par][:, (4 * h + t) * P:(4 * h + t + 1) * P],
                                         wqkv[par][:, 2, :], start=True, stop=True)
                    last.then_inc(v_made, 1)
                    last_use[0] = (v_taken, 2 * i + h + 1)

                def pv(g, r, kp):
                    par = (r // GPP) % 2
                    pe.wait_ge(evac, 8 * g + 2 * kp + 2)
                    if kp == 0:
                        if not (isinstance(g, int) and g == 0):
                            pe.wait_ge(o_ready, g)
                        pe.wait_ge(v_taken, 2 * (g // GPP) + 2)
                    for kk in range(2):
                        for h in range(2):
                            kt = 2 * kp + kk
                            last = pe.matmul(acc[h * HD:(h + 1) * HD, 0:QT * P], V[par][:, kt, h * HD:(h + 1) * HD],
                                             pT[(2 * kp + h) % 4][:, kk * QT * P:(kk + 1) * QT * P],
                                             start=kt == 0, stop=kt == TPB - 1)
                    last.then_inc(pv_done, 1)

                def slot(j, r, scores, finish):
                    sl, par = 8 * j + r, r // GPP
                    g, gr = sl - LAG, (r - LAG) % 8
                    before = not (isinstance(sl, int) and sl <= LAG)
                    for k in range(GT):
                        if scores:
                            h, q = k // QT, (r % GPP) * QT + k % QT
                            if k == 0:
                                i = 2 * j + par
                                pe.wait_ge(q_dealt, 64 * (i + 1))
                                pe.wait_ge(k_dealt, 128 * (i + 1))
                            if not (isinstance(sl, int) and sl == 0 and k < 2):
                                pe.wait_ge(prob_ready, 4 * sl + k - 1)
                            for c in range(2):
                                for n, Kx in enumerate((KH, KL)):
                                    last = pe.matmul(score[k % 2][:, c * HALF:(c + 1) * HALF], QS[par][h][:, q * P:(q + 1) * P],
                                                     Kx[par][h][:, c * HALF:(c + 1) * HALF], start=n == 0, stop=n == 1)
                            last.then_inc(scored, 1)
                        if finish:
                            if k == 0:
                                pe.wait_ge(scaled, 4 * g + 4)
                            for h in range(2):
                                if before or k > 0:
                                    pe.wait_ge(evac, 8 * g + 2 * k + h - 1)
                                for kk in range(2):
                                    for q in range(QT):
                                        last = pe.transpose(turn[h][:, (kk * QT + q) * P:(kk * QT + q + 1) * P],
                                                            prob[gr % 4][h * QT + q][:, (2 * k + kk) * P:(2 * k + kk + 1) * P],
                                                            ident[:])
                                last.then_inc(turned, 1)
                        if k == 0 and before:
                            pv(g - 1, (gr - 1) % 8, 3)
                        if k > 0 and finish:
                            pv(g, gr, k - 1)
                        if k == 1 and before:
                            misc_free()
                            pe.wait_ge(o_ready, g)
                            hp = ((g - 1) // GPP) % (HEADS // 2)
                            for q in range(QT):
                                last = pe.matmul(misc[:, q * D:(q + 1) * D], oT[(gr - 1) % 2][:, q * P:(q + 1) * P],
                                                 wo[:, bass.ds(hp, 1), :].rearrange("p a d -> p (a d)"), start=True, stop=True)
                            last.then_inc(wo_done, 1)
                            last_use[0] = (wo_taken, g)
                        if k >= 2 and scores:
                            i, nxt = 2 * j + par, (par + 1) % 2
                            if r % GPP == 1:
                                qk_proj(i + 1, nxt, k - 2)
                            if r % GPP == 2:
                                qk_proj(i + 1, nxt, k)
                            if r % GPP == 3:
                                v_proj(i + 1, nxt, k - 2)

                for u in range(4):
                    qk_proj(0, 0, u)
                for h in range(2):
                    v_proj(0, 0, h)
                pe.wait_ge(wo_loaded, 16)
                for r in range(8):
                    slot(0, r, True, r >= LAG)
                with pe.Fori(1, PAIRS // 2) as j:
                    last_use[0] = (v_taken, 4 * j + 2)
                    for r in range(8):
                        slot(j, r, True, True)
                last_use[0] = (v_taken, 2 * PAIRS + 2)
                for r in range(LAG + 1):
                    slot(PAIRS // 2, r, False, r < LAG)

            @block.scalar
            def _(act):
                def high(i, u):
                    kind, h = "qk"[u // 2], u % 2
                    act.wait_ge(qk_made, 4 * i + u + 1)
                    if not (isinstance(i, int) and i == 0):
                        act.wait_ge(q_dealt if kind == "q" else k_dealt, (64 if kind == "q" else 128) * i)
                    act.activation(parts[kind][0][:, h * HALF:(h + 1) * HALF], misc[:], ACT.Copy,
                                   scale=HD ** -0.5 if kind == "q" else 1.0).then_inc(high_ready, 1)

                def v_copy(i, par, h, clear):
                    act.wait_ge(v_made, 2 * i + h + 1)
                    if clear:
                        act.wait_ge(pv_done, 16 * (i - 1))
                    act.activation(V[par][:, 4 * h:4 * h + 4, :].rearrange("p t e -> p (t e)"), misc[:], ACT.Copy).then_inc(v_taken, 1)

                def slot(j, r, scores, finish):
                    sl = 8 * j + r
                    g, gr = sl - LAG, (r - LAG) % 8
                    before = not (isinstance(sl, int) and sl <= LAG)
                    for k in range(GT):
                        if finish:
                            for h in range(2):
                                act.wait_ge(turned, 8 * g + 2 * k + h + 1)
                                if before or k >= 2:
                                    act.wait_ge(pv_done, 4 * g + k - 1)
                                act.activation(pT[(2 * k + h) % 4][:], turn[h][:], ACT.Copy).then_inc(evac, 1)
                        made = projected(j, r, k, scores)
                        if made and made[0] == "qk":
                            high(made[1], made[3])
                        if made and made[0] == "v":
                            v_copy(*made[1:], clear=not (isinstance(made[1], int) and made[1] < 2))
                        if scores:
                            act.wait_ge(max_ready, 4 * sl + k + 1)
                            if k == 0 and not (isinstance(sl, int) and sl < 4):
                                act.wait_ge(turned, 8 * (sl - 3))
                            act.activation(prob[r % 4][k][:], score[k % 2][:], ACT.Exp,
                                           bias=neg_m[r % 2][:, k:k + 1]).then_inc(prob_ready, 1)
                        if k == 0 and before:
                            act.wait_ge(pv_done, 4 * g)
                            act.activation(oT[(gr - 1) % 2][:], acc[:, 0:QT * P], ACT.Copy).then_inc(o_ready, 1)
                        if k == 0 and not (isinstance(sl, int) and sl == 0) and (scores or r == 0):
                            act.wait_ge(drop_ready, sl)
                            act.activation(flat(rise), flat(drop), ACT.Exp, scale=-1.0).then_inc(rise_ready, 1)

                for u in range(4):
                    high(0, u)
                for h in range(2):
                    v_copy(0, 0, h, False)
                slots(act, slot)

            @block.vector
            def _(dve):
                chain = Chain(dve, shared)

                def low(i, u):
                    kind, h = "qk"[u // 2], u % 2
                    hi, lo = (t[:, h * HALF:(h + 1) * HALF] for t in parts[kind])
                    dve.wait_ge(high_ready, 4 * i + u + 1)
                    dve.scalar_tensor_tensor(lo, misc[:], HD ** -0.5 if kind == "q" else 1.0, hi.bitcast(F32),
                                             ALU.mult, ALU.subtract).then_inc(qk_taken, 1)

                def block_sums(n, r, k):
                    dve.wait_ge(prob_ready, 4 * n + k + 1)
                    dve.tensor_reduce(bsum[r % 2][:, k, :], prob[r % 4][k][:].rearrange("p (n c) -> p n c", c=KV_BLOCK), AX,
                                      ALU.add).then_inc(sum_ready, 1)

                def weights_begin(n, r):
                    dve.wait_ge(sum_ready, 4 * n + 4)
                    chain.link(dve.tensor_tensor_scan(flat(run_max), flat(first_low), flat(bmax[r % 2]), 0.0, ALU.add, ALU.max))
                    dve.tensor_tensor_scan(flat(run_sum), flat(first_zero), flat(bsum[r % 2]), 0.0, ALU.mult, ALU.add)
                    chain.link(dve.tensor_tensor(run_max[:], run_max[:], neg_m[r % 2][:].unsqueeze(2).to_broadcast([P, GT, NB]), ALU.add))
                    dve.tensor_scalar(flat(drop), flat(run_max), -80.0, None, ALU.max).then_inc(drop_ready, 1)

                def weights_end(n, r, clear):
                    dve.wait_ge(rise_ready, n + 1)
                    chain.link(dve.tensor_tensor(flat(inv_l), flat(rise), flat(run_sum), ALU.mult))
                    chain.link(dve.tensor_scalar(flat(run_sum), flat(inv_l), 1.0, None, ALU.max))
                    chain.link(dve.reciprocal(flat(inv_l), flat(run_sum)))
                    if clear:
                        dve.wait_ge(scaled, 4 * n - 4)
                    dve.tensor_tensor_scan(flat(weight[r % 2])[:, ::-1], flat(last_one)[:, ::-1], flat(inv_l)[:, ::-1], 0.0,
                                           ALU.max, ALU.mult).then_inc(weight_ready, 1)

                def slot(j, r, scores, finish):
                    sl = 8 * j + r
                    g, gr = sl - LAG, (r - LAG) % 8
                    first = isinstance(sl, int) and sl == 0
                    before = not (isinstance(sl, int) and sl <= LAG)
                    rest = not first and (scores or r == 0)
                    for k in range(GT):
                        if scores:
                            dve.wait_ge(scored, 4 * sl + k + 1)
                            chain.link(dve.tensor_reduce(bmax[r % 2][:, k, :], score[k % 2][:].rearrange("p (n c) -> p n c", c=KV_BLOCK), AX, ALU.max))
                            dve.tensor_reduce(neg_m[r % 2][:, k:k + 1], bmax[r % 2][:, k, :], AX, ALU.max, negate=True).then_inc(max_ready, 1)
                        if k == 1 and before:
                            q = (gr - 1) % GPP
                            b = (g - 1) // (4 * HEADS // 2)
                            Xq = X[:, bass.ds(b * TPB + q * QT, QT), :]
                            dve.wait_ge(wo_done, g)
                            dve.tensor_tensor(Xq, misc[:, 0:QT * D].rearrange("p (q d) -> p q d", d=D), Xq, ALU.add).then_inc(wo_taken, 1)
                        if k == 0 and rest:
                            block_sums(sl - 1, (r - 1) % 8, GT - 1)
                        if k > 0 and scores:
                            block_sums(sl, r, k - 1)
                        made = projected(j, r, k, scores)
                        if made and made[0] == "qk":
                            low(made[1], made[3])
                        if k == 0 and rest:
                            weights_begin(sl - 1, (r - 1) % 8)
                        if k == 1 and rest:
                            weights_end(sl - 1, (r - 1) % 8, not (isinstance(sl, int) and sl < 3 and scores))

                chain.link(dve.memset(first_low[:], 0.0))
                chain.link(dve.memset(first_low[:, :, 0:1], -BIG))
                chain.link(dve.memset(first_zero[:], 1.0))
                chain.link(dve.memset(first_zero[:, :, 0:1], 0.0))
                chain.link(dve.memset(last_one[:], 0.0))
                chain.link(dve.memset(last_one[:, :, NB - 1:NB], 1.0))
                for u in range(4):
                    low(0, u)

                links = GT + 2 + 3
                for r in range(8):
                    slot(0, r, True, r >= LAG)
                with dve.Fori(1, PAIRS // 2) as j:
                    chain.enter_from(j, 1, 8 * links)
                    for r in range(8):
                        slot(j, r, True, True)
                chain.leave(PAIRS // 2 - 1)
                for r in range(LAG + 1):
                    slot(PAIRS // 2, r, False, r < LAG)
                chain.close()

            @block.gpsimd
            def _(pool):
                def weigh(n, r, k):
                    pool.wait_ge(weight_ready, n + 1)
                    tile = prob[r % 4][k][:].rearrange("p (n c) -> p n c", c=KV_BLOCK)
                    pool.tensor_tensor(tile, tile, weight[r % 2][:, k, :].unsqueeze(2).to_broadcast([P, NB, KV_BLOCK]),
                                       ALU.mult).then_inc(scaled, 1)

                def slot(j, r, scores, finish):
                    sl = 8 * j + r
                    for k in range(GT):
                        if (scores or r == 0) and not (isinstance(sl, int) and sl == 0):
                            weigh(sl - 1, (r - 1) % 8, k)

                slots(pool, slot)


def program(nc, w, out):
    with ExitStack() as ctx:
        X = ctx.enter_context(nc.sbuf_tensor("X", [P, TILES, D], F32))
        ident = ctx.enter_context(nc.sbuf_tensor("ident", [P, P], F32))
        shared = Shared(lambda name: ctx.enter_context(nc.semaphore(name)))
        x_loaded = ctx.enter_context(nc.semaphore("x_loaded"))
        ident_made = ctx.enter_context(nc.semaphore("ident_made"))
        x_stored = ctx.enter_context(nc.semaphore("x_stored"))
        tiles = lambda t: t.rearrange("b (n p) d -> p (b n) d", p=P)

        with nc.Block() as block:

            @block.sync
            def _(sp):
                sp.dma_start(X[:], tiles(w["L0_attn_a_x"])).then_inc(x_loaded, 16)
                sp.wait_ge(x_loaded, 16)

            @block.gpsimd
            def _(pool):
                pool.memset(ident[:], 0.0).then_inc(ident_made, 1)
                pool.wait_ge(ident_made, 1)
                pool.affine_select(out=ident[:], in_=ident[:], compare_op=ALU.not_equal, fill=1.0, base=0,
                                   pattern=[[-1, P]], channel_multiplier=1).then_inc(ident_made, 1)
                pool.wait_ge(ident_made, 2)

        folded = ExpertWeights(nc)
        sigmoid_attention(nc, X, ident, w, folded, shared)
        gated_experts(nc, X, ident, w, folded, shared, "f1_")
        block_softmax_attention(nc, X, ident, w, shared)
        gated_experts(nc, X, ident, w, folded, shared, "f2_")

        with nc.Block() as block:

            @block.sync
            def _(sp):
                sp.dma_start(tiles(out), X[:]).then_inc(x_stored, 16)
                sp.wait_ge(x_stored, 16)


INPUTS = ["L0_attn_a_x", "L0_attn_a_Wq", "L0_attn_a_bq", "L0_attn_a_Wk", "L0_attn_a_bk", "L0_attn_a_Wv", "L0_attn_a_bv",
          "L0_attn_a_Wo", "L0_attn_a_bo", "L0_attn_a_layerscale", "L0_attn_b_Wq", "L0_attn_b_Wk", "L0_attn_b_Wv",
          "L0_attn_b_Wo", "L0_ffn_ln_g", "L0_ffn_ln_b", "L0_ffn_router_w", "L0_ffn_eg", "L0_ffn_eb", "L0_ffn_W1",
          "L0_ffn_b1", "L0_ffn_W2", "L0_ffn_b2", "L0_ffn_Wo", "L0_ffn_bo"]


def kernel(**inputs):
    import numpy as np
    import concourse.bacc as bacc
    from concourse.bass_utils import run_bass_kernel_spmd

    nc = bacc.Bacc("TRN2", target_bir_lowering=False, num_devices=1)
    arrays, w = {}, {}
    for name in INPUTS:
        arrays["in_" + name] = np.ascontiguousarray(inputs[name])
        w[name] = nc.dram_tensor("in_" + name, arrays["in_" + name].shape, F32, kind="ExternalInput").ap()
    out = nc.dram_tensor("out_0", arrays["in_L0_attn_a_x"].shape, F32, kind="ExternalOutput").ap()
    program(nc, w, out)
    r = run_bass_kernel_spmd(nc, [arrays], core_ids=[0])
    return r.results[0]["out_0"]
```

```python
import math
from contextlib import ExitStack

import concourse.bass as bass
from concourse import mybir

F32 = mybir.dt.float32
F32R = mybir.dt.float32r
ALU = mybir.AluOpType
ACT = mybir.ActivationFunctionType
AX = mybir.AxisListType.X

P = 128
D = 128
BATCH = 4
SEQ = 1024
TPB = SEQ // P
TILES = BATCH * TPB
HALF = 512
EPS = 1e-5


class Shared:

    def __init__(self, sem):
        self.chain_sem = sem("dve_chain")
        self.links = 0
        self.norm_sems = [sem("ln_" + n) for n in ("centred", "squared", "var_ready", "std_ready")]
        self.norms = 0


class Chain:

    def __init__(self, eng, shared):
        self.eng, self.shared, self.sem = eng, shared, shared.chain_sem
        self.base, self.k = shared.links, 0

    def close(self):
        self.shared.links = self.base + self.k

    def link(self, ins):
        ins.then_inc(self.sem, 1)
        self.k += 1
        self.eng.wait_ge(self.sem, self.base + self.k)

    def mark(self, ins):
        ins.then_inc(self.sem, 1)
        self.k += 1
        return self.base + self.k

    def wait(self, value):
        self.eng.wait_ge(self.sem, value)

    def enter_from(self, i, first, per):
        self.start, self.per = self.base + self.k, per
        self.base, self.k = (i - first) * per + self.start, 0

    def leave(self, times):
        assert self.k == self.per, (self.k, self.per)
        self.base, self.k = self.start + times * self.per, 0


class Norm:

    def __init__(self, sb, shared, rows, calls, ways=1):
        many = lambda name, cols: [sb(f"ln_{name}{i}", [P, cols]) for i in range(ways)]
        self.sums, self.mean, self.var, self.std, self.rstd = (many(n, rows) for n in ("sums", "mean", "var", "std", "rstd"))
        self.sq = many("sq", rows * D)
        self.centred, self.squared, self.var_ready, self.std_ready = shared.norm_sems
        self.before = shared.norms
        shared.norms += calls

    @staticmethod
    def wide(t, n, shape):
        per = t[:, 0:n] if len(shape) == 3 else t[:, 0:n].rearrange("p (a b) -> p a b", b=shape[2])
        return per, per.unsqueeze(len(shape) - 1).to_broadcast(shape)

    def centre(self, dve, chain, src, dst, n, call, way=0):
        sums, mean, shape = self.sums[way], self.mean[way], list(src.shape)
        chain.link(dve.tensor_reduce(self.wide(sums, n, shape)[0], src, AX, ALU.add))
        chain.link(dve.tensor_scalar(mean[:, 0:n], sums[:, 0:n], 1.0 / D, None, ALU.mult))
        dve.tensor_tensor(dst, src, self.wide(mean, n, shape)[1], ALU.subtract).then_inc(self.centred, 1)

    def square(self, act, dst, n, call, way=0):
        act.wait_ge(self.centred, self.before + call + 1)
        sq = self.sq[way][:, 0:n * D]
        sq = sq.rearrange("p (n d) -> p n d", d=D) if len(dst.shape) == 3 else sq.rearrange("p (a b d) -> p a b d", b=dst.shape[2], d=D)
        act.activation(sq, dst, ACT.Square).then_inc(self.squared, 1)

    def variance(self, dve, chain, n, call, way=0, gain=1.0, add=EPS):
        dve.wait_ge(self.squared, self.before + call + 1)
        chain.link(dve.tensor_reduce(self.sums[way][:, 0:n], self.sq[way][:, 0:n * D].rearrange("p (n d) -> p n d", d=D), AX, ALU.add))
        dve.tensor_scalar(self.var[way][:, 0:n], self.sums[way][:, 0:n], gain / D, add, ALU.mult, ALU.add).then_inc(self.var_ready, 1)

    def root(self, act, n, call, way=0):
        act.wait_ge(self.var_ready, self.before + call + 1)
        act.activation(self.std[way][:, 0:n], self.var[way][:, 0:n], ACT.Sqrt).then_inc(self.std_ready, 1)

    def scale(self, dve, chain, dst, n, call, way=0):
        sums, mean, var, std, rstd = (t[way][:, 0:n] for t in (self.sums, self.mean, self.var, self.std, self.rstd))
        dve.wait_ge(self.std_ready, self.before + call + 1)
        chain.link(dve.reciprocal(rstd, std))
        chain.link(dve.tensor_tensor(mean, rstd, rstd, ALU.mult))
        chain.link(dve.tensor_tensor(sums, mean, var, ALU.mult))
        chain.link(dve.tensor_scalar(mean, sums, -0.5, 1.5, ALU.mult, ALU.add))
        chain.link(dve.tensor_tensor(rstd, rstd, mean, ALU.mult))
        return dve.tensor_tensor(dst, dst, self.wide(self.rstd[way], n, list(dst.shape))[1], ALU.mult)


SQUARE_AT, ROOT_AT, FOLD_AT = 8, 11, 13


def sigmoid_attention(nc, X, ident, w, folded, shared):
    with ExitStack() as ctx:
        sb = lambda name, shape, dt=F32: ctx.enter_context(nc.sbuf_tensor("a_" + name, shape, dt))
        bank = lambda name: ctx.enter_context(nc.psum_tensor("a_" + name, [P, HALF], F32))
        sem = lambda name: ctx.enter_context(nc.semaphore("a_" + name))

        wnat = sb("wnat", [P, 4, D])
        wT = sb("wT", [P, 4, D])
        bqkv = sb("bqkv", [P, 3, D])
        bo = sb("bo", [P, D])
        ls = sb("ls", [P, D])
        norm = Norm(sb, shared, 2 * TPB, 2 * BATCH, ways=2)
        fold = Fold(sb, sem, w, folded)
        clear = Clear(sb, sem, folded)
        hn = sb("hn", [P, TPB, D])
        hT = sb("hT", [P, SEQ])
        qkv = [sb(f"qkv{i}", [P, TPB, 3, D]) for i in range(2)]
        qkT = [sb(f"qkT{i}", [P, 2, SEQ]) for i in range(2)]
        AT = sb("AT", [P, 3, HALF])
        oT = sb("oT", [P, SEQ])
        upd = sb("upd", [P, 2, 4, D])
        neg_log = sb("neg_log", [P, 1])

        ring = [bank(f"ring{i}") for i in range(2)]
        score = [bank(f"score{i}") for i in range(2)]
        acc = [bank(f"acc{i}") for i in range(2)]
        proj = [bank(f"proj{i}") for i in range(2)]

        loaded = sem("loaded")
        consts = sem("consts")
        w_turned = sem("w_turned")
        w_ready = sem("w_ready")
        hn_ready = sem("hn_ready")
        turned = sem("turned")
        evac = sem("evac")
        qkv_made = sem("qkv_made")
        qkv_taken = sem("qkv_taken")
        qk_ready = sem("qk_ready")
        scored = sem("scored")
        attn_ready = sem("attn_ready")
        pv_done = sem("pv_done")
        o_ready = sem("o_ready")
        proj_done = sem("proj_done")
        proj_taken = sem("proj_taken")


        with nc.allow_non_contiguous_dma("small vectors, once"), nc.Block() as block:

            @block.sync
            def _(sp):
                for i, name in enumerate(("Wq", "Wk", "Wv", "Wo")):
                    sp.dma_start(wnat[:, i, :], w["L0_attn_a_" + name]).then_inc(loaded, 16)
                for i, name in enumerate(("bq", "bk", "bv")):
                    sp.dma_start(bqkv[:, i, :], w["L0_attn_a_" + name].partition_broadcast(P)).then_inc(loaded, 16)
                sp.dma_start(bo[:], w["L0_attn_a_bo"].partition_broadcast(P)).then_inc(loaded, 16)
                sp.dma_start(ls[:], w["L0_attn_a_layerscale"].partition_broadcast(P)).then_inc(loaded, 16)
                fold.sync(sp)

            @block.gpsimd
            def _(pool):
                clear.pool(pool)
                fold.pool(pool)

            @block.tensor
            def _(pe):
                def turn_tokens(b):
                    pe.wait_ge(hn_ready, b + 1)
                    for g in range(2):
                        for j in range(4):
                            last = pe.transpose(ring[g][:, j * P:(j + 1) * P], hn[:, 4 * g + j, :], ident[:])
                        last.then_inc(turned, 1)

                def project(b, j):
                    if j < 2:
                        pe.wait_ge(evac, 6 * b + 2)
                    else:
                        pe.wait_ge(qkv_taken, TPB * b + j - 1)
                    pe.matmul(ring[j % 2][:, 0:3 * D], hT[:, j * P:(j + 1) * P],
                              wT[:, 0:3, :].rearrange("p a e -> p (a e)"), start=True, stop=True).then_inc(qkv_made, 1)

                def turn_qk(b, g):
                    if g == 0:
                        pe.wait_ge(qk_ready, b + 1)
                    if g >= 2:
                        pe.wait_ge(evac, 6 * b + g + 1)
                    for j in range(4):
                        last = pe.transpose(ring[g % 2][:, j * P:(j + 1) * P], qkv[b % 2][:, 4 * (g % 2) + j, g // 2, :], ident[:])
                    last.then_inc(turned, 1)

                def scores(b, u):
                    t, h = u // 2, u % 2
                    if u >= 2:
                        pe.wait_ge(attn_ready, 16 * b + u - 1)
                    pe.matmul(score[u % 2][:], qkT[b % 2][:, 1, t * P:(t + 1) * P], qkT[b % 2][:, 0, h * HALF:(h + 1) * HALF],
                              start=True, stop=True).then_inc(scored, 1)

                def beside(b, u):
                    if u == 0:
                        turn_tokens(b)
                    if 1 <= u <= TPB // 2:
                        project(b, 2 * u - 2)
                        project(b, 2 * u - 1)
                    if u >= 2 * TPB - 2:
                        turn_qk(b, 2 * (u - 2 * TPB + 2))
                        turn_qk(b, 2 * (u - 2 * TPB + 2) + 1)

                pe.wait_ge(loaded, 9 * 16)
                for i in range(4):
                    last = pe.transpose(ring[0][:, i * P:(i + 1) * P], wnat[:, i, :], ident[:])
                last.then_inc(w_turned, 1)
                pe.wait_ge(w_ready, 1)
                for u in range(2 * TPB):
                    beside(0, u)
                for b in range(BATCH):
                    pe.wait_ge(evac, 6 * b + 6)
                    scores(b, 0)
                    for u in range(2 * TPB):
                        if u + 1 < 2 * TPB:
                            scores(b, u + 1)
                        if b + 1 < BATCH:
                            beside(b + 1, u)
                        if u == FOLD_AT:
                            if b:
                                pe.wait_ge(proj_taken, 2 * b)
                            for e in (2 * b, 2 * b + 1):
                                fold.tensor(pe, e, proj[e % 2])
                        t, h = u // 2, u % 2
                        pe.wait_ge(attn_ready, 16 * b + u + 1)
                        pe.matmul(acc[h][:], qkv[b % 2][:, t, 2, :], AT[:, u % 3, :], start=t == 0, stop=t == TPB - 1).then_inc(pv_done, 1)
                    pe.wait_ge(fold.bias_ready, 2 * b + 2)
                    for h in range(2):
                        pe.wait_ge(o_ready, 2 * b + h + 1)
                        for j in range(4):
                            last = pe.matmul(proj[h][:, j * D:(j + 1) * D], oT[:, (4 * h + j) * P:(4 * h + j + 1) * P],
                                             wT[:, 3, :], start=True, stop=True)
                        last.then_inc(proj_done, 1)

            @block.scalar
            def _(act):
                def copy_tokens(b):
                    for g in range(2):
                        act.wait_ge(turned, 6 * b + g + 1)
                        act.activation(hT[:, g * HALF:(g + 1) * HALF], ring[g][:], ACT.Copy).then_inc(evac, 1)

                def copy_qk(b, g):
                    act.wait_ge(turned, 6 * b + 3 + g)
                    act.activation(qkT[b % 2][:, g // 2, (g % 2) * HALF:(g % 2 + 1) * HALF], ring[g % 2][:], ACT.Copy).then_inc(evac, 1)

                def beside(b, u):
                    if u == 0:
                        copy_tokens(b)
                    if u == SQUARE_AT:
                        norm.square(act, qkv[b % 2][:, :, 0:2, :], 2 * TPB, 2 * b + 1, 0)
                    if u == SQUARE_AT + 1 and b + 1 < BATCH:
                        norm.square(act, hn[:], TPB, 2 * b + 2, 1)
                    if u == ROOT_AT:
                        norm.root(act, 2 * TPB, 2 * b + 1, 0)
                        if b + 1 < BATCH:
                            norm.root(act, TPB, 2 * b + 2, 1)
                    if u >= 2 * TPB - 2:
                        copy_qk(b, 2 * (u - 2 * TPB + 2))
                        copy_qk(b, 2 * (u - 2 * TPB + 2) + 1)

                norm.square(act, hn[:], TPB, 0, 1)
                norm.root(act, TPB, 0, 1)
                for u in range(2 * TPB):
                    beside(0, u)
                act.wait_ge(consts, 1)
                for b in range(BATCH):
                    clear.act(act, b)
                    for u in range(2 * TPB):
                        act.wait_ge(scored, 16 * b + u + 1)
                        if u >= 3:
                            act.wait_ge(pv_done, 16 * b + u - 2)
                        act.activation(AT[:, u % 3, :], score[u % 2][:], ACT.Sigmoid, bias=neg_log[:],
                                       scale=1.0 / math.sqrt(D)).then_inc(attn_ready, 1)
                        if b + 1 < BATCH:
                            beside(b + 1, u)
                    for h in range(2):
                        act.wait_ge(pv_done, 16 * b + 15 + h)
                        act.activation(oT[:, h * HALF:(h + 1) * HALF], acc[h][:], ACT.Copy).then_inc(o_ready, 1)
                clear.act_end(act)

            @block.vector
            def _(dve):
                chain = Chain(dve, shared)

                def tokens(b):
                    return X[:, b * TPB:(b + 1) * TPB, :]

                def add_bias(b):
                    for j in range(TPB):
                        dve.wait_ge(qkv_made, TPB * b + j + 1)
                        dve.tensor_tensor(qkv[b % 2][:, j, :, :].rearrange("p a e -> p (a e)"), ring[j % 2][:, 0:3 * D],
                                          bqkv[:].rearrange("p a e -> p (a e)"), ALU.add).then_inc(qkv_taken, 1)
                    dve.wait_ge(qkv_taken, TPB * (b + 1))

                def norms(b):
                    qk, more = qkv[b % 2][:, :, 0:2, :], b + 1 < BATCH
                    norm.centre(dve, chain, qk, qk, 2 * TPB, 2 * b + 1, 0)
                    if more:
                        norm.centre(dve, chain, tokens(b + 1), hn[:], TPB, 2 * b + 2, 1)
                    norm.variance(dve, chain, 2 * TPB, 2 * b + 1, 0)
                    if more:
                        norm.variance(dve, chain, TPB, 2 * b + 2, 1)
                    norm.scale(dve, chain, qk, 2 * TPB, 2 * b + 1, 0).then_inc(qk_ready, 1)
                    if more:
                        norm.scale(dve, chain, hn[:], TPB, 2 * b + 2, 1).then_inc(hn_ready, 1)

                def update(b):
                    for h in range(2):
                        dve.wait_ge(proj_done, 2 * b + h + 1)
                        wide = lambda t: t[:].unsqueeze(1).to_broadcast([P, 4, D])
                        Xh = X[:, b * TPB + 4 * h:b * TPB + 4 * h + 4, :]
                        chain.link(dve.tensor_tensor(upd[:, h], proj[h][:].rearrange("p (j e) -> p j e", e=D), wide(bo), ALU.add))
                        chain.link(dve.tensor_tensor(upd[:, h], upd[:, h], wide(ls), ALU.mult))
                        dve.tensor_tensor(Xh, Xh, upd[:, h], ALU.add).then_inc(proj_taken, 1)

                dve.memset(neg_log[:], -math.log(float(SEQ))).then_inc(consts, 1)
                norm.centre(dve, chain, tokens(0), hn[:], TPB, 0, 1)
                norm.variance(dve, chain, TPB, 0, 1)
                norm.scale(dve, chain, hn[:], TPB, 0, 1).then_inc(hn_ready, 1)
                dve.wait_ge(loaded, 9 * 16)
                dve.wait_ge(w_turned, 1)
                dve.tensor_copy(wT[:].rearrange("p a e -> p (a e)"), ring[0][:]).then_inc(w_ready, 1)
                add_bias(0)
                norms(0)
                for b in range(BATCH):
                    if b:
                        update(b - 1)
                    if b + 1 < BATCH:
                        add_bias(b + 1)
                        norms(b + 1)
                    for e in (2 * b, 2 * b + 1):
                        fold.vector(dve, chain, e, proj[e % 2])
                update(BATCH - 1)
                chain.close()




EXPERTS = 8
HIDDEN = 512
HC = HIDDEN // P
ROWS = 512
BLOCKS = (2 * BATCH * SEQ - EXPERTS) // ROWS + EXPERTS
MOST = BATCH * SEQ // ROWS
PLACES = EXPERTS * MOST + 1
CLAMP = 10000.0


class ExpertWeights:

    def __init__(self, nc):
        dram = lambda name, shape: nc.dram_tensor(name, shape, F32, kind="Internal").ap()
        self.w12 = dram("f_w12", [EXPERTS * P, 2 * HIDDEN])
        self.bias = dram("f_bias", [EXPERTS * P, 4 * HC])
        self.sorted_rows = dram("f_sorted", [PLACES * ROWS, D])


class Clear:

    def __init__(self, sb, sem, folded):
        self.zero = sb("zero", [P, ROWS // P * D])
        self.rows = folded.sorted_rows.rearrange("(n p k) d -> n p (k d)", p=P, k=ROWS // P)
        self.zeroed, self.cleared = sem("zeroed"), sem("cleared")

    def pool(self, pool):
        pool.memset(self.zero[:], 0.0).then_inc(self.zeroed, 1)

    def act(self, act, b):
        if b == 0:
            act.wait_ge(self.zeroed, 1)
        for n in range(b * PLACES // BATCH, (b + 1) * PLACES // BATCH):
            act.dma_start(self.rows[n], self.zero[:]).then_inc(self.cleared, 16)

    def act_end(self, act):
        act.wait_ge(self.cleared, 16 * PLACES)


class Fold:

    def __init__(self, sb, sem, w, folded):
        self.w, self.folded = w, folded
        self.eg, self.eb = sb("eg", [P, EXPERTS]), sb("eb", [P, EXPERTS])
        self.b12 = sb("b12", [P, EXPERTS, 2 * HC])
        self.wbuf = [sb(f"wbuf{i}", [P, 2, HIDDEN]) for i in range(2)]
        self.wg = [sb(f"wg{i}", [P, 2, HIDDEN]) for i in range(2)]
        self.bout = [sb(f"bout{i}", [P, 4, HC]) for i in range(2)]
        self.vec_loaded, self.made, self.scaled, self.bias_ready = (sem("fold_" + n) for n in ("vec_loaded", "made", "scaled", "bias_ready"))
        self.loaded, self.stored = ([sem(f"fold_{n}{i}") for i in range(2)] for n in ("loaded", "stored"))
        self.VECTORS = 16 * (2 + 2 * EXPERTS)

    def sync(self, sp):
        def load(e):
            for a, name in enumerate(("W1", "W2")):
                sp.dma_start(self.wbuf[e % 2][:, a, :], self.w["L0_ffn_" + name][e, :, :]).then_inc(self.loaded[e % 2], 16)

        sp.dma_start(self.eg[:], self.w["L0_ffn_eg"].rearrange("e d -> d e")).then_inc(self.vec_loaded, 16)
        sp.dma_start(self.eb[:], self.w["L0_ffn_eb"].rearrange("e d -> d e")).then_inc(self.vec_loaded, 16)
        for a, name in enumerate(("b1", "b2")):
            for e in range(EXPERTS):
                sp.dma_start(self.b12[:, e, a * HC:(a + 1) * HC], self.w["L0_ffn_" + name][e, :].rearrange("(c p) -> p c", p=P))\
                  .then_inc(self.vec_loaded, 16)
        load(0)
        load(1)
        for e in range(EXPERTS):
            sp.wait_ge(self.scaled, e + 1)
            sp.dma_start(self.folded.w12[e * P:(e + 1) * P, :], self.wg[e % 2][:].rearrange("p a h -> p (a h)")).then_inc(self.stored[e % 2], 16)
            sp.wait_ge(self.bias_ready, e + 1)
            sp.dma_start(self.folded.bias[e * P:(e + 1) * P, :], self.bout[e % 2][:].rearrange("p a c -> p (a c)")).then_inc(self.stored[e % 2], 16)
            if e + 2 < EXPERTS:
                load(e + 2)
        for i in range(2):
            sp.wait_ge(self.stored[i], 16 * EXPERTS)

    def pool(self, pool):
        pool.wait_ge(self.vec_loaded, self.VECTORS)
        for e in range(EXPERTS):
            pool.wait_ge(self.loaded[e % 2], 32 * (e // 2 + 1))
            if e >= 2:
                pool.wait_ge(self.stored[e % 2], 32 * (e // 2))
            pool.tensor_tensor(self.wg[e % 2][:], self.wbuf[e % 2][:],
                               self.eg[:, e:e + 1].unsqueeze(2).to_broadcast([P, 2, HIDDEN]), ALU.mult).then_inc(self.scaled, 1)

    def tensor(self, pe, e, bank):
        if e == 0:
            pe.wait_ge(self.vec_loaded, self.VECTORS)
        pe.wait_ge(self.loaded[e % 2], 32 * (e // 2 + 1))
        for a in range(2):
            for c in range(HC):
                last = pe.matmul(bank[:, a * HC + c:a * HC + c + 1], self.wbuf[e % 2][:, a, c * P:(c + 1) * P],
                                 self.eb[:, e:e + 1], start=True, stop=True)
        last.then_inc(self.made, 1)

    def vector(self, dve, chain, e, bank):
        bout = self.bout[e % 2]
        if e == 0:
            dve.wait_ge(self.vec_loaded, self.VECTORS)
        if e >= 2:
            dve.wait_ge(self.stored[e % 2], 32 * (e // 2))
        dve.wait_ge(self.made, e + 1)
        chain.link(dve.tensor_tensor(bout[:, 0:2, :].rearrange("p a c -> p (a c)"), bank[:, 0:2 * HC], self.b12[:, e, :], ALU.add))
        dve.tensor_scalar(bout[:, 2, :], bout[:, 1, :], -1.0, -20.0, ALU.mult, ALU.add)
        dve.tensor_scalar(bout[:, 3, :], bout[:, 1, :], -1.0, 20.0, ALU.mult, ALU.add).then_inc(self.bias_ready, 1)


class Choices:

    def __init__(self, sb):
        self.slots = sb("slots", [P, 2, TILES], mybir.dt.uint32)
        self.gates = sb("gates", [P, 2, TILES])


def gated_experts(nc, X, ident, w, folded, choices, shared, tag):
    with ExitStack() as ctx:
        sb = lambda name, shape, dt=F32: ctx.enter_context(nc.sbuf_tensor(tag + name, shape, dt))
        blocks = sb("blocks", [P, 2, BLOCKS], mybir.dt.int32)
        sort_tokens(nc, X, ident, w, choices.slots, choices.gates, blocks, folded.sorted_rows, shared, tag + "s_")
        run_experts(nc, ident, w, folded, blocks, shared, tag + "e_")


def sort_tokens(nc, X, ident, w, slots, gates, blocks, sorted_rows, shared, tag):
    E8 = EXPERTS
    HT = 2 * TPB
    with ExitStack() as ctx:
        sb = lambda name, shape, dt=F32: ctx.enter_context(nc.sbuf_tensor(tag + name, shape, dt))
        bank = lambda name: ctx.enter_context(nc.psum_tensor(tag + name, [P, HALF], F32))
        sem = lambda name: ctx.enter_context(nc.semaphore(tag + name))
        norm = Norm(sb, shared, TPB, 2 * BATCH, ways=2)
        gain, shift = sb("gain", [P, D]), sb("shift", [P, D])
        rw = sb("rw", [P, EXPERTS])
        zall = sb("zall", [P, TILES, D])
        logits = sb("logits", [P, TILES, EXPERTS])
        xn = [sb(f"xn{i}", [P, TPB, D]) for i in range(2)]
        xfT = [sb(f"xfT{i}", [P, SEQ]) for i in range(2)]
        tri = sb("tri", [P, E8, E8])
        before = sb("before", [P, P])
        ones = sb("ones", [P, P])
        counts_to = sb("counts_to", [P, E8, MOST])
        block_no = sb("block_no", [P, BLOCKS])
        origin = sb("origin", [P, E8])
        first_zero = sb("first_zero", [P, E8, HT])
        cmp = sb("cmp", [P, HT, E8, E8])
        cmp2 = sb("cmp2", [P, HT, E8, E8])
        rank = sb("rank", [P, HT, E8])
        picked = sb("picked", [P, 3, TILES, E8])
        work = sb("work", [P, TILES, E8])
        top = sb("top", [P, 4, TILES])
        per_tile = sb("per_tile", [P, E8, HT])
        prefix = sb("prefix", [P, E8, HT])
        pos = sb("pos", [P, HT, E8])
        place = [sb(f"place{i}", [P, E8]) for i in range(3)]
        total = sb("total", [P, E8])
        blocks_of = sb("blocks_of", [P, E8])
        block_end = sb("block_end", [P, E8])
        all_one = sb("all_one", [P, E8])
        cmp3 = sb("cmp3", [P, E8, MOST])
        ended = sb("ended", [P, BLOCKS, E8 - 1])
        ends = sb("ends", [P, BLOCKS, E8 - 1])
        owner = sb("owner", [P, BLOCKS])
        first = sb("first", [P, BLOCKS])
        slot_f = sb("slot_f", [P, 2, HT])
        turn = [bank(f"turn{i}") for i in range(4)]
        lg = [bank(f"lg{i}") for i in range(2)]
        within, totals = bank("within"), bank("totals")
        (loaded, normed, gained, xf_ready, turned, evac, routed, consts, picked_ready, counted, gap_ready, exp_ready,
         slots_ready, moved) = (sem(n) for n in ("loaded", "normed", "gained", "xf_ready", "turned", "evac", "routed", "consts",
                                                 "picked_ready", "counted", "gap_ready", "exp_ready", "slots_ready", "moved"))
        n_consts = 8
        HEAD_START = 4

        with nc.Block() as block:

            @block.sync
            def _(sp):
                sp.dma_start(gain[:], w["L0_ffn_ln_g"].partition_broadcast(P)).then_inc(loaded, 16)
                sp.dma_start(shift[:], w["L0_ffn_ln_b"].partition_broadcast(P)).then_inc(loaded, 16)
                sp.dma_start(rw[:], w["L0_ffn_router_w"]).then_inc(loaded, 16)

            @block.gpsimd
            def _(pool):
                pool.memset(tri[:], 1.0).then_inc(consts, 1)
                pool.memset(before[:], 1.0).then_inc(consts, 1)
                pool.memset(ones[:], 1.0).then_inc(consts, 1)
                pool.wait_ge(consts, 3)
                pool.affine_select(out=tri[:], in_=tri[:], compare_op=ALU.is_gt, fill=0.0, base=0,
                                   pattern=[[1, E8], [-1, E8]], channel_multiplier=0).then_inc(consts, 1)
                pool.affine_select(out=before[:], in_=before[:], compare_op=ALU.is_gt, fill=0.0, base=0,
                                   pattern=[[1, P]], channel_multiplier=-1).then_inc(consts, 1)
                imprecise = dict(base=0, channel_multiplier=0, allow_small_or_imprecise_dtypes=True)
                pool.iota(counts_to[:], pattern=[[0, E8], [ROWS, MOST]], **imprecise).then_inc(consts, 1)
                pool.iota(block_no[:], pattern=[[1, BLOCKS]], **imprecise).then_inc(consts, 1)
                pool.iota(origin[:], pattern=[[BATCH * SEQ, E8]], **imprecise).then_inc(consts, 1)

                pool.wait_ge(loaded, 48)
                wide = lambda t: t[:].unsqueeze(1).to_broadcast([P, TPB, D])

                def gain_and_bias(b):
                    pool.wait_ge(normed, b + 1)
                    pool.tensor_tensor(xn[b % 2][:], xn[b % 2][:], wide(gain), ALU.mult).then_inc(gained, 1)
                    pool.wait_ge(gained, b + 1)
                    pool.tensor_tensor(xn[b % 2][:], xn[b % 2][:], wide(shift), ALU.add).then_inc(xf_ready, 1)

                def scatter(n):
                    for k in range(2):
                        pool.indirect_dma_start(out=sorted_rows, out_offset=bass.IndirectOffsetOnAxis(ap=slots[:, k, n:n + 1], axis=0),
                                                in_=zall[:, n, :], in_offset=None).then_inc(moved, 16)

                for b in range(2):
                    gain_and_bias(b)
                pool.wait_ge(slots_ready, 1)
                for n in range(HEAD_START):
                    scatter(n)
                for b in range(2, 4):
                    gain_and_bias(b)
                for n in range(HEAD_START, HT):
                    scatter(n)
                pool.wait_ge(slots_ready, 2)
                for n in range(HT, TILES):
                    scatter(n)
                pool.wait_ge(moved, 32 * TILES)

            @block.tensor
            def _(pe):
                pe.wait_ge(loaded, 48)
                for b in range(BATCH):
                    way = b % 2
                    pe.wait_ge(xf_ready, b + 1)
                    for g in range(2):
                        for t in range(4):
                            last = pe.transpose(turn[2 * way + g][:, t * P:(t + 1) * P], xn[way][:, 4 * g + t, :], ident[:])
                        last.then_inc(turned, 1)
                    pe.wait_ge(evac, 2 * b + 2)
                    for t in range(TPB):
                        last = pe.matmul(lg[way][:, t * EXPERTS:(t + 1) * EXPERTS], xfT[way][:, t * P:(t + 1) * P], rw[:], start=True, stop=True)
                    last.then_inc(routed, 1)
                    if way:
                        j = b // 2
                        if j == 0:
                            pe.wait_ge(consts, n_consts)
                        pe.wait_ge(picked_ready, j + 1)
                        flat = picked[:, 2, j * HT:(j + 1) * HT, :].rearrange("p n e -> p (n e)")
                        pe.matmul(within[:, 0:HT * E8], before[:], flat, start=True, stop=True)
                        pe.matmul(totals[:, 0:HT * E8], ones[:], flat, start=True, stop=True).then_inc(counted, 1)

            @block.scalar
            def _(act):
                for j in range(BATCH // 2):
                    for way in range(2):
                        norm.square(act, xn[way][:], TPB, 4 * j + way, way)
                    for way in range(2):
                        norm.root(act, TPB, 4 * j + way, way)
                    for way in range(2):
                        b = 2 * j + way
                        for g in range(2):
                            act.wait_ge(turned, 2 * b + g + 1)
                            act.activation(xfT[way][:, g * HALF:(g + 1) * HALF], turn[2 * way + g][:], ACT.Copy).then_inc(evac, 1)
                        norm.square(act, zall[:, b * TPB:(b + 1) * TPB, :], TPB, 4 * j + 2 + way, way)
                    for way in range(2):
                        norm.root(act, TPB, 4 * j + 2 + way, way)
                act.wait_ge(gap_ready, 1)
                act.activation(top[:, 3, :], top[:, 2, :], ACT.Exp).then_inc(exp_ready, 1)

            @block.vector
            def _(dve):
                chain = Chain(dve, shared)
                link, tt, ts = chain.link, dve.tensor_tensor, dve.tensor_scalar

                def route(j):
                    tiles = [slice((2 * j + way) * TPB, (2 * j + way + 1) * TPB) for way in range(2)]
                    for way in range(2):
                        if j:
                            dve.wait_ge(routed, 2 * j - 1 + way)
                        norm.centre(dve, chain, X[:, tiles[way], :], xn[way][:], TPB, 4 * j + way, way)
                    for way in range(2):
                        norm.variance(dve, chain, TPB, 4 * j + way, way, gain=1.0 + EPS, add=EPS * EPS)
                    for way in range(2):
                        norm.scale(dve, chain, xn[way][:], TPB, 4 * j + way, way).then_inc(normed, 1)
                    for way in range(2):
                        dve.wait_ge(xf_ready, 2 * j + way + 1)
                        norm.centre(dve, chain, xn[way][:], zall[:, tiles[way], :], TPB, 4 * j + 2 + way, way)
                    for way in range(2):
                        norm.variance(dve, chain, TPB, 4 * j + 2 + way, way)
                    for way in range(2):
                        link(norm.scale(dve, chain, zall[:, tiles[way], :], TPB, 4 * j + 2 + way, way))
                    for way in range(2):
                        dve.wait_ge(routed, 2 * j + way + 1)
                        link(dve.tensor_copy(logits[:, tiles[way], :], lg[way][:, 0:TPB * EXPERTS].rearrange("p (j e) -> p j e", e=EXPERTS)))

                def find_rows(j):
                    T = slice(j * HT, (j + 1) * HT)
                    full = [P, HT, E8, E8]
                    other, own = logits[:, T, :].unsqueeze(2).to_broadcast(full), logits[:, T, :].unsqueeze(3).to_broadcast(full)
                    tt(cmp[:], other, own, ALU.is_gt)
                    link(tt(cmp2[:], other, own, ALU.is_equal))
                    link(tt(cmp2[:], cmp2[:], tri[:].unsqueeze(1).to_broadcast(full), ALU.mult))
                    link(tt(cmp[:], cmp[:], cmp2[:], ALU.add))
                    link(dve.tensor_reduce(rank[:], cmp[:], AX, ALU.add))
                    link(ts(picked[:, 0, T], rank[:], 0.0, None, ALU.is_equal))
                    link(ts(picked[:, 1, T], rank[:], 1.0, None, ALU.is_equal))
                    tt(picked[:, 2, T], picked[:, 0, T], picked[:, 1, T], ALU.add).then_inc(picked_ready, 1)
                    dve.wait_ge(counted, j + 1)
                    flat = lambda t: t[:].rearrange("p e n -> p (e n)")
                    link(dve.tensor_copy(per_tile[:], totals[:, 0:HT * E8].rearrange("p (n e) -> p e n", e=E8)))
                    link(dve.tensor_tensor_scan(flat(prefix), flat(first_zero), flat(per_tile), 0.0, ALU.mult, ALU.add))
                    link(tt(place[j + 1][:].unsqueeze(2), place[j][:].unsqueeze(2), prefix[:, :, HT - 1:HT], ALU.add))
                    link(tt(prefix[:], prefix[:], per_tile[:], ALU.subtract))
                    link(tt(prefix[:], prefix[:], place[j][:].unsqueeze(2).to_broadcast([P, E8, HT]), ALU.add))
                    link(tt(pos[:], within[:, 0:HT * E8].rearrange("p (n e) -> p n e", e=E8), prefix[:].rearrange("p e n -> p n e"), ALU.add))
                    for k in range(2):
                        link(tt(work[:, T, :], pos[:], picked[:, k, T], ALU.mult))
                        link(dve.tensor_reduce(slot_f[:, k, :], work[:, T, :], AX, ALU.add))
                    dve.tensor_copy(slots[:, :, T], slot_f[:]).then_inc(slots_ready, 1)

                dve.wait_ge(consts, n_consts)
                link(dve.tensor_copy(place[0][:], origin[:]))
                link(dve.memset(first_zero[:], 1.0))
                link(dve.memset(first_zero[:, :, 0:1], 0.0))
                link(dve.memset(all_one[:], 1.0))
                for j in range(2):
                    route(j)
                    find_rows(j)
                link(tt(work[:], logits[:], picked[:, 1], ALU.mult))
                link(dve.tensor_reduce(top[:, 1, :], work[:], AX, ALU.add))
                link(dve.tensor_reduce(top[:, 0, :], logits[:], AX, ALU.max))
                tt(top[:, 2, :], top[:, 1, :], top[:, 0, :], ALU.subtract).then_inc(gap_ready, 1)
                dve.wait_ge(exp_ready, 1)
                link(ts(top[:, 0, :], top[:, 3, :], 1.0, None, ALU.add))
                link(dve.reciprocal(gates[:, 0, :], top[:, 0, :]))
                link(tt(gates[:, 1, :], gates[:, 0, :], top[:, 3, :], ALU.mult))
                link(tt(total[:], place[2][:], origin[:], ALU.subtract))
                link(tt(cmp3[:], total[:].unsqueeze(2).to_broadcast([P, E8, MOST]), counts_to[:], ALU.is_gt))
                link(dve.tensor_reduce(blocks_of[:], cmp3[:], AX, ALU.add))
                link(dve.tensor_tensor_scan(block_end[:], all_one[:], blocks_of[:], 0.0, ALU.mult, ALU.add))
                most = [P, BLOCKS, E8 - 1]
                end = block_end[:, 0:E8 - 1].unsqueeze(1).to_broadcast(most)
                link(tt(ended[:], end, block_no[:].unsqueeze(2).to_broadcast(most), ALU.is_le))
                link(dve.tensor_reduce(owner[:], ended[:], AX, ALU.add))
                link(tt(ends[:], ended[:], end, ALU.mult))
                link(dve.tensor_reduce(first[:], ends[:], AX, ALU.max))
                link(tt(first[:], block_no[:], first[:], ALU.subtract))
                link(dve.tensor_copy(blocks[:, 0, :], owner[:]))
                link(ts(owner[:], owner[:], float(MOST), None, ALU.mult))
                link(tt(first[:], first[:], owner[:], ALU.add))
                link(ts(blocks[:, 1, :], first[:], float(PLACES - 1), None, ALU.min))
                chain.close()


def run_experts(nc, ident, w, folded, blocks, shared, tag):
    QB = ROWS // P
    TURN_AT = 0
    with ExitStack() as ctx:
        sb = lambda name, shape, dt=F32: ctx.enter_context(nc.sbuf_tensor(tag + name, shape, dt))
        bank = lambda name: ctx.enter_context(nc.psum_tensor(tag + name, [P, HALF], F32))
        sem = lambda name: ctx.enter_context(nc.semaphore(tag + name))
        both = lambda name, shape: [sb(f"{name}{i}", shape) for i in range(2)]
        w12 = both("w12", [P, 2, HIDDEN])
        wo = both("wo", [P, HC, D])
        bias = both("bias", [P, 4, HC])
        bo = both("bo", [P, D])
        z = both("z", [P, QB, D])
        zT = both("zT", [P, ROWS])
        x2 = both("x2", [P, ROWS])
        act2 = both("act2", [P, ROWS])
        hid = both("hid", [P, ROWS])
        hT = both("hT", [P, HC, ROWS])
        y = both("y", [P, QB, D])
        turn = bank("turn")
        p1 = [bank(f"p1{i}") for i in range(2)]
        p2 = [bank(f"p2{i}") for i in range(2)]
        py = [bank(f"py{i}") for i in range(2)]
        turned, zT_ready, x2_done, up_done, x2_ready, act_ready, x1_taken, hT_ready, down_done, y_ready = (
            sem(n) for n in ("turned", "zT_ready", "x2_done", "up_done", "x2_ready", "act_ready", "x1_taken", "hT_ready", "down_done", "y_ready"))
        up_loaded, down_loaded, z_loaded, stored = ([sem(f"{n}{i}") for i in range(2)]
                                                    for n in ("up_loaded", "down_loaded", "z_loaded", "stored"))

        def loop(eng, step):
            for t in range(4):
                step(t // 2, t, t % 2)
            with eng.Fori(2, BLOCKS // 2) as j:
                for par in range(2):
                    step(j, 2 * j + par, par)
            for t in range(BLOCKS // 2 * 2, BLOCKS):
                step(t // 2, t, t % 2)

        view = folded.sorted_rows.rearrange("(t q p) d -> t p q d", q=QB, p=P)

        with nc.Block() as block:

            @block.sync
            def _(sp):
                def expert(t):
                    return sp.value_load(blocks[0:1, 0, bass.ds(t, 1)], min_val=0, max_val=EXPERTS - 1)

                def place(t):
                    return sp.value_load(blocks[0:1, 1, bass.ds(t, 1)], min_val=0, max_val=PLACES - 1)

                def load_rows(at, par):
                    sp.dma_start(z[par][:], view[bass.ds(at, 1), :, :, :].rearrange("a p q d -> (a p) q d")).then_inc(z_loaded[par], 16)

                def load_down(par, e):
                    sp.dma_start(wo[par][:], w["L0_ffn_Wo"][bass.ds(e, 1), :, :].rearrange("a (c p) d -> (a p) c d", p=P)).then_inc(down_loaded[par], 16)
                    sp.dma_start(bo[par][:], w["L0_ffn_bo"][bass.ds(e, 1), :].rearrange("a d -> (a d)").partition_broadcast(P)).then_inc(down_loaded[par], 16)

                def store(at, par):
                    sp.dma_start(view[bass.ds(at, 1), :, :, :].rearrange("a p q d -> (a p) q d"), y[par][:]).then_inc(stored[par], 16)

                def step(j, t, par):
                    known = isinstance(t, int)
                    row = expert(t) * P
                    e_before = None if known and t == 0 else expert(t - 1)
                    at = place((t + 1) % BLOCKS)
                    y_at = None if known and t < 3 else place(t - 3)
                    if not (known and t == 0):
                        sp.wait_ge(turned, t)
                    load_rows(at, 1 - par)
                    if not (known and t < 2):
                        sp.wait_ge(x1_taken, HC * (t - 1))
                    sp.dma_start(w12[par][:].rearrange("p a h -> p (a h)"), folded.w12[bass.ds(row, P), :]).then_inc(up_loaded[par], 16)
                    sp.dma_start(bias[par][:].rearrange("p a c -> p (a c)"), folded.bias[bass.ds(row, P), :]).then_inc(up_loaded[par], 16)
                    if not (known and t < 3):
                        sp.wait_ge(y_ready, t - 2)
                        store(y_at, 1 - par)
                    if not (known and t == 0):
                        load_down(1 - par, e_before)

                load_rows(place(0), 0)
                loop(sp, step)
                e, y_at = expert(BLOCKS - 1), [place(BLOCKS - 3 + i) for i in range(3)]
                for i in range(3):
                    sp.wait_ge(y_ready, BLOCKS - 2 + i)
                    store(y_at[i], (BLOCKS - 3 + i) % 2)
                    if i == 0:
                        load_down((BLOCKS - 1) % 2, e)
                sp.wait_ge(z_loaded[BLOCKS % 2], 16 * (BLOCKS // 2 + 1))
                for par in range(2):
                    sp.wait_ge(stored[par], 16 * ((BLOCKS + 1 - par) // 2))

            @block.tensor
            def _(pe):
                def up(t, par, c):
                    n = HC * t + c
                    if not (isinstance(n, int) and n < 2):
                        pe.wait_ge(x1_taken, n - 1)
                    pe.matmul(p2[c % 2][:], w12[par][:, 1, c * P:(c + 1) * P], zT[par][:], start=True, stop=True).then_inc(x2_done, 1)
                    pe.matmul(p1[c % 2][:], w12[par][:, 0, c * P:(c + 1) * P], zT[par][:], start=True, stop=True).then_inc(up_done, 1)

                def down(j, t, par, q):
                    if q == 0:
                        pe.wait_ge(down_loaded[par], 32 * (j + 1))
                        pe.wait_ge(hT_ready, HC * (t + 1))
                        if not (isinstance(t, int) and t < 2):
                            pe.wait_ge(y_ready, t - 1)
                    for c in range(HC):
                        last = pe.matmul(py[par][:, q * D:(q + 1) * D], hT[par][:, c, q * P:(q + 1) * P], wo[par][:, c, :],
                                         start=c == 0, stop=c == HC - 1)
                    if q == QB - 1:
                        last.then_inc(down_done, 1)

                def turn_rows(j, t, par):
                    pe.wait_ge(z_loaded[par], 16 * (j + 1))
                    for q in range(QB):
                        last = pe.transpose(turn[:, q * P:(q + 1) * P], z[par][:, q, :], ident[:])
                    last.then_inc(turned, 1)

                def step(j, t, par):
                    pe.wait_ge(up_loaded[par], 32 * (j + 1))
                    pe.wait_ge(zT_ready, t + 1)
                    for c in range(HC):
                        up(t, par, c)
                        if c == 0 and not (isinstance(t, int) and t < 2):
                            down(j - 1, t - 2, par, QB - 1)
                        if c > 0 and not (isinstance(t, int) and t == 0):
                            down(j - (1 - par), t - 1, 1 - par, c - 1)
                        if c == TURN_AT:
                            turn_rows(j + par, t + 1, 1 - par)

                turn_rows(0, 0, 0)
                loop(pe, step)
                down((BLOCKS - 2) // 2, BLOCKS - 2, (BLOCKS - 2) % 2, QB - 1)
                for q in range(QB):
                    down((BLOCKS - 1) // 2, BLOCKS - 1, (BLOCKS - 1) % 2, q)

            @block.scalar
            def _(act):
                def tokens(t, par):
                    act.wait_ge(turned, t + 1)
                    act.activation(zT[par][:], turn[:], ACT.Copy).then_inc(zT_ready, 1)

                def step(j, t, par):
                    for c in range(HC):
                        act.wait_ge(x2_ready, HC * t + c + 1)
                        act.activation(act2[c % 2][:], x2[c % 2][:], ACT.Silu, bias=bias[par][:, 1, c:c + 1]).then_inc(act_ready, 1)
                        if c == TURN_AT:
                            tokens(t + 1, 1 - par)

                tokens(0, 0)
                loop(act, step)

            @block.vector
            def _(dve):
                chain = Chain(dve, shared)

                def finish(j, t, par):
                    dve.wait_ge(down_done, t + 1)
                    if not isinstance(t, int) or t >= 2:
                        dve.wait_ge(stored[par], 16 * j)
                    chain.link(dve.tensor_tensor(y[par][:], py[par][:].rearrange("p (q d) -> p q d", d=D),
                                                 bo[par][:].unsqueeze(1).to_broadcast([P, QB, D]), ALU.add))
                    dve.tensor_scalar(y[par][:], y[par][:], CLAMP, -CLAMP, ALU.min, ALU.max).then_inc(y_ready, 1)

                def clip_x2(j, t, par, c):
                    if c == 0:
                        dve.wait_ge(up_loaded[par], 32 * (j + 1))
                    dve.wait_ge(x2_done, HC * t + c + 1)
                    dve.tensor_scalar(x2[c % 2][:], p2[c % 2][:], bias[par][:, 2, c:c + 1], bias[par][:, 3, c:c + 1],
                                      ALU.max, ALU.min).then_inc(x2_ready, 1)

                def step(j, t, par):
                    for c in range(HC):
                        if c < HC - 1:
                            clip_x2(j, t, par, c + 1)
                        elif not (isinstance(t, int) and t == BLOCKS - 1):
                            clip_x2(j + par, t + 1, 1 - par, 0)
                        product(t, par, c)
                        if c == 1 and not (isinstance(t, int) and t < 2):
                            finish(j - 1, t - 2, par)

                def product(t, par, c):
                    dve.wait_ge(act_ready, HC * t + c + 1)
                    dve.wait_ge(up_done, HC * t + c + 1)
                    dve.scalar_tensor_tensor(hid[c % 2][:], p1[c % 2][:], bias[par][:, 0, c:c + 1], act2[c % 2][:],
                                             ALU.add, ALU.mult).then_inc(x1_taken, 1)
                    dve.wait_ge(x1_taken, HC * t + c + 1)
                    if not (isinstance(t, int) and t < 2) and c == 0:
                        dve.wait_ge(down_done, t - 1)
                    dve.tensor_scalar(hT[par][:, c, :], hid[c % 2][:], CLAMP, -CLAMP, ALU.min, ALU.max).then_inc(hT_ready, 1)

                clip_x2(0, 0, 0, 0)
                for t in range(4):
                    step(t // 2, t, t % 2)
                turns = (BLOCKS - 1) // 2
                with dve.Fori(2, turns) as j:
                    chain.enter_from(j, 2, 2)
                    for par in range(2):
                        step(j, 2 * j + par, par)
                chain.leave(turns - 2)
                for t in range(2 * turns, BLOCKS):
                    step(t // 2, t, t % 2)
                for t in (BLOCKS - 2, BLOCKS - 1):
                    finish(t // 2, t, t % 2)
                chain.close()


class Combine:
    DEPTH = 4
    PER = DEPTH // 2

    def __init__(self, sb, sem, choices, folded):
        self.rows = [sb(f"rows{i}", [P, D]) for i in range(self.DEPTH)]
        self.fetched = [sem(f"fetched{i}") for i in range(self.DEPTH)]
        self.added = sem("added")
        self.choices, self.folded = choices, folded

    def pool(self, pool):
        for m in range(TILES // self.PER):
            for i in range(self.DEPTH):
                k, n = i % 2, m * self.PER + i // 2
                if m > 0:
                    pool.wait_ge(self.fetched[i], 16 * m)
                    pool.wait_ge(self.added, self.DEPTH * (m - 1) + i + 1)
                pool.indirect_dma_start(out=self.rows[i][:], out_offset=None, in_=self.folded.sorted_rows,
                                        in_offset=bass.IndirectOffsetOnAxis(ap=self.choices.slots[:, k, n:n + 1], axis=0))\
                    .then_inc(self.fetched[i], 16)

    def vector(self, dve, X, m):
        for i in range(self.DEPTH):
            k, n = i % 2, m * self.PER + i // 2
            dve.wait_ge(self.fetched[i], 16 * (m + 1))
            if k:
                dve.wait_ge(self.added, self.DEPTH * m + i)
            dve.scalar_tensor_tensor(X[:, n, :], self.rows[i][:], self.choices.gates[:, k, n:n + 1], X[:, n, :],
                                     ALU.mult, ALU.add).then_inc(self.added, 1)


def combine_and_store(nc, X, choices, folded, out):
    with ExitStack() as ctx:
        sb = lambda name, shape, dt=F32: ctx.enter_context(nc.sbuf_tensor("c_" + name, shape, dt))
        sem = lambda name: ctx.enter_context(nc.semaphore("c_" + name))
        combine = Combine(sb, sem, choices, folded)
        stored = sem("stored")
        turns = TPB // combine.PER

        with nc.Block() as block:

            @block.gpsimd
            def _(pool):
                combine.pool(pool)

            @block.vector
            def _(dve):
                for m in range(BATCH * turns):
                    combine.vector(dve, X, m)

            @block.sync
            def _(sp):
                for b in range(BATCH):
                    sp.wait_ge(combine.added, 2 * TPB * (b + 1))
                    sp.dma_start(out[b].rearrange("(n p) d -> p n d", p=P), X[:, b * TPB:(b + 1) * TPB, :]).then_inc(stored, 16)
                sp.wait_ge(stored, 16 * BATCH)




HEADS = 16
HD = 64
KV_BLOCK = 64
NB = SEQ // KV_BLOCK
PAIRS = BATCH * HEADS // 2
QT = 2
GT = 2 * QT
GPP = TPB // QT
LAG = 3
BIG = 3.0e38


def head_inputs(nc, X, ident, hT_dram, choices, folded, shared, tag):
    with ExitStack() as ctx:
        sb = lambda name, shape, dt=F32: ctx.enter_context(nc.sbuf_tensor(tag + name, shape, dt))
        sem = lambda name: ctx.enter_context(nc.semaphore(tag + name))
        combine = Combine(sb, sem, choices, folded)
        norm = Norm(sb, shared, TPB, BATCH, ways=2)
        hn = [sb(f"hn{i}", [P, TPB, D]) for i in range(2)]
        hT = [sb(f"hT{i}", [P, SEQ]) for i in range(2)]
        ring = [ctx.enter_context(nc.psum_tensor(f"{tag}ring{i}", [P, HALF], F32)) for i in range(4)]
        hn_ready, turned, evac, stored0, stored1 = (sem(n) for n in ("hn_ready", "turned", "evac", "stored0", "stored1"))
        stored = (stored0, stored1)

        with nc.Block() as block:

            @block.gpsimd
            def _(pool):
                combine.pool(pool)

            @block.vector
            def _(dve):
                chain = Chain(dve, shared)
                turns = TPB // combine.PER
                for b in range(BATCH + 1):
                    for turn in range(turns):
                        if b < BATCH:
                            combine.vector(dve, X, b * turns + turn)
                        n, way = b - 1, (b - 1) % 2
                        if n >= 0 and turn == 0:
                            dve.wait_ge(combine.added, 2 * TPB * (n + 1))
                            if n >= 2:
                                dve.wait_ge(evac, 2 * (n - 1))
                                dve.wait_ge(stored[way], 16 * (n // 2))
                            norm.centre(dve, chain, X[:, n * TPB:(n + 1) * TPB, :], hn[way][:], TPB, n, way)
                        if n >= 0 and turn == 1:
                            norm.variance(dve, chain, TPB, n, way)
                        if n >= 0 and turn == 2:
                            norm.scale(dve, chain, hn[way][:], TPB, n, way).then_inc(hn_ready, 1)
                chain.close()

            @block.scalar
            def _(act):
                for n in range(BATCH):
                    way = n % 2
                    norm.square(act, hn[way][:], TPB, n, way)
                    norm.root(act, TPB, n, way)
                    for g in range(2):
                        act.wait_ge(turned, 2 * n + g + 1)
                        act.activation(hT[way][:, g * HALF:(g + 1) * HALF], ring[2 * way + g][:], ACT.Copy).then_inc(evac, 1)

            @block.tensor
            def _(pe):
                for n in range(BATCH):
                    way = n % 2
                    pe.wait_ge(hn_ready, n + 1)
                    for g in range(2):
                        for t in range(4):
                            last = pe.transpose(ring[2 * way + g][:, t * P:(t + 1) * P], hn[way][:, 4 * g + t, :], ident[:])
                        last.then_inc(turned, 1)

            @block.sync
            def _(sp):
                for n in range(BATCH):
                    sp.wait_ge(evac, 2 * (n + 1))
                    sp.dma_start(hT_dram[:, n * SEQ:(n + 1) * SEQ], hT[n % 2][:]).then_inc(stored[n % 2], 16)
                for way in range(2):
                    sp.wait_ge(stored[way], 16 * (BATCH // 2))


def block_softmax_attention(nc, X, ident, w, choices, folded, shared):
    hT_dram = nc.dram_tensor("b_hT", [D, BATCH * SEQ], F32, kind="Internal").ap()
    head_inputs(nc, X, ident, hT_dram, choices, folded, shared, "bh_")
    with ExitStack() as ctx:
        sb = lambda name, shape, dt=F32: ctx.enter_context(nc.sbuf_tensor("b_" + name, shape, dt))
        psum = lambda name, cols: ctx.enter_context(nc.psum_tensor("b_" + name, [P, cols], F32))
        sem = lambda name: ctx.enter_context(nc.semaphore("b_" + name))

        hb = [sb(f"hb{i}", [P, SEQ]) for i in range(2)]
        wqkv = [sb(f"wqkv{i}", [P, 3, P]) for i in range(2)]
        QS = [[sb(f"QS{i}{h}", [P, SEQ], F32R) for h in range(2)] for i in range(2)]
        KH = [[sb(f"KH{i}{h}", [P, SEQ], F32R) for h in range(2)] for i in range(2)]
        KL = [[sb(f"KL{i}{h}", [P, SEQ], F32R) for h in range(2)] for i in range(2)]
        V = [sb(f"V{i}", [P, TPB, P]) for i in range(2)]
        parts = {"q": (sb("q_high", [P, SEQ], F32R), sb("q_low", [P, SEQ], F32R)),
                 "k": (sb("k_high", [P, SEQ], F32R), sb("k_low", [P, SEQ], F32R))}
        wo = sb("wo", [P, HEADS // 2, D])
        prob = [[sb(f"prob{i}{t}", [P, SEQ]) for t in range(GT)] for i in range(4)]
        bmax = [sb(f"bmax{i}", [P, GT, NB]) for i in range(2)]
        bsum = [sb(f"bsum{i}", [P, GT, NB]) for i in range(2)]
        neg_m = [sb(f"neg_m{i}", [P, GT]) for i in range(2)]
        run_max = sb("run_max", [P, GT, NB])
        run_sum = sb("run_sum", [P, GT, NB])
        drop = sb("drop", [P, GT, NB])
        rise = sb("rise", [P, GT, NB])
        inv_l = sb("inv_l", [P, GT, NB])
        weight = [sb(f"weight{i}", [P, GT, NB]) for i in range(2)]
        first_low = sb("first_low", [P, GT, NB])
        first_zero = sb("first_zero", [P, GT, NB])
        last_one = sb("last_one", [P, GT, NB])
        pT = [sb(f"pT{i}", [P, HALF]) for i in range(4)]
        oT = [sb(f"oT{i}", [P, QT * P]) for i in range(2)]

        score = [psum(f"score{i}", SEQ) for i in range(2)]
        turn = [psum(f"turn{i}", HALF) for i in range(2)]
        acc = psum("acc", HALF)
        misc = psum("misc", HALF)

        names = ("wo_loaded", "loaded", "scored", "max_ready", "prob_ready", "sum_ready", "drop_ready", "rise_ready",
                 "weight_ready", "scaled", "turned", "evac", "pv_done", "o_ready", "wo_done", "wo_taken",
                 "qk_made", "high_ready", "qk_taken", "q_dealt", "k_dealt", "v_made", "v_taken")
        s = {n: sem(n) for n in names}
        (wo_loaded, loaded, scored, max_ready, prob_ready, sum_ready, drop_ready, rise_ready,
         weight_ready, scaled, turned, evac, pv_done, o_ready, wo_done, wo_taken,
         qk_made, high_ready, qk_taken, q_dealt, k_dealt, v_made, v_taken) = (s[n] for n in names)

        flat = lambda t: t[:].rearrange("p t n -> p (t n)")
        Wq, Wk, Wv, Wo = (w["L0_attn_b_" + n] for n in ("Wq", "Wk", "Wv", "Wo"))

        def slots(eng, slot):
            for r in range(8):
                slot(0, r, True, r >= LAG)
            with eng.Fori(1, PAIRS // 2) as j:
                for r in range(8):
                    slot(j, r, True, True)
            for r in range(LAG + 1):
                slot(PAIRS // 2, r, False, r < LAG)

        groups = 4 * PAIRS

        def projected(j, r, k, scores):
            if k >= 2 and scores:
                rr, n = r, k - 2
            else:
                return None
            i, par = 2 * j + rr // GPP + 1, (rr // GPP + 1) % 2
            return {0: None, 1: ("qk", i, par, n), 2: ("qk", i, par, 2 + n), 3: ("v", i, par, n)}[rr % GPP]

        with nc.Block() as block:

            @block.sync
            def _(sp):
                raw = lambda ap: ap.bitcast(F32)
                sp.dma_start(wo[:], Wo.rearrange("(c p) d -> p c d", p=P)).then_inc(wo_loaded, 16)

                def places(i):
                    b, hp = (i % PAIRS) // (HEADS // 2), i % (HEADS // 2)
                    return (b * SEQ, hp * P) if isinstance(i, int) else (sp.snap(b * SEQ), sp.snap(hp * P))

                def load(par, token, column):
                    sp.dma_start(hb[par][:], hT_dram[:, bass.ds(token, SEQ)]).then_inc(loaded, 16)
                    for a, W in enumerate((Wq, Wk, Wv)):
                        sp.dma_start(wqkv[par][:, a, :], W[:, bass.ds(column, P)]).then_inc(loaded, 16)

                def deal(kind, par):
                    high, low = parts[kind]
                    for h in range(2):
                        mine = slice(h * HD, (h + 1) * HD)
                        if kind == "q":
                            sp.dma_start(raw(QS[par][h][0:HD, :]), raw(high[mine, :])).then_inc(q_dealt, 16)
                            sp.dma_start(raw(QS[par][h][HD:P, :]), raw(low[mine, :])).then_inc(q_dealt, 16)
                        else:
                            for part, dst in ((high, KH), (low, KL)):
                                sp.dma_start(raw(dst[par][h][0:HD, :]), raw(part[mine, :])).then_inc(k_dealt, 16)
                                sp.dma_start(raw(dst[par][h][HD:P, :]), raw(part[mine, :])).then_inc(k_dealt, 16)

                load(0, *places(0))
                sp.wait_ge(qk_taken, 2)
                deal("q", 0)
                sp.wait_ge(qk_taken, 4)
                deal("k", 0)

                def pair(i, c):
                    par, at = (c + 1) % 2, places(i + 1)
                    fixed = lambda v: v if isinstance(v, int) else sp.snap(v)
                    v_before, q_parts, k_parts = (fixed(v) for v in (2 * i, 4 * i + 6, 4 * i + 8))
                    if c == 1 or not isinstance(i, int):
                        sp.wait_ge(v_made, v_before)
                    load(par, *at)
                    sp.wait_ge(qk_taken, q_parts)
                    deal("q", par)
                    sp.wait_ge(qk_taken, k_parts)
                    deal("k", par)

                for c in range(2):
                    pair(c, c)
                with sp.Fori(1, PAIRS // 2) as j:
                    for c in range(2):
                        pair(2 * j + c, c)
                sp.wait_ge(q_dealt, 64 * (PAIRS + 1))
                sp.wait_ge(k_dealt, 128 * (PAIRS + 1))

            @block.tensor
            def _(pe):
                last_use = [None]

                def misc_free():
                    if last_use[0]:
                        pe.wait_ge(*last_use[0])

                def qk_proj(i, par, u):
                    kind, h = u // 2, u % 2
                    misc_free()
                    if u == 0:
                        pe.wait_ge(loaded, 64 * (i + 1))
                    pe.matmul(misc[:], wqkv[par][:, kind, :], hb[par][:, h * HALF:(h + 1) * HALF],
                              start=True, stop=True).then_inc(qk_made, 1)
                    last_use[0] = (qk_taken, 4 * i + u + 1)

                def v_proj(i, par, h):
                    misc_free()
                    for t in range(4):
                        last = pe.matmul(misc[:, t * P:(t + 1) * P], hb[par][:, (4 * h + t) * P:(4 * h + t + 1) * P],
                                         wqkv[par][:, 2, :], start=True, stop=True)
                    last.then_inc(v_made, 1)
                    last_use[0] = (v_taken, 2 * i + h + 1)

                def pv(g, r, kp):
                    par = (r // GPP) % 2
                    pe.wait_ge(evac, 8 * g + 2 * kp + 2)
                    if kp == 0:
                        if not (isinstance(g, int) and g == 0):
                            pe.wait_ge(o_ready, g)
                        pe.wait_ge(v_taken, 2 * (g // GPP) + 2)
                    for kk in range(2):
                        for h in range(2):
                            kt = 2 * kp + kk
                            last = pe.matmul(acc[h * HD:(h + 1) * HD, 0:QT * P], V[par][:, kt, h * HD:(h + 1) * HD],
                                             pT[(2 * kp + h) % 4][:, kk * QT * P:(kk + 1) * QT * P],
                                             start=kt == 0, stop=kt == TPB - 1)
                    last.then_inc(pv_done, 1)

                def slot(j, r, scores, finish):
                    sl, par = 8 * j + r, r // GPP
                    g, gr = sl - LAG, (r - LAG) % 8
                    before = not (isinstance(sl, int) and sl <= LAG)
                    for k in range(GT):
                        if scores:
                            h, q = k // QT, (r % GPP) * QT + k % QT
                            if k == 0:
                                i = 2 * j + par
                                pe.wait_ge(q_dealt, 64 * (i + 1))
                                pe.wait_ge(k_dealt, 128 * (i + 1))
                            if not (isinstance(sl, int) and sl == 0 and k < 2):
                                pe.wait_ge(prob_ready, 4 * sl + k - 1)
                            for c in range(2):
                                for n, Kx in enumerate((KH, KL)):
                                    last = pe.matmul(score[k % 2][:, c * HALF:(c + 1) * HALF], QS[par][h][:, q * P:(q + 1) * P],
                                                     Kx[par][h][:, c * HALF:(c + 1) * HALF], start=n == 0, stop=n == 1)
                            last.then_inc(scored, 1)
                        if finish:
                            if k == 0:
                                pe.wait_ge(scaled, 4 * g + 4)
                            for h in range(2):
                                if before or k > 0:
                                    pe.wait_ge(evac, 8 * g + 2 * k + h - 1)
                                for kk in range(2):
                                    for q in range(QT):
                                        last = pe.transpose(turn[h][:, (kk * QT + q) * P:(kk * QT + q + 1) * P],
                                                            prob[gr % 4][h * QT + q][:, (2 * k + kk) * P:(2 * k + kk + 1) * P],
                                                            ident[:])
                                last.then_inc(turned, 1)
                        if k == 0 and before:
                            pv(g - 1, (gr - 1) % 8, 3)
                        if k > 0 and finish:
                            pv(g, gr, k - 1)
                        if k == 1 and before:
                            misc_free()
                            pe.wait_ge(o_ready, g)
                            hp = ((g - 1) // GPP) % (HEADS // 2)
                            for q in range(QT):
                                last = pe.matmul(misc[:, q * D:(q + 1) * D], oT[(gr - 1) % 2][:, q * P:(q + 1) * P],
                                                 wo[:, bass.ds(hp, 1), :].rearrange("p a d -> p (a d)"), start=True, stop=True)
                            last.then_inc(wo_done, 1)
                            last_use[0] = (wo_taken, g)
                        if k >= 2 and scores:
                            i, nxt = 2 * j + par, (par + 1) % 2
                            if r % GPP == 1:
                                qk_proj(i + 1, nxt, k - 2)
                            if r % GPP == 2:
                                qk_proj(i + 1, nxt, k)
                            if r % GPP == 3:
                                v_proj(i + 1, nxt, k - 2)

                for u in range(4):
                    qk_proj(0, 0, u)
                for h in range(2):
                    v_proj(0, 0, h)
                pe.wait_ge(wo_loaded, 16)
                for r in range(8):
                    slot(0, r, True, r >= LAG)
                with pe.Fori(1, PAIRS // 2) as j:
                    last_use[0] = (v_taken, 4 * j + 2)
                    for r in range(8):
                        slot(j, r, True, True)
                last_use[0] = (v_taken, 2 * PAIRS + 2)
                for r in range(LAG + 1):
                    slot(PAIRS // 2, r, False, r < LAG)

            @block.scalar
            def _(act):
                def high(i, u):
                    kind, h = "qk"[u // 2], u % 2
                    act.wait_ge(qk_made, 4 * i + u + 1)
                    if not (isinstance(i, int) and i == 0):
                        act.wait_ge(q_dealt if kind == "q" else k_dealt, (64 if kind == "q" else 128) * i)
                    act.activation(parts[kind][0][:, h * HALF:(h + 1) * HALF], misc[:], ACT.Copy,
                                   scale=HD ** -0.5 if kind == "q" else 1.0).then_inc(high_ready, 1)

                def v_copy(i, par, h, clear):
                    act.wait_ge(v_made, 2 * i + h + 1)
                    if clear:
                        act.wait_ge(pv_done, 16 * (i - 1))
                    act.activation(V[par][:, 4 * h:4 * h + 4, :].rearrange("p t e -> p (t e)"), misc[:], ACT.Copy).then_inc(v_taken, 1)

                def slot(j, r, scores, finish):
                    sl = 8 * j + r
                    g, gr = sl - LAG, (r - LAG) % 8
                    before = not (isinstance(sl, int) and sl <= LAG)
                    for k in range(GT):
                        if finish:
                            for h in range(2):
                                act.wait_ge(turned, 8 * g + 2 * k + h + 1)
                                if before or k >= 2:
                                    act.wait_ge(pv_done, 4 * g + k - 1)
                                act.activation(pT[(2 * k + h) % 4][:], turn[h][:], ACT.Copy).then_inc(evac, 1)
                        made = projected(j, r, k, scores)
                        if made and made[0] == "qk":
                            high(made[1], made[3])
                        if made and made[0] == "v":
                            v_copy(*made[1:], clear=not (isinstance(made[1], int) and made[1] < 2))
                        if k == 0 and before:
                            act.wait_ge(pv_done, 4 * g)
                            act.activation(oT[(gr - 1) % 2][:], acc[:, 0:QT * P], ACT.Copy).then_inc(o_ready, 1)
                        if scores:
                            act.wait_ge(max_ready, 4 * sl + k + 1)
                            if k == 0 and not (isinstance(sl, int) and sl < 4):
                                act.wait_ge(turned, 8 * (sl - 3))
                            act.activation(prob[r % 4][k][:], score[k % 2][:], ACT.Exp,
                                           bias=neg_m[r % 2][:, k:k + 1]).then_inc(prob_ready, 1)
                        if k == 0 and not (isinstance(sl, int) and sl == 0) and (scores or r == 0):
                            act.wait_ge(drop_ready, sl)
                            act.activation(flat(rise), flat(drop), ACT.Exp, scale=-1.0).then_inc(rise_ready, 1)

                for u in range(4):
                    high(0, u)
                for h in range(2):
                    v_copy(0, 0, h, False)
                slots(act, slot)

            @block.vector
            def _(dve):
                chain = Chain(dve, shared)

                def low(i, u):
                    kind, h = "qk"[u // 2], u % 2
                    hi, lo = (t[:, h * HALF:(h + 1) * HALF] for t in parts[kind])
                    dve.wait_ge(high_ready, 4 * i + u + 1)
                    dve.scalar_tensor_tensor(lo, misc[:], HD ** -0.5 if kind == "q" else 1.0, hi.bitcast(F32),
                                             ALU.mult, ALU.subtract).then_inc(qk_taken, 1)

                def block_sums(n, r, k):
                    dve.wait_ge(prob_ready, 4 * n + k + 1)
                    dve.tensor_reduce(bsum[r % 2][:, k, :], prob[r % 4][k][:].rearrange("p (n c) -> p n c", c=KV_BLOCK), AX,
                                      ALU.add).then_inc(sum_ready, 1)

                def slot(j, r, scores, finish):
                    sl = 8 * j + r
                    g, gr = sl - LAG, (r - LAG) % 8
                    first = isinstance(sl, int) and sl == 0
                    before = not (isinstance(sl, int) and sl <= LAG)
                    rest = not first and (scores or r == 0)
                    n, nr = sl - 1, (r - 1) % 8
                    for k in range(GT):
                        if scores:
                            dve.wait_ge(scored, 4 * sl + k + 1)
                            maxima = chain.mark(dve.tensor_reduce(bmax[r % 2][:, k, :], score[k % 2][:].rearrange("p (n c) -> p n c", c=KV_BLOCK), AX, ALU.max))
                        if k == 0 and rest:
                            m_i = chain.mark(dve.tensor_tensor_scan(flat(run_max), flat(first_low), flat(bmax[nr % 2]), 0.0, ALU.add, ALU.max))
                        if k == 1 and rest:
                            dve.wait_ge(rise_ready, n + 1)
                            chain.wait(sums)
                            scaled_sums = chain.mark(dve.tensor_tensor(flat(inv_l), flat(rise), flat(run_sum), ALU.mult))
                        if scores:
                            chain.wait(maxima)
                            dve.tensor_reduce(neg_m[r % 2][:, k:k + 1], bmax[r % 2][:, k, :], AX, ALU.max, negate=True).then_inc(max_ready, 1)
                        if k == 0 and rest:
                            block_sums(n, nr, GT - 1)
                            chain.wait(m_i)
                            gap = chain.mark(dve.tensor_tensor(run_max[:], run_max[:], neg_m[nr % 2][:].unsqueeze(2).to_broadcast([P, GT, NB]), ALU.add))
                            dve.wait_ge(sum_ready, 4 * n + 4)
                            sums = chain.mark(dve.tensor_tensor_scan(flat(run_sum), flat(first_zero), flat(bsum[nr % 2]), 0.0, ALU.mult, ALU.add))
                            chain.wait(gap)
                            dve.tensor_scalar(flat(drop), flat(run_max), -80.0, None, ALU.max).then_inc(drop_ready, 1)
                        if k == 1 and before:
                            q = (gr - 1) % GPP
                            b = (g - 1) // (4 * HEADS // 2)
                            Xq = X[:, bass.ds(b * TPB + q * QT, QT), :]
                            dve.wait_ge(wo_done, g)
                            dve.tensor_tensor(Xq, misc[:, 0:QT * D].rearrange("p (q d) -> p q d", d=D), Xq, ALU.add).then_inc(wo_taken, 1)
                        if k == 1 and rest:
                            chain.wait(scaled_sums)
                            l_i = chain.mark(dve.tensor_scalar(flat(run_sum), flat(inv_l), 1.0, None, ALU.max))
                        if k > 0 and scores:
                            block_sums(sl, r, k - 1)
                        if k == 1 and rest:
                            chain.wait(l_i)
                            inverse = chain.mark(dve.reciprocal(flat(inv_l), flat(run_sum)))
                            if not (isinstance(sl, int) and sl < 3 and scores):
                                dve.wait_ge(scaled, 4 * n - 4)
                            chain.wait(inverse)
                            dve.tensor_tensor_scan(flat(weight[nr % 2])[:, ::-1], flat(last_one)[:, ::-1], flat(inv_l)[:, ::-1], 0.0,
                                                   ALU.max, ALU.mult).then_inc(weight_ready, 1)
                        made = projected(j, r, k, scores)
                        if made and made[0] == "qk":
                            low(made[1], made[3])

                chain.link(dve.memset(first_low[:], 0.0))
                chain.link(dve.memset(first_low[:, :, 0:1], -BIG))
                chain.link(dve.memset(first_zero[:], 1.0))
                chain.link(dve.memset(first_zero[:, :, 0:1], 0.0))
                chain.link(dve.memset(last_one[:], 0.0))
                chain.link(dve.memset(last_one[:, :, NB - 1:NB], 1.0))
                for u in range(4):
                    low(0, u)

                links = GT + 6
                for r in range(8):
                    slot(0, r, True, r >= LAG)
                with dve.Fori(1, PAIRS // 2) as j:
                    chain.enter_from(j, 1, 8 * links)
                    for r in range(8):
                        slot(j, r, True, True)
                chain.leave(PAIRS // 2 - 1)
                for r in range(LAG + 1):
                    slot(PAIRS // 2, r, False, r < LAG)
                chain.close()

            @block.gpsimd
            def _(pool):
                def weigh(n, r, k):
                    pool.wait_ge(weight_ready, n + 1)
                    tile = prob[r % 4][k][:].rearrange("p (n c) -> p n c", c=KV_BLOCK)
                    pool.tensor_tensor(tile, tile, weight[r % 2][:, k, :].unsqueeze(2).to_broadcast([P, NB, KV_BLOCK]),
                                       ALU.mult).then_inc(scaled, 1)

                def slot(j, r, scores, finish):
                    sl = 8 * j + r
                    for k in range(GT):
                        if (scores or r == 0) and not (isinstance(sl, int) and sl == 0):
                            weigh(sl - 1, (r - 1) % 8, k)

                slots(pool, slot)


def program(nc, w, out):
    with ExitStack() as ctx:
        X = ctx.enter_context(nc.sbuf_tensor("X", [P, TILES, D], F32))
        ident = ctx.enter_context(nc.sbuf_tensor("ident", [P, P], F32))
        shared = Shared(lambda name: ctx.enter_context(nc.semaphore(name)))
        x_loaded = ctx.enter_context(nc.semaphore("x_loaded"))
        ident_made = ctx.enter_context(nc.semaphore("ident_made"))
        tiles = lambda t: t.rearrange("b (n p) d -> p (b n) d", p=P)

        with nc.Block() as block:

            @block.sync
            def _(sp):
                sp.dma_start(X[:], tiles(w["L0_attn_a_x"])).then_inc(x_loaded, 16)
                sp.wait_ge(x_loaded, 16)

            @block.gpsimd
            def _(pool):
                pool.memset(ident[:], 0.0).then_inc(ident_made, 1)
                pool.wait_ge(ident_made, 1)
                pool.affine_select(out=ident[:], in_=ident[:], compare_op=ALU.not_equal, fill=1.0, base=0,
                                   pattern=[[-1, P]], channel_multiplier=1).then_inc(ident_made, 1)
                pool.wait_ge(ident_made, 2)

        choices = Choices(lambda name, shape, dt=F32: ctx.enter_context(nc.sbuf_tensor(name, shape, dt)))
        folded = ExpertWeights(nc)
        sigmoid_attention(nc, X, ident, w, folded, shared)
        gated_experts(nc, X, ident, w, folded, choices, shared, "f1_")
        block_softmax_attention(nc, X, ident, w, choices, folded, shared)
        gated_experts(nc, X, ident, w, folded, choices, shared, "f2_")
        combine_and_store(nc, X, choices, folded, out)


INPUTS = ["L0_attn_a_x", "L0_attn_a_Wq", "L0_attn_a_bq", "L0_attn_a_Wk", "L0_attn_a_bk", "L0_attn_a_Wv", "L0_attn_a_bv",
          "L0_attn_a_Wo", "L0_attn_a_bo", "L0_attn_a_layerscale", "L0_attn_b_Wq", "L0_attn_b_Wk", "L0_attn_b_Wv",
          "L0_attn_b_Wo", "L0_ffn_ln_g", "L0_ffn_ln_b", "L0_ffn_router_w", "L0_ffn_eg", "L0_ffn_eb", "L0_ffn_W1",
          "L0_ffn_b1", "L0_ffn_W2", "L0_ffn_b2", "L0_ffn_Wo", "L0_ffn_bo"]


def kernel(**inputs):
    import numpy as np
    import concourse.bacc as bacc
    from concourse.bass_utils import run_bass_kernel_spmd

    nc = bacc.Bacc("TRN2", target_bir_lowering=False, num_devices=1)
    arrays, w = {}, {}
    for name in INPUTS:
        arrays["in_" + name] = np.ascontiguousarray(inputs[name])
        w[name] = nc.dram_tensor("in_" + name, arrays["in_" + name].shape, F32, kind="ExternalInput").ap()
    out = nc.dram_tensor("out_0", arrays["in_L0_attn_a_x"].shape, F32, kind="ExternalOutput").ap()
    program(nc, w, out)
    r = run_bass_kernel_spmd(nc, [arrays], core_ids=[0])
    return r.results[0]["out_0"]
```
